# Optimizing a Trainium2 kernel written in Bass

```python
import numpy as np
import jax
import jax.numpy as jnp

def _softmax(x, axis=-1):
    return jax.nn.softmax(x, axis=axis)

def _gelu(x):
    return jax.nn.gelu(x, approximate=True)

def _silu(x):
    return jax.nn.silu(x)

def _sigmoid(x):
    return jax.nn.sigmoid(x)

def _layernorm(x, axis=-1, eps=1e-05):
    m = jnp.mean(x, axis=axis, keepdims=True)
    v = jnp.var(x, axis=axis, keepdims=True)
    return (x - m) / jnp.sqrt(v + eps)

def _scatter_add(tgt, idx, src, axis=0):
    return tgt.at[idx].add(src)

def _segment_sum(src, seg, n):
    return jax.ops.segment_sum(src, seg, n)
kernel_name = 'mk_gnn_ffn_d1_gnn_r8_f67b9c'

def setup_inputs(seed: int=0):
    np.random.seed(seed)
    _w = jnp.asarray

    def _rec_inputs():
        import jax
        import jax.numpy as jnp
        _gk = jax.random.key(seed)
        x = -0.0001126 + 1 * jax.random.normal(jax.random.fold_in(_gk, 1), (1250, 768), jnp.float32)
        src = jax.random.randint(jax.random.fold_in(_gk, 2), (20000,), 0, 1250, jnp.int32)
        dst = jax.random.randint(jax.random.fold_in(_gk, 3), (20000,), 0, 1250, jnp.int32)
        _o = jnp.argsort(dst, stable=True)
        src = src[_o]
        dst = dst[_o]
        edge_weight1 = -0.00472126 + 0.997171 * jax.random.normal(jax.random.fold_in(_gk, 13), (20000, 1), jnp.float32)
        return (x, src, dst, edge_weight1)
    x, src, dst, edge_weight1 = _rec_inputs()

    def _L0_gnn_setup():
        import jax, jax.numpy as jnp
        import numpy as np
        N, E, D, H, C = (1250, 12500, 768, 4, 192)
        NEG_SLOPE = 0.2

        def gat_conv(x, src, dst, W, a_src, a_dst, b):
            h = (x @ W).reshape(N, H, C)
            as_n = (h * a_src).sum(-1)
            ad_n = (h * a_dst).sum(-1)
            e = jax.nn.leaky_relu(as_n[src] + ad_n[dst], NEG_SLOPE)
            m = jax.ops.segment_max(e, dst, num_segments=N)
            p = jnp.exp(e - m[dst])
            s = jax.ops.segment_sum(p, dst, num_segments=N)
            alpha = p / (s[dst] + 1e-16)
            out = jax.ops.segment_sum(alpha[:, :, None] * h[src], dst, num_segments=N)
            return out.reshape(N, H * C) + b
        key = jax.random.key(seed)
        ks = jax.random.split(key, 16)
        w = lambda k, shape: jax.random.normal(k, shape, dtype=jnp.float32) * 0.02
        inp = {}
        inp['x'] = jax.random.normal(ks[0], (N, D), dtype=jnp.float32)
        inp['edge_index'] = jax.random.randint(ks[1], (2, E), 0, N, dtype=jnp.int32)
        inp['batch'] = jnp.zeros((N,), dtype=jnp.int32)
        inp['edge_attr'] = jax.random.normal(ks[2], (E, 1), dtype=jnp.float32)
        inp['W_ah'] = w(ks[3], (D, D))
        inp['b_ah'] = jnp.zeros((D,), jnp.float32)
        for i in range(3):
            inp[f'W{i}'] = w(ks[4 + 3 * i], (D, H * C))
            inp[f'a_src{i}'] = w(ks[5 + 3 * i], (H, C))
            inp[f'a_dst{i}'] = w(ks[6 + 3 * i], (H, C))
            inp[f'b{i}'] = jnp.zeros((H * C,), jnp.float32)
        inp['W_out'] = w(ks[13], (3 * D, D))
        inp['b_out'] = jnp.zeros((D,), jnp.float32)
        return inp
    _L0_gnn_all = _L0_gnn_setup()
    _L0_gnn_in = {k: v for k, v in _L0_gnn_all.items() if k in ('W_ah', 'b_ah', 'W0', 'a_src0', 'a_dst0', 'b0', 'W1', 'a_src1', 'a_dst1', 'b1', 'W2', 'a_src2', 'a_dst2', 'b2', 'W_out', 'b_out')}
    del _L0_gnn_all

    def _L0_ffn_setup():
        import jax, jax.numpy as jnp
        import numpy as np
        E = 8
        TOP_K = 2
        CAP_RATIO = 1.2
        key = jax.random.key(seed)
        k1, k2, k3, k4 = jax.random.split(key, 4)
        B, L, D, H = (2, 256, 768, 256)
        x = jax.random.normal(k1, (B, L, D), dtype=jnp.float32)
        Wg = jax.random.normal(k2, (D, E), dtype=jnp.float32) * 0.02
        W1 = jax.random.normal(k3, (E, D, 2 * H), dtype=jnp.float32) * 0.02
        W2 = jax.random.normal(k4, (E, H, D), dtype=jnp.float32) * 0.02
        return {'x': x, 'Wg': Wg, 'W1': W1, 'W2': W2}
    _L0_ffn_all = _L0_ffn_setup()
    _L0_ffn_in = {k: v for k, v in _L0_ffn_all.items() if k in ('Wg', 'W1', 'W2')}
    del _L0_ffn_all
    return {'x': x, 'src': src, 'dst': dst, 'edge_weight1': edge_weight1, 'L0_gnn_W_ah': _L0_gnn_in['W_ah'], 'L0_gnn_b_ah': _L0_gnn_in['b_ah'], 'L0_gnn_W0': _L0_gnn_in['W0'], 'L0_gnn_a_src0': _L0_gnn_in['a_src0'], 'L0_gnn_a_dst0': _L0_gnn_in['a_dst0'], 'L0_gnn_b0': _L0_gnn_in['b0'], 'L0_gnn_W1': _L0_gnn_in['W1'], 'L0_gnn_a_src1': _L0_gnn_in['a_src1'], 'L0_gnn_a_dst1': _L0_gnn_in['a_dst1'], 'L0_gnn_b1': _L0_gnn_in['b1'], 'L0_gnn_W2': _L0_gnn_in['W2'], 'L0_gnn_a_src2': _L0_gnn_in['a_src2'], 'L0_gnn_a_dst2': _L0_gnn_in['a_dst2'], 'L0_gnn_b2': _L0_gnn_in['b2'], 'L0_gnn_W_out': _L0_gnn_in['W_out'], 'L0_gnn_b_out': _L0_gnn_in['b_out'], 'L0_ffn_Wg': _L0_ffn_in['Wg'], 'L0_ffn_W1': _L0_ffn_in['W1'], 'L0_ffn_W2': _L0_ffn_in['W2']}

def reference(x, src, dst, edge_weight1, L0_gnn_W_ah, L0_gnn_b_ah, L0_gnn_W0, L0_gnn_a_src0, L0_gnn_a_dst0, L0_gnn_b0, L0_gnn_W1, L0_gnn_a_src1, L0_gnn_a_dst1, L0_gnn_b1, L0_gnn_W2, L0_gnn_a_src2, L0_gnn_a_dst2, L0_gnn_b2, L0_gnn_W_out, L0_gnn_b_out, L0_ffn_Wg, L0_ffn_W1, L0_ffn_W2):
    import jax
    import jax.numpy as jnp

    def _L0_gnn_ref(x, edge_index, batch, edge_attr, W_ah, b_ah, W0, a_src0, a_dst0, b0, W1, a_src1, a_dst1, b1, W2, a_src2, a_dst2, b2, W_out, b_out):
        import jax, jax.numpy as jnp
        import numpy as np
        N, E, D, H, C = (1250, 12500, 768, 4, 192)
        NEG_SLOPE = 0.2

        def gat_conv(x, src, dst, W, a_src, a_dst, b):
            h = (x @ W).reshape(N, H, C)
            as_n = (h * a_src).sum(-1)
            ad_n = (h * a_dst).sum(-1)
            e = jax.nn.leaky_relu(as_n[src] + ad_n[dst], NEG_SLOPE)
            m = jax.ops.segment_max(e, dst, num_segments=N)
            p = jnp.exp(e - m[dst])
            s = jax.ops.segment_sum(p, dst, num_segments=N)
            alpha = p / (s[dst] + 1e-16)
            out = jax.ops.segment_sum(alpha[:, :, None] * h[src], dst, num_segments=N)
            return out.reshape(N, H * C) + b
        loops = jnp.arange(N, dtype=edge_index.dtype)
        src = jnp.concatenate([edge_index[0], loops])
        dst = jnp.concatenate([edge_index[1], loops])
        x1 = jax.nn.relu(x @ W_ah + b_ah)
        xs = [jax.nn.relu(gat_conv(x1, src, dst, W, a_s, a_d, b)) for W, a_s, a_d, b in ((W0, a_src0, a_dst0, b0), (W1, a_src1, a_dst1, b1), (W2, a_src2, a_dst2, b2))]
        node_emb = jnp.concatenate(xs, axis=1)
        return jax.nn.relu(node_emb @ W_out + b_out)

    def _L0_ffn_ref(x, Wg, W1, W2):
        import jax, jax.numpy as jnp
        import numpy as np
        E = 8
        TOP_K = 2
        CAP_RATIO = 1.2
        B, L, D = x.shape
        H = W2.shape[1]
        xf = x.reshape(-1, D)
        N = xf.shape[0]
        capacity = int(CAP_RATIO * N / E)
        logits = xf @ Wg
        scores, idx = jax.lax.top_k(logits, TOP_K)
        weights = jax.nn.softmax(scores, axis=-1)
        xpad = jnp.concatenate([xf, jnp.zeros((1, D), xf.dtype)], axis=0)
        wpad_zero = jnp.zeros((1,), weights.dtype)
        out = jnp.zeros((N, D), x.dtype)
        for k in range(TOP_K):
            ik = idx[:, k]
            onehot = ik[:, None] == jnp.arange(E)[None, :]
            pos = jnp.cumsum(onehot, axis=0) - 1
            posk = jnp.take_along_axis(pos, ik[:, None], axis=1)[:, 0]
            keep = posk < capacity
            buf = jnp.full((E, capacity), N, dtype=jnp.int32)
            buf = buf.at[ik, posk].set(jnp.arange(N, dtype=jnp.int32), mode='drop')
            xg = xpad[buf]
            h = jnp.einsum('ecd,edh->ech', xg, W1)
            act = h[..., :H] * jax.nn.silu(h[..., H:])
            ye = jnp.einsum('ech,ehd->ecd', act, W2)
            wk = jnp.where(keep, weights[:, k], 0.0)
            w_buf = jnp.concatenate([wk, wpad_zero])[buf]
            out = out.at[buf.reshape(-1)].add((w_buf[..., None] * ye).reshape(E * capacity, D), mode='drop')
        return out.reshape(B, L, D)
    edge_index = jnp.stack([src, dst])
    batch0 = jnp.zeros((1250,), jnp.int32)
    x = x + _L0_gnn_ref(_layernorm(x, axis=-1), edge_index, batch0, edge_weight1, L0_gnn_W_ah, L0_gnn_b_ah, L0_gnn_W0, L0_gnn_a_src0, L0_gnn_a_dst0, L0_gnn_b0, L0_gnn_W1, L0_gnn_a_src1, L0_gnn_a_dst1, L0_gnn_b1, L0_gnn_W2, L0_gnn_a_src2, L0_gnn_a_dst2, L0_gnn_b2, L0_gnn_W_out, L0_gnn_b_out)
    x = x + _L0_ffn_ref(_layernorm(x, axis=-1)[None], L0_ffn_Wg, L0_ffn_W1, L0_ffn_W2)[0]
    return x

_drawn_inputs = setup_inputs


def setup_inputs(seed=0):
    import zlib

    import numpy as np

    out = dict(_drawn_inputs(seed))
    spreads = {'L0_gnn_b_ah': (0.0, 0.625),
     'L0_gnn_b0': (0.0, 0.313),
     'L0_gnn_b1': (0.0, 0.326),
     'L0_gnn_b2': (0.0, 0.32),
     'L0_gnn_b_out': (0.0, 0.1)}
    factors = {'L0_gnn_W_ah': 2.824,
     'L0_gnn_a_src0': 8.0,
     'L0_gnn_a_dst0': 8.0,
     'L0_gnn_a_src1': 8.0,
     'L0_gnn_a_dst1': 8.0,
     'L0_gnn_a_src2': 8.0,
     'L0_gnn_a_dst2': 8.0}
    for name, (base, spread) in spreads.items():
        noise = np.random.default_rng([zlib.crc32(name.encode()), seed]).standard_normal(out[name].shape)
        drawn = base * np.exp(spread * noise) if base else spread * noise
        out[name] = jnp.asarray(drawn.astype(out[name].dtype))
    for name, factor in factors.items():
        out[name] = (out[name] * factor).astype(out[name].dtype)
    return out
```

```python
from contextlib import ExitStack

import concourse.bass as bass
from concourse import mybir

F32 = mybir.dt.float32
F16 = mybir.dt.float16
BF16 = mybir.dt.bfloat16
I32 = mybir.dt.int32
U32 = mybir.dt.uint32
I16 = mybir.dt.int16
ALU = mybir.AluOpType
ACT = mybir.ActivationFunctionType
AX = mybir.AxisListType
ds = bass.ds

N = 1250
T = 125
NT = N // T
D = 768
P = 128
KT = D // P
LAYERS = 3
HEADS = 4
C = D // HEADS
CP = C + 1
HEADS_ALL = LAYERS * HEADS
PAIRS = HEADS_ALL // 2
SLOPE = 0.2
LN_EPS = 1e-5
BIG = 1.0e30

E = 20000
ET = E // T
GROUP = 4
SLOTS = GROUP * P
NG = (E + NT * (SLOTS - 1)) // SLOTS
NG += NG % 2
ST = NG * GROUP
CHUNK = 417
CW = 3 * CHUNK
CHUNKS = [(0, CHUNK), (CHUNK, CHUNK), (2 * CHUNK, N - 2 * CHUNK)]

EXPERTS = 8
TOPK = 2
HID = 256
CAP = int(1.2 * N / EXPERTS)
RT = 3
ROWS = RT * T
assert TOPK * CAP < ROWS and NG * SLOTS >= E + NT * (SLOTS - 1) - SLOTS


def gnn_moe(nc, x, src, dst, W_ah, b_ah, Wl, a_src, a_dst, bl, W_out, b_out, Wg, W1, W2, out):
    h_dram = nc.dram_tensor("h_rows", (HEADS_ALL, N, C), F32, kind="Internal").ap()
    logit_rows = nc.dram_tensor("logit_rows", (2 * HEADS_ALL, N), F32, kind="Internal").ap()
    uv_rows = nc.dram_tensor("uv_rows", (2 * HEADS_ALL, N), F32, kind="Internal").ap()
    emb_dram = nc.dram_tensor("emb_t", (LAYERS * D, N), F32, kind="Internal").ap()
    y_dram = nc.dram_tensor("y_rows", (N + 1, D), F32, kind="Internal").ap()
    ye_dram = nc.dram_tensor("expert_rows", (EXPERTS * ROWS, D), F32, kind="Internal").ap()

    with ExitStack() as ctx:
        ctx.enter_context(nc.allow_non_contiguous_dma("bias columns and node tiles"))

        def sem(name):
            return ctx.enter_context(nc.semaphore(name))

        def alloc(stack):
            return lambda name, shape, dt: stack.enter_context(nc.sbuf_tensor(name, shape, dt))

        sb = alloc(ctx)
        PS = ctx.enter_context(nc.psum_tensor("PS", [P, 8, 512], F32))
        PSB = PS[:, :, :].rearrange("p b c -> p (b c)").bitcast(BF16).rearrange("p (b c) -> p b c", b=8)

        ident = sb("ident", [P, P], F32)
        identb = sb("identb", [P, P], BF16)
        iota1 = sb("iota1", [P, CW], F16)
        tri = sb("tri", [T, T], F16)
        ones = sb("ones", [T, T], F16)
        CT = sb("CT", [T, 3 * NT, CHUNK], I16)
        CTf = CT[:, :, :].rearrange("p a b -> p (a b)")
        b_ahT = sb("b_ahT", [P, KT], F32)
        blT = sb("blT", [P, LAYERS * KT], F32)
        as8 = sb("as8", [T, HEADS_ALL * NT], F32)
        as2 = sb("as2", [T, HEADS_ALL * NT], F32)
        small = sb("small", [T, 64], F32)
        tokv = sb("tokv", [T, NT], F32)

        p1 = ExitStack()
        s1 = alloc(p1)
        x1T = s1("x1T", [P, KT, N], F32)
        pa = ExitStack()
        sa = alloc(pa)
        X = sa("X", [T, NT, D], F32)
        xnT = sa("xnT", [P, KT, N], F32)
        pa.close()
        pb = ExitStack()
        sB = alloc(pb)
        NEG = sB("NEG", [T, NT, N], BF16)
        asB = [sB(f"asB{i}", [P, N], F32) for i in range(2)]
        junk = [sB(f"junk{i}", [T, N], BF16) for i in range(2)]
        maskb = [sB(f"maskb{i}", [T, N], BF16) for i in range(2)]
        UVr = sB("UVr", [2 * HEADS_ALL, N], F32)
        Lr = sB("Lr", [2 * HEADS_ALL, N], F32)
        logitc = sB("logitc", [T, NT, 2 * HEADS_ALL], F32)
        Mx = sB("Mx", [T, NT, HEADS_ALL], F32)
        zz = sB("zz", [T, NT, HEADS_ALL], F32)
        UV = sB("UV", [T, NT, 2 * HEADS_ALL], F32)
        pb.close()
        s1("overlaid", [P, max(4 * (NT * D + KT * N), 2 * (NT * N) + 4 * 5 * N + 4 * NT * 72) // 4], F32)
        W = [s1(f"W{i}", [P, KT, D], F32) for i in range(2)]
        aB = s1("aB", [P, 2, D], F32)
        wa = s1("wa", [P, KT, 2 * HEADS_ALL], F32)
        xn = [s1(f"xn{i}", [T, D], F32) for i in range(2)]
        hsb = [s1(f"hsb{i}", [T, D], F32) for i in range(2)]
        wjunk = s1("wjunk", [P, 2, C], F32)
        stats = s1("stats", [T, NT, 12], F32)
        mv = s1("mv", [T, NT, 2], F32)
        ve = s1("ve", [T, NT], F32)
        mhalf = s1("mhalf", [T, NT], F32)
        rstd = s1("rstd", [T, NT], F32)
        srcI = s1("srcI", [T, ET], I32)
        dstI = s1("dstI", [T, ET], I32)
        key = s1("key", [T, ET], F32)
        other1 = s1("other1", [T, ET], F32)
        bucket = s1("bucket", [T, ET], F32)
        local1 = s1("local1", [T, ET], F32)
        inb = s1("inb", [T, NT, ET], F16)
        cum = s1("cum", [T, NT, ET], F16)
        one_row = s1("one_row", [T, ET], F16)
        tot16 = s1("tot16", [T, NT], F16)
        cols = s1("cols", [T, 8, NT], F32)
        colsI = s1("colsI", [T, 2, NT], I32)
        tmpj = s1("tmpj", [T, ET], F32)
        pos = s1("pos", [T, ET], F32)
        posI = s1("posI", [T, 3, ET], I32)
        slot1 = s1("slot1", [T, ET], F32)
        tile1 = s1("tile1", [T, ET], F32)
        gbF = s1("gbF", [1, NG], F32)
        gbI = s1("gbI", [1, NG], I32)
        pick = [s1(f"pick{i}", [T, P], F16) for i in range(4)]
        put = [s1(f"put{i}", [T, 2 * ST], F16) for i in range(4)]
        sorted_ = s1("sorted", [P, 2 * ST], F32)
        oh_src = [s1(f"oh_src{i}", [P, T], F16) for i in range(4)]
        oh_dst = [s1(f"oh_dst{i}", [P, CW], F16) for i in range(4)]
        p1.close()

        p2 = ExitStack()
        s2 = alloc(p2)
        Wo = s2("Wo", [P, LAYERS * KT, D], F32)
        p3 = ExitStack()
        s3 = alloc(p3)
        hs = [s3(f"hs{i}", [T, NT, CP], F32) for i in range(2)]
        uB = [s3(f"uB{i}", [P, N], F32) for i in range(2)]
        vB = [s3(f"vB{i}", [P, N], F32) for i in range(2)]
        tt = [s3(f"tt{i}", [T, N], F32) for i in range(2)]
        ex = [s3(f"ex{i}", [T, N], F32) for i in range(2)]
        pr = [s3(f"pr{i}", [T, N], F32) for i in range(2)]
        col8 = [s3(f"col8_{i}", [T, NT], F32) for i in range(2)]
        col2 = [s3(f"col2_{i}", [T, NT], F32) for i in range(2)]
        bcol = s3("bcol", [P, 3], F32)
        emb = s3("emb", [T, NT, 2 * C], F32)
        embT = s3("embT", [P, 3, N], F32)
        den = s3("den", [T, NT], F32)
        rs = s3("rs", [T, NT], F32)
        p3.close()

        p4 = ExitStack()
        s4 = alloc(p4)
        x2 = s4("x2", [T, NT, D], F32)
        p5 = ExitStack()
        s5 = alloc(p5)
        EB = [s5(f"EB{i}", [P, LAYERS * KT, T], F32) for i in range(2)]
        xr = [s5(f"xr{i}", [T, D], F32) for i in range(2)]
        boB = s5("boB", [P, D], F32)
        rr = s5("rr", [T, D], F32)
        y = [s5(f"y{i}", [T, D], F32) for i in range(2)]
        zrow = s5("zrow", [1, D], F32)
        yT = s5("yT", [P, KT, T], F32)
        WgS = s5("WgS", [P, KT, EXPERTS], F32)
        st2 = s5("st2", [T, 12], F32)
        mv2 = s5("mv2", [T, 4], F32)
        rstd2 = s5("rstd2", [T, 2], F32)
        mh2 = s5("mh2", [T, 1], F32)
        lg = s5("lg", [T, NT, EXPERTS], F32)
        top = s5("top", [T, NT, 8], F32)
        tidx = s5("tidx", [T, NT, 8], U32)
        idxF = s5("idxF", [T, NT, TOPK], F32)
        oh2 = s5("oh2", [T, NT, TOPK * EXPERTS], F16)
        ohp = s5("ohp", [T, NT, TOPK * EXPERTS], F32)
        posk = s5("posk", [T, NT, TOPK], F32)
        keep = s5("keep", [T, NT, TOPK], F32)
        rk = s5("rk", [T, NT, TOPK], F32)
        rsub = s5("rsub", [T, NT, TOPK], F32)
        rtile = s5("rtile", [T, NT, TOPK], F32)
        rslot = s5("rslot", [T, NT, TOPK], F32)
        tmpk = s5("tmpk", [T, NT, TOPK], F32)
        rowF = s5("rowF", [T, NT, TOPK], F32)
        ohs = [s5(f"ohs{i}", [T, T], F16) for i in range(2)]
        oht = [s5(f"oht{i}", [T, EXPERTS * RT], F16) for i in range(2)]
        edt = s5("edt", [T, NT], F32)
        p5.close()
        p4.close()
        p2.close()

        p6 = ExitStack()
        s6 = alloc(p6)
        s6("below_x2", [P, LAYERS * KT * D], F32)
        s6("x2_again", [T, NT, D], F32)
        s6("stage6", [P, 12500], F32)
        rowI = s6("rowI", [T, NT * TOPK], I32)
        tokI = s6("tokI", [T, EXPERTS * RT], I32)
        wk = s6("wk", [T, NT, TOPK], F32)
        p6.close()
        p7 = ExitStack()
        s7 = alloc(p7)
        W1s = [s7(f"W1s{i}", [P, KT, 2 * HID], F32) for i in range(2)]
        W2s = [s7(f"W2s{i}", [P, 2, D], F32) for i in range(2)]
        XgT = s7("XgT", [P, KT, ROWS], F32)
        p7.close()
        p8 = ExitStack()
        s8 = alloc(p8)
        s8("below_x2b", [P, LAYERS * KT * D], F32)
        s8("x2_againb", [T, NT, D], F32)
        Xg = [s8(f"Xg{i}", [T, D], F32) for i in range(3)]
        sg = [s8(f"sg{i}", [P, ROWS], F32) for i in range(2)]
        actT = s8("actT", [P, 2, ROWS], F32)
        ye = [s8(f"ye{i}", [T, D], F32) for i in range(2)]
        g0 = [s8(f"g0{i}", [T, D], F32) for i in range(2)]
        g1 = [s8(f"g1{i}", [T, D], F32) for i in range(2)]
        p8.close()

        s_x = [sem(f"x_tile{t}") for t in range(NT)]
        s_wah = sem("wah_loaded")
        s_small = sem("small_loaded")
        s_edges = sem("edges_loaded")
        s_w = [sem(f"w_loaded{i}") for i in range(2)]
        s_aB = sem("a_rows_loaded")
        s_c = sem("pool_constants")
        s_cv = sem("vector_constants")
        s_ve = sem("variance_ready")
        s_rstd = sem("rstd_ready")
        s_xn = sem("xn_ready")
        s_tp = sem("xn_transposed")
        s_tpe = sem("xnT_stored")
        s_x1 = sem("x1_banks")
        s_x1e = sem("x1T_stored")
        s_h = sem("h_banks")
        s_he = sem("h_evacuated")
        s_hd = [sem(f"h_written{i}") for i in range(2)]
        s_wj = sem("logit_weight_column")
        s_wa = sem("wa_ready")
        s_lr = sem("logit_row_banks")
        s_lre = sem("logit_rows_stored")
        s_lrd = sem("logit_rows_written")
        s_lc = sem("logit_columns")
        s_tot = sem("bucket_totals")
        s_pre = sem("bucket_prefixes")
        s_pick = sem("permutation_ready")
        s_perm = sem("permutation_used")
        s_sorted = sem("edges_sorted")
        s_oh = sem("count_onehots_ready")
        s_ohu = sem("count_onehots_used")
        s_ct = sem("counts_added")
        s_mask = sem("mask_ready")
        s_mt = sem("mask_transposed")
        s_neg = sem("neg_stored")
        s_asB = [sem(f"source_row_loaded{i}") for i in range(2)]
        s_mx = sem("neighbour_max")
        s_uv = sem("uv_columns")
        s_uvt = sem("uv_transposed")
        s_uvr = sem("uv_rows_stored")
        s_uvd = sem("uv_rows_written")
        s_b1 = sem("stage_4_left")
        s_b2 = sem("stage_5_left")
        s_b3 = sem("stage_6_left")
        s_wo = sem("wout_loaded")
        s_hs = [sem(f"h_slice_loaded{i}") for i in range(2)]
        s_bc = sem("pair_bias_loaded")
        s_ones = sem("ones_column")
        s_tt = sem("exponent_ready")
        s_ex = sem("exp_ready")
        s_p = sem("probs_ready")
        s_pu = sem("probs_used")
        s_ob = sem("head_banks_full")
        s_den = sem("row_sums_guarded")
        s_rs = sem("row_sums_inverted")
        s_oe = sem("head_tiles_stored")
        s_tr = sem("emb_transposed")
        s_te = sem("embT_stored")
        s_ed = sem("embT_written")
        s_eb = [sem(f"emb_tile_loaded{i}") for i in range(2)]
        s_xr = [sem(f"residual_loaded{i}") for i in range(2)]
        s_misc = sem("stage6_small_loaded")
        s_pj = sem("projection_banks")
        s_pje = sem("projection_evacuated")
        s_v2 = sem("variance2_ready")
        s_r2 = sem("rstd2_ready")
        s_y = sem("y_ready")
        s_yd = [sem(f"y_written{i}") for i in range(2)]
        s_yt = sem("y_transposed")
        s_yte = sem("yT_stored")
        s_lg = sem("gate_logits")
        s_oh2 = sem("expert_onehots")
        s_cum = sem("expert_counts")
        s_sm = sem("gate_differences")
        s_sme = sem("gate_exp")
        s_tk = sem("token_onehots")
        s_tku = sem("token_onehots_used")
        s_zr = sem("zero_row_written")
        s_w1 = [sem(f"expert_w1_loaded{i}") for i in range(2)]
        s_w2 = [sem(f"expert_w2_loaded{i}") for i in range(2)]
        s_xg = [sem(f"rows_gathered{i}") for i in range(3)]
        s_xt = sem("rows_transposed")
        s_xte = sem("rows_transposed_stored")
        s_h1 = sem("hidden_banks")
        s_sg = sem("silu_ready")
        s_ac = sem("hidden_act_ready")
        s_ye = sem("expert_out_banks")
        s_yee = sem("expert_out_stored")
        s_yed = [sem(f"expert_rows_written{i}") for i in range(2)]
        s_g0 = [sem(f"first_rows_gathered{i}") for i in range(2)]
        s_g1 = [sem(f"second_rows_gathered{i}") for i in range(2)]
        s_fin = sem("result_ready")
        s_od = [sem(f"result_written{i}") for i in range(2)]
        s_dch = sem("vector_chain")
        s_gch = sem("pool_chain")

        def row(ap):
            return ap.rearrange("(o n) -> o n", o=1)

        block = ctx.enter_context(nc.Block())

        @block.sync
        def _(sp):
            for t in range(NT):
                sp.dma_start(X[:, t, :], x[t * T:(t + 1) * T, :]).then_inc(s_x[t], 16)
            sp.dma_start(W[0][:, :, :], W_ah.rearrange("(k p) n -> p k n", p=P)).then_inc(s_wah, 16)
            sp.dma_start(b_ahT[:, :], b_ah.rearrange("(k p) -> p k", p=P)).then_inc(s_small, 16)
            for l in range(LAYERS):
                sp.dma_start(blT[:, l * KT:(l + 1) * KT],
                             bl[l].rearrange("(k p) -> p k", p=P)).then_inc(s_small, 16)
            for l in range(LAYERS):
                b = (l + 1) % 2
                if l > 0:
                    if l == 1:
                        sp.wait_ge(s_x1, 3 * KT)
                    else:
                        sp.wait_ge(s_h, NT * (l - 1))
                        sp.wait_ge(s_wa, l - 1)
                    sp.wait_ge(s_wa, l)
                sp.dma_start(W[b][:, :, :], Wl[l].rearrange("(k p) n -> p k n", p=P)).then_inc(s_w[b], 16)
                for i, a in enumerate((a_src[l], a_dst[l])):
                    sp.dma_start(aB[:, i, :], row(a.rearrange("h c -> (h c)")).broadcast_to([P, D])).then_inc(s_aB, 16)
            sp.wait_ge(s_lre, 3)
            sp.dma_start(logit_rows[:, :], Lr[:, :]).then_inc(s_lrd, 16)
            sp.wait_ge(s_lrd, 16)
            for j in range(HEADS_ALL):
                l, h = divmod(j, HEADS)
                if j >= 2:
                    sp.wait_ge(s_mx, NT * (j - 1))
                r0 = l * 2 * HEADS + h
                sp.dma_start(asB[j % 2][:, :], logit_rows[r0:r0 + 1, :].broadcast_to([P, N])).then_inc(s_asB[j % 2], 16)
            sp.wait_ge(s_uvr, 3)
            sp.dma_start(uv_rows[:, :], UVr[:, :]).then_inc(s_uvd, 16)
            sp.wait_ge(s_uvd, 16)
            sp.wait_ge(s_hd[0], 16 * LAYERS * NT // 2)
            sp.wait_ge(s_hd[1], 16 * LAYERS * NT // 2)
            sp.wait_ge(s_b1, 4)
            sp.dma_start(Wo[:, :, :], W_out.rearrange("(k p) n -> p k n", p=P)).then_inc(s_wo, 16)

            def load_head(hh, head):
                sp.dma_start(hs[hh][:, :, 0:C], h_dram[ds(head, 1)].rearrange("o (t p) c -> p (o t) c", p=T)
                             ).then_inc(s_hs[hh], 16)
                sp.dma_start(uB[hh][:, :], uv_rows[ds(head, 1), :].broadcast_to([P, N])).then_inc(s_hs[hh], 16)
                sp.dma_start(vB[hh][:, :], uv_rows[ds(head + HEADS_ALL, 1), :].broadcast_to([P, N])
                             ).then_inc(s_hs[hh], 16)
                sp.dma_start(col8[hh][:, :], as8[:, ds(head * NT, NT)]).then_inc(s_hs[hh], 16)
                sp.dma_start(col2[hh][:, :], as2[:, ds(head * NT, NT)]).then_inc(s_hs[hh], 16)

            def load_bias(pair):
                sp.dma_start(bcol[:, :], blT[:, ds(pair * 3, 3)]).then_inc(s_bc, 16)

            def store_pair(pair):
                sp.wait_ge(s_te, 3 + 9 * pair + 9)
                sp.dma_start(emb_dram.rearrange("(r k p) n -> r p k n", k=3, p=P)[ds(pair, 1)]
                             .rearrange("o p k n -> (o p) k n"), embT[:, :, :]).then_inc(s_ed, 16)
            load_bias(0)
            for hh in range(2):
                load_head(hh, hh)
            with sp.Fori(0, PAIRS - 1) as i:
                for hh in range(2):
                    sp.wait_ge(s_pu, 2 + i * 2 * NT + (hh + 1) * NT)
                    load_head(hh, i * 2 + 2 + hh)
                store_pair(i)
                load_bias(i + 1)
            store_pair(PAIRS - 1)
            sp.wait_ge(s_ed, 16 * (PAIRS + 1))
            sp.wait_ge(s_b2, 3)
            sp.dma_start(boB[:, :], row(b_out).broadcast_to([P, D])).then_inc(s_misc, 16)
            sp.dma_start(WgS[:, :, :], Wg.rearrange("(k p) e -> p k e", p=P)).then_inc(s_misc, 16)
            for t in range(NT):
                if t >= 2:
                    sp.wait_ge(s_pje, 2 * (t - 1))
                sp.dma_start(EB[t % 2][:, :, :], emb_dram.rearrange("(k p) n -> p k n", p=P)[:, :, t * T:(t + 1) * T]
                             ).then_inc(s_eb[t % 2], 16)
                sp.dma_start(xr[t % 2][:, :], x[t * T:(t + 1) * T, :]).then_inc(s_xr[t % 2], 16)
                if t >= 1:
                    sp.wait_ge(s_y, t)
                    sp.dma_start(y_dram[(t - 1) * T:t * T, :], y[(t - 1) % 2][:, :]).then_inc(s_yd[(t - 1) % 2], 16)
            sp.wait_ge(s_y, NT)
            sp.dma_start(y_dram[(NT - 1) * T:NT * T, :], y[(NT - 1) % 2][:, :]).then_inc(s_yd[(NT - 1) % 2], 16)
            sp.wait_ge(s_zr, 1)
            sp.dma_start(y_dram[N:N + 1, :], zrow[:, :]).then_inc(s_zr, 16)
            sp.wait_ge(s_b3, 3)
            for e in range(EXPERTS):
                if e >= 2:
                    sp.wait_ge(s_h1, 4 * (e - 1))
                    sp.wait_ge(s_ye, RT * (e - 1))
                sp.dma_start(W1s[e % 2][:, :, :], W1[e].rearrange("(k p) n -> p k n", p=P)).then_inc(s_w1[e % 2], 16)
                sp.dma_start(W2s[e % 2][:, :, :], W2[e].rearrange("(k p) n -> p k n", p=P)).then_inc(s_w2[e % 2], 16)
            for t in range(NT):
                sp.wait_ge(s_fin, t + 1)
                sp.dma_start(out[t * T:(t + 1) * T, :], g1[t % 2][:, :]).then_inc(s_od[t % 2], 16)
            for q in range(2):
                sp.wait_ge(s_od[q], 16 * NT // 2)

        @block.gpsimd
        def _(g):
            chain = [0]

            def link(ins):
                chain[0] += 1
                ins.then_inc(s_gch, 1)
                g.wait_ge(s_gch, chain[0])

            g.dma_start(srcI[:, :], src.rearrange("(p t) -> p t", p=T)).then_inc(s_edges, 16)
            g.dma_start(dstI[:, :], dst.rearrange("(p t) -> p t", p=T)).then_inc(s_edges, 16)
            g.iota(iota1[:, :], [[1, CW]], base=1, channel_multiplier=0,
                   allow_small_or_imprecise_dtypes=True).then_inc(s_c, 1)
            link(g.memset(ident[:, :], 0.0))
            link(g.memset(tri[:, :], 1.0))
            g.affine_select(out=ident[:, :], in_=ident[:, :], compare_op=ALU.not_equal, fill=1.0, base=0,
                            pattern=[[-1, P]], channel_multiplier=1).then_inc(s_c, 1)
            g.affine_select(out=tri[:, :], in_=tri[:, :], compare_op=ALU.is_gt, fill=0.0, base=0,
                            pattern=[[1, T]], channel_multiplier=-1).then_inc(s_c, 1)
            g.memset(ones[:, :], 1.0).then_inc(s_c, 1)
            g.iota(tokv[:, :], [[T, NT]], base=-N, channel_multiplier=1,
                   allow_small_or_imprecise_dtypes=True).then_inc(s_c, 1)
            g.memset(mhalf[:, :], -0.5).then_inc(s_gch, 1)
            chain[0] += 1
            g.wait_ge(s_gch, chain[0])
            g.wait_ge(s_ve, 1)
            g.tensor_tensor(rstd[:, :], ve[:, :], mhalf[:, :], ALU.pow).then_inc(s_rstd, 1)
            g.drain()
            g.sem_inc(s_b1, 1)
            g.wait_ge(s_b2, 3)
            link(g.memset(mh2[:, :], -0.5))
            for t in range(NT):
                g.wait_ge(s_v2, t + 1)
                g.tensor_tensor(rstd2[:, t % 2:t % 2 + 1], mv2[:, 2:3], mh2[:, :], ALU.pow).then_inc(s_r2, 1)
            g.wait_ge(s_b3, 3)
            g.wait_ge(s_yd[0], 16 * NT // 2)
            g.wait_ge(s_yd[1], 16 * NT // 2)
            g.wait_ge(s_zr, 17)
            for u in range(EXPERTS * RT):
                if u >= RT:
                    g.wait_ge(s_xt, 2 * (u - RT + 1))
                g.indirect_dma_start(out=Xg[u % 3][:, :], out_offset=None, in_=y_dram[:, :],
                                     in_offset=bass.IndirectOffsetOnAxis(ap=tokI[:, u:u + 1], axis=0)
                                     ).then_inc(s_xg[u % 3], 16)
            for q in range(2):
                g.wait_ge(s_yed[q], 16 * EXPERTS * RT // 2)
            for t in range(NT):
                if t >= 2:
                    g.wait_ge(s_od[t % 2], 16 * (t // 2))
                    g.wait_ge(s_fin, t - 1)
                for k, (gb, sg_) in enumerate(((g0, s_g0), (g1, s_g1))):
                    g.indirect_dma_start(out=gb[t % 2][:, :], out_offset=None, in_=ye_dram[:, :],
                                         in_offset=bass.IndirectOffsetOnAxis(
                                             ap=rowI[:, TOPK * t + k:TOPK * t + k + 1], axis=0)
                                         ).then_inc(sg_[t % 2], 16)

        @block.tensor
        def _(pe):
            pe.wait_ge(s_c, 5)
            for t in range(NT):
                pe.wait_ge(s_xn, t + 1)
                for half in range(2):
                    u = 2 * t + half
                    if u >= 4:
                        pe.wait_ge(s_tpe, u - 3)
                    for k in range(3):
                        mm = pe.transpose(PS[:, u % 4, k * T:(k + 1) * T], xn[t % 2][:, (3 * half + k) * P:(3 * half + k + 1) * P],
                                          ident[0:T, 0:T])
                    mm.then_inc(s_tp, 1)
            pe.wait_ge(s_wah, 16)
            pe.wait_ge(s_tpe, 2 * NT)
            for m in range(KT):
                for c, (c0, cn) in enumerate(CHUNKS):
                    u = 3 * m + c
                    if u >= 2:
                        pe.wait_ge(s_x1e, u - 1)
                    for k in range(KT):
                        mm = pe.matmul(PS[:, 4 + u % 2, 0:cn], W[0][:, k, m * P:(m + 1) * P], xnT[:, k, c0:c0 + cn],
                                       start=(k == 0), stop=(k == KT - 1))
                    mm.then_inc(s_x1, 1)
            pe.wait_ge(s_tot, 1)
            pe.matmul(PS[0:T, 7, 0:NT], tri[:, :], tot16[:, :], start=True, stop=True)
            pe.matmul(PS[0:T, 7, 16:16 + NT], ones[:, :], tot16[:, :], start=True, stop=True).then_inc(s_pre, 1)

            def permute(q, n, first=False, last=False):
                pe.wait_ge(s_pick, n)
                pe.matmul(PS[:, 6, 0:2 * ST], pick[q][:, :], put[q][:, :], start=first, stop=last,
                          skip_group_check=True).then_inc(s_perm, 1)
            for q in range(4):
                permute(q, q + 1, first=(q == 0))
            with pe.Fori(1, ET // 4) as i:
                for q in range(4):
                    permute(q, i * 4 + q + 1)
            pe.wait_ge(s_x1e, 3 * KT)
            for l in range(LAYERS):
                b = (l + 1) % 2
                pe.wait_ge(s_w[b], 16 * (l // 2 + 1))
                for t in range(NT):
                    u = l * NT + t
                    if u >= 2:
                        pe.wait_ge(s_he, u - 1)
                    for c in range(2):
                        for k in range(KT):
                            mm = pe.matmul(PS[0:T, 2 * (u % 2) + c, 0:D // 2], x1T[:, k, t * T:(t + 1) * T],
                                           W[b][:, k, c * D // 2:(c + 1) * D // 2], start=(k == 0), stop=(k == KT - 1))
                    mm.then_inc(s_h, 1)
            pe.wait_ge(s_wa, LAYERS)
            for c, (c0, cn) in enumerate(CHUNKS):
                if c == 2:
                    pe.wait_ge(s_lre, 1)
                for k in range(KT):
                    mm = pe.matmul(PS[0:2 * HEADS_ALL, 4 + c % 2, 0:cn], wa[:, k, :], x1T[:, k, c0:c0 + cn],
                                   start=(k == 0), stop=(k == KT - 1))
                mm.then_inc(s_lr, 1)
            for t in range(NT):
                for k in range(KT):
                    mm = pe.matmul(PS[0:T, 7, t * 24:(t + 1) * 24], x1T[:, k, t * T:(t + 1) * T], wa[:, k, :],
                                   start=(k == 0), stop=(k == KT - 1))
            mm.then_inc(s_lc, 1)
            pe.wait_ge(s_he, LAYERS * NT)
            pe.wait_ge(s_lre, 3)

            def count(par, n):
                for q in range(GROUP):
                    pe.wait_ge(s_oh, n * GROUP + q + 1)
                    for c in range(3):
                        mm = pe.matmul(PS[0:T, 3 * par + c, 0:CHUNK], oh_src[q][:, :], oh_dst[q][:, c * CHUNK:(c + 1) * CHUNK],
                                       start=(q == 0), stop=(q == GROUP - 1))
                    mm.then_inc(s_ohu, 1)
            with pe.Fori(0, NG // 2) as i:
                for par in range(2):
                    pe.wait_ge(s_ct, i * 2 + par + 1)
                    count(par, i * 2 + par)
            pe.wait_ge(s_lc, 1)
            for s in range(NT):
                pe.wait_ge(s_mask, s + 1)
                for half in range(2):
                    u = 2 * s + half
                    if u >= 2:
                        pe.wait_ge(s_neg, u - 1)
                    for k in range(5):
                        mm = pe.transpose(PSB[0:T, 6 + half, k * 126:k * 126 + T],
                                          maskb[s % 2][:, (5 * half + k) * T:(5 * half + k + 1) * T], identb[0:T, 0:T])
                    mm.then_inc(s_mt, 1)
            pe.wait_ge(s_uv, 1)
            for t in range(NT):
                mm = pe.transpose(PS[0:2 * HEADS_ALL, t // 4, (t % 4) * T:(t % 4 + 1) * T], UV[:, t, :], ident[0:T, 0:T])
                if t in (3, 7, 9):
                    mm.then_inc(s_uvt, 1)
            pe.drain()
            pe.sem_inc(s_b1, 1)
            pe.sem_inc(s_tr, 1)
            pe.sem_inc(s_pu, 2)
            pe.wait_ge(s_ones, 2)
            with pe.Fori(0, PAIRS) as i:
                for hh in range(2):
                    pe.wait_ge(s_hs[hh], i * 80 + 80)
                    for st in range(NT):
                        pe.wait_ge(s_p, i * 2 * NT + hh * NT + st + 3)
                        for dt in range(NT):
                            b, r = divmod(dt, 2)
                            if st == 0 and r == 0:
                                pe.wait_ge(s_oe, i * 2 * NT + hh * NT + 2 * (b + 1))
                            mm = pe.matmul(PS[0:T, b, r * 256:r * 256 + CP], pr[st % 2][:, dt * T:(dt + 1) * T],
                                           hs[hh][:, st, :], start=(st == 0 and r == 0), stop=(st == NT - 1),
                                           skip_group_check=True)
                            if st == NT - 1 and r == 1 and b < 4:
                                mm.then_inc(s_ob, 1)
                        mm.then_inc(s_pu, 1)
                pe.wait_ge(s_oe, i * 2 * NT + 2 * NT + NT)
                for k in range(3):
                    for q in range(3):
                        u = 3 * k + q
                        pe.wait_ge(s_te, i * 9 + u + 1)
                        for t in range(4 * q, min(4 * q + 4, NT)):
                            mm = pe.transpose(PS[:, 5 + q, (t % 4) * T:(t % 4 + 1) * T], emb[:, t, k * P:(k + 1) * P],
                                              ident[0:T, 0:T])
                        mm.then_inc(s_tr, 1)
            pe.drain()
            pe.sem_inc(s_b2, 1)
            pe.wait_ge(s_wo, 16)
            pe.wait_ge(s_misc, 32)
            for t in range(NT):
                pe.wait_ge(s_eb[t % 2], 16 * (t // 2 + 1))
                if t == 0:
                    pe.wait_ge(s_te, 3 + 9 * PAIRS)
                if t >= 2:
                    pe.wait_ge(s_pje, 2 * (t - 1))
                for c in range(2):
                    for k in range(LAYERS * KT):
                        mm = pe.matmul(PS[0:T, 2 * (t % 2) + c, 0:D // 2], EB[t % 2][:, k, :],
                                       Wo[:, k, c * D // 2:(c + 1) * D // 2], start=(k == 0), stop=(k == LAYERS * KT - 1))
                    mm.then_inc(s_pj, 1)
                pe.wait_ge(s_y, t + 1)
                for half in range(2):
                    if t >= 1:
                        pe.wait_ge(s_yte, 2 * (t - 1) + half + 1)
                    for k in range(3):
                        mm = pe.transpose(PS[:, 4 + half, k * T:(k + 1) * T], y[t % 2][:, (3 * half + k) * P:(3 * half + k + 1) * P],
                                          ident[0:T, 0:T])
                    mm.then_inc(s_yt, 1)
                pe.wait_ge(s_yte, 2 * t + 2)
                for k in range(KT):
                    mm = pe.matmul(PS[0:T, 6, t * EXPERTS:(t + 1) * EXPERTS], yT[:, k, :], WgS[:, k, :],
                                   start=(k == 0), stop=(k == KT - 1))
                mm.then_inc(s_lg, 1)
            pe.wait_ge(s_oh2, 1)
            for t in range(NT):
                for q in range(t):
                    pe.matmul(PS[0:T, 7, t * 16:(t + 1) * 16], ones[:, :], oh2[:, q, :], start=(q == 0), stop=False)
                mm = pe.matmul(PS[0:T, 7, t * 16:(t + 1) * 16], tri[:, :], oh2[:, t, :], start=(t == 0), stop=True)
            mm.then_inc(s_cum, 1)
            for u in range(TOPK * NT):
                pe.wait_ge(s_tk, u + 1)
                mm = pe.matmul(PS[0:T, 0, 0:EXPERTS * RT], ohs[u % 2][:, :], oht[u % 2][:, :], start=(u == 0),
                               stop=(u == TOPK * NT - 1)).then_inc(s_tku, 1)
            pe.drain()
            pe.sem_inc(s_b3, 1)
            pe.wait_ge(s_b3, 3)
            for e in range(EXPERTS):
                for j in range(RT):
                    u = e * RT + j
                    pe.wait_ge(s_xg[u % 3], 16 * (u // 3 + 1))
                    for half in range(2):
                        v = 2 * u + half
                        if v >= 2:
                            pe.wait_ge(s_xte, v - 1)
                        for k in range(3):
                            mm = pe.transpose(PS[:, half, k * T:(k + 1) * T], Xg[u % 3][:, (3 * half + k) * P:(3 * half + k + 1) * P],
                                              ident[0:T, 0:T])
                        mm.then_inc(s_xt, 1)
                pe.wait_ge(s_xte, 2 * RT * (e + 1))
                pe.wait_ge(s_w1[e % 2], 16 * (e // 2 + 1))
                if e >= 1:
                    pe.wait_ge(s_ac, 2 * e)
                for m in (2, 3, 0, 1):
                    for k in range(KT):
                        mm = pe.matmul(PS[:, 2 + m, 0:ROWS], W1s[e % 2][:, k, m * P:(m + 1) * P], XgT[:, k, :],
                                       start=(k == 0), stop=(k == KT - 1))
                    mm.then_inc(s_h1, 1)
                pe.wait_ge(s_w2[e % 2], 16 * (e // 2 + 1))
                pe.wait_ge(s_ac, 2 * (e + 1))
                for j in range(RT):
                    u = e * RT + j
                    if u >= 1:
                        pe.wait_ge(s_yee, u)
                    for c in range(2):
                        for k in range(2):
                            mm = pe.matmul(PS[0:T, 6 + c, 0:D // 2], actT[:, k, j * T:(j + 1) * T],
                                           W2s[e % 2][:, k, c * D // 2:(c + 1) * D // 2], start=(k == 0), stop=(k == 1))
                    mm.then_inc(s_ye, 1)

        @block.scalar
        def _(act):
            for u in range(2 * NT):
                t, half = divmod(u, 2)
                act.wait_ge(s_tp, u + 1)
                act.activation(xnT[:, 3 * half:3 * half + 3, t * T:(t + 1) * T],
                               PS[:, u % 4, 0:3 * T].rearrange("p (k n) -> p k n", k=3), ACT.Copy).then_inc(s_tpe, 1)
            act.wait_ge(s_small, 64)
            for m in range(KT):
                for c, (c0, cn) in enumerate(CHUNKS):
                    u = 3 * m + c
                    act.wait_ge(s_x1, u + 1)
                    act.activation(x1T[:, m, c0:c0 + cn], PS[:, 4 + u % 2, 0:cn], ACT.Relu,
                                   bias=b_ahT[:, m:m + 1]).then_inc(s_x1e, 1)
            for u in range(LAYERS * NT):
                act.wait_ge(s_h, u + 1)
                if u >= 2:
                    act.wait_ge(s_hd[u % 2], 16 * (u // 2))
                act.activation(hsb[u % 2][:, :].rearrange("p (a b) -> p a b", a=2),
                               PS[0:T, 2 * (u % 2):2 * (u % 2) + 2, 0:D // 2], ACT.Copy).then_inc(s_he, 1)
                act.wait_ge(s_he, u + 1)
                l, t = divmod(u, NT)
                act.dma_start(h_dram[l * HEADS:(l + 1) * HEADS, t * T:(t + 1) * T, :].rearrange("q p c -> p q c"),
                              hsb[u % 2][:, :].rearrange("p (q c) -> p q c", q=HEADS)).then_inc(s_hd[u % 2], 16)
            for c, (c0, cn) in enumerate(CHUNKS):
                act.wait_ge(s_lr, c + 1)
                if c == 0:
                    act.wait_ge(s_x1e, 3 * KT)
                act.activation(Lr[:, c0:c0 + cn], PS[0:2 * HEADS_ALL, 4 + c % 2, 0:cn], ACT.Copy).then_inc(s_lre, 1)
            for q, (t0, t1) in enumerate(((0, 4), (4, 8), (8, 10))):
                act.wait_ge(s_uvt, q + 1)
                act.activation(UVr[:, t0 * T:t1 * T], PS[0:2 * HEADS_ALL, q, 0:(t1 - t0) * T], ACT.Copy).then_inc(s_uvr, 1)
            act.drain()
            act.sem_inc(s_b1, 1)
            act.wait_ge(s_b1, 4)
            act.sem_inc(s_oe, NT)
            act.sem_inc(s_te, 3)
            act.sem_inc(s_ex, 2)
            act.sem_inc(s_ed, 16)
            with act.Fori(0, PAIRS) as i:
                def exp(hh, st):
                    u = hh * NT + st
                    act.wait_ge(s_tt, i * 2 * NT + u + 1)
                    act.wait_ge(s_p, i * 2 * NT + u + 1)
                    act.activation(ex[st % 2][:, :], tt[st % 2][:, :], ACT.Exp,
                                   bias=col2[hh][:, st:st + 1]).then_inc(s_ex, 1)

                def store(hh):
                    for dt in range(NT):
                        b, r = divmod(dt, 2)
                        if r == 0:
                            act.wait_ge(s_rs, i * 10 + hh * 5 + b + 1)
                            if hh == 0 and b == 0:
                                act.wait_ge(s_tr, i * 9 + 1)
                        act.activation(emb[:, dt, hh * C:(hh + 1) * C], PS[0:T, b, r * 256:r * 256 + C], ACT.Copy,
                                       scale=rs[:, dt:dt + 1]).then_inc(s_oe, 1)
                for st in range(NT):
                    exp(0, st)
                exp(1, 0)
                exp(1, 1)
                store(0)
                for st in range(2, NT):
                    exp(1, st)
                store(1)
                act.wait_ge(s_ed, i * 16 + 16)
                act.wait_ge(s_bc, i * 16 + 16)
                for k in range(3):
                    for q in range(3):
                        u = 3 * k + q
                        n = min(4, NT - 4 * q) * T
                        act.wait_ge(s_tr, i * 9 + u + 2)
                        act.activation(embT[:, k, 4 * q * T:4 * q * T + n], PS[:, 5 + q, 0:n], ACT.Relu,
                                       bias=bcol[:, k:k + 1]).then_inc(s_te, 1)
            act.drain()
            act.sem_inc(s_b2, 1)
            for t in range(NT):
                for half in range(2):
                    act.wait_ge(s_yt, 2 * t + half + 1)
                    if t >= 1 and half == 0:
                        act.wait_ge(s_lg, t)
                    act.activation(yT[:, 3 * half:3 * half + 3, :],
                                   PS[:, 4 + half, 0:3 * T].rearrange("p (k n) -> p k n", k=3), ACT.Copy).then_inc(s_yte, 1)
            act.wait_ge(s_sm, 1)
            act.activation(edt[:, :], small[:, 0:NT], ACT.Exp).then_inc(s_sme, 1)
            act.drain()
            act.sem_inc(s_b3, 1)
            act.wait_ge(s_b3, 3)
            for e in range(EXPERTS):
                for j in range(RT):
                    for half in range(2):
                        v = 2 * (e * RT + j) + half
                        act.wait_ge(s_xt, v + 1)
                        if e >= 1 and j == 0 and half == 0:
                            act.wait_ge(s_h1, 4 * e)
                        act.activation(XgT[:, 3 * half:3 * half + 3, j * T:(j + 1) * T],
                                       PS[:, half, 0:3 * T].rearrange("p (k n) -> p k n", k=3), ACT.Copy).then_inc(s_xte, 1)
                for m in range(2):
                    act.wait_ge(s_h1, 4 * e + m + 1)
                    if e >= 1:
                        act.wait_ge(s_ac, 2 * (e - 1) + m + 1)
                    act.activation(sg[m][:, :], PS[:, 4 + m, 0:ROWS], ACT.Silu).then_inc(s_sg, 1)
                for j in range(RT):
                    u = e * RT + j
                    act.wait_ge(s_ye, u + 1)
                    if u >= 2:
                        act.wait_ge(s_yed[u % 2], 16 * (u // 2))
                    act.activation(ye[u % 2][:, :].rearrange("p (a b) -> p a b", a=2), PS[0:T, 6:8, 0:D // 2],
                                   ACT.Copy).then_inc(s_yee, 1)
                    act.wait_ge(s_yee, u + 1)
                    act.dma_start(ye_dram[u * T:(u + 1) * T, :], ye[u % 2][:, :]).then_inc(s_yed[u % 2], 16)

        @block.vector
        def _(v):
            chain = [0]

            def link(ins):
                chain[0] += 1
                ins.then_inc(s_dch, 1)
                v.wait_ge(s_dch, chain[0])

            link(v.memset(CTf, 0))
            link(v.memset(one_row[:, :], 1.0))
            for t in range(NT):
                v.wait_ge(s_x[t], 16)
                v.bn_stats(stats[:, t, 0:6], X[:, t, 0:D // 2]).then_inc(s_dch, 1)
                chain[0] += 1
                link(v.bn_stats(stats[:, t, 6:12], X[:, t, D // 2:D]))
                link(v.bn_aggr(mv[:, t, :], stats[:, t, :]))
            v.tensor_scalar(ve[:, :], mv[:, :, 1], LN_EPS, None, ALU.add).then_inc(s_ve, 1)
            v.wait_ge(s_rstd, 1)
            for t in range(NT):
                if t >= 2:
                    v.wait_ge(s_tp, 2 * (t - 1))
                v.tensor_scalar(xn[t % 2][:, :], X[:, t, :], mv[:, t, 0:1], rstd[:, t:t + 1], ALU.subtract,
                                ALU.mult).then_inc(s_xn, 1)
            v.wait_ge(s_c, 5)
            v.wait_ge(s_edges, 32)
            link(v.tensor_copy(identb[:, :], ident[:, :]))
            link(v.tensor_copy(key[:, :], srcI[:, :]))
            link(v.tensor_scalar(other1[:, :], dstI[:, :], 1.0, None, ALU.add))
            link(v.tensor_scalar(bucket[:, :], key[:, :], float(T), None, ALU.is_ge))
            for j in range(2, NT):
                link(v.scalar_tensor_tensor(out=bucket[:, :], in0=key[:, :], scalar=float(T * j), in1=bucket[:, :],
                                            op0=ALU.is_ge, op1=ALU.add))
            link(v.scalar_tensor_tensor(out=local1[:, :], in0=bucket[:, :], scalar=-float(T), in1=key[:, :],
                                        op0=ALU.mult, op1=ALU.add))
            link(v.tensor_scalar(local1[:, :], local1[:, :], 1.0, None, ALU.add))
            for j in range(NT):
                link(v.tensor_scalar(inb[:, j, :], bucket[:, :], float(j), None, ALU.is_equal))
                link(v.tensor_tensor_scan(cum[:, j, :], one_row[:, :], inb[:, j, :], 0.0, ALU.mult, ALU.add))
            v.tensor_copy(tot16[:, :], cum[:, :, ET - 1]).then_inc(s_tot, 1)
            v.wait_ge(s_pre, 1)
            link(v.tensor_scalar(colsI[:, 0, :], PS[0:T, 7, 16:16 + NT], float(SLOTS - 1), None, ALU.add))
            link(v.tensor_scalar(colsI[:, 1, :], colsI[:, 0, :], SLOTS.bit_length() - 1, None, ALU.arith_shift_right))
            link(v.tensor_copy(cols[:, 0, :], colsI[:, 1, :]))
            link(v.tensor_tensor_scan(cols[:, 1, :], one_row[:, 0:NT], cols[:, 0, :], 0.0, ALU.mult, ALU.add))
            link(v.tensor_tensor(cols[:, 2, :], cols[:, 1, :], cols[:, 0, :], ALU.subtract))
            link(v.scalar_tensor_tensor(out=cols[:, 3, :], in0=cols[:, 2, :], scalar=float(SLOTS), in1=PS[0:T, 7, 0:NT],
                                        op0=ALU.mult, op1=ALU.add))
            link(v.tensor_scalar(cols[:, 4, :], cols[:, 3, :], -1.0, None, ALU.add))
            for j in range(NT):
                dstt = pos if j == 0 else tmpj
                link(v.scalar_tensor_tensor(out=dstt[:, :], in0=cum[:, j, :], scalar=cols[:, 4, j:j + 1], in1=inb[:, j, :],
                                            op0=ALU.add, op1=ALU.mult))
                if j:
                    link(v.tensor_tensor(pos[:, :], pos[:, :], tmpj[:, :], ALU.add))
            link(v.tensor_copy(posI[:, 0, :], pos[:, :]))
            link(v.tensor_scalar(posI[:, 1, :], posI[:, 0, :], P - 1, None, ALU.bitwise_and))
            link(v.tensor_scalar(posI[:, 2, :], posI[:, 0, :], P.bit_length() - 1, None, ALU.arith_shift_right))
            link(v.tensor_scalar(slot1[:, :], posI[:, 1, :], 1.0, None, ALU.add))
            link(v.tensor_scalar(tile1[:, :], posI[:, 2, :], 1.0, None, ALU.add))
            link(v.tensor_scalar(gbF[:, :], iota1[0:1, 0:NG], cols[0:1, 2, 1:2], None, ALU.is_gt))
            for j in range(2, NT):
                link(v.scalar_tensor_tensor(out=gbF[:, :], in0=iota1[0:1, 0:NG], scalar=cols[0:1, 2, j:j + 1],
                                            in1=gbF[:, :], op0=ALU.is_gt, op1=ALU.add))
            link(v.tensor_scalar(gbI[:, :], gbF[:, :], 3.0, None, ALU.mult))

            def place(q, t, free=None):
                if free is not None:
                    v.wait_ge(s_perm, free)
                v.tensor_scalar(pick[q][:, :], iota1[0:T, 0:P], slot1[:, ds(t, 1)], None, ALU.is_equal)
                v.tensor_scalar(put[q][:, 0:ST], iota1[0:T, 0:ST], tile1[:, ds(t, 1)], local1[:, ds(t, 1)],
                                ALU.is_equal, ALU.mult)
                v.tensor_scalar(put[q][:, ST:2 * ST], iota1[0:T, 0:ST], tile1[:, ds(t, 1)], other1[:, ds(t, 1)],
                                ALU.is_equal, ALU.mult).then_inc(s_pick, 1)
            for q in range(4):
                place(q, q)
            with v.Fori(1, ET // 4) as i:
                for q in range(4):
                    place(q, i * 4 + q, i * 4 + q - 3)
            v.wait_ge(s_perm, ET)
            v.tensor_copy(sorted_[:, :], PS[:, 6, 0:2 * ST]).then_inc(s_sorted, 1)
            v.wait_ge(s_sorted, 1)
            nj = 0
            for l in range(LAYERS):
                b = (l + 1) % 2
                v.wait_ge(s_w[b], 16 * (l // 2 + 1))
                v.wait_ge(s_aB, 32 * (l + 1))
                for k in range(KT):
                    for sd in range(2):
                        for h in range(HEADS):
                            col = l * 2 * HEADS + sd * HEADS + h
                            v.tensor_tensor_reduce(wjunk[:, h % 2, :], W[b][:, k, h * C:(h + 1) * C],
                                                         aB[:, sd, h * C:(h + 1) * C], 1.0, 0.0, ALU.mult, ALU.add,
                                                         wa[:, k, col:col + 1]).then_inc(s_wj, 1)
                            nj += 1
                            if nj >= 2:
                                v.wait_ge(s_wj, nj - 1)
                v.wait_ge(s_wj, nj)
                v.sem_inc(s_wa, 1)

            def onehots(n):
                for q in range(GROUP):
                    col = n * GROUP + q
                    v.wait_ge(s_ohu, col + 1)
                    v.tensor_scalar(oh_src[q][:, :], iota1[:, 0:T], sorted_[:, ds(col, 1)], None, ALU.is_equal)
                    v.tensor_scalar(oh_dst[q][:, :], iota1[:, :], sorted_[:, ds(col + ST, 1)], None,
                                    ALU.is_equal).then_inc(s_oh, 1)

            def add_counts(par, n):
                r = v.value_load(gbI[0:1, ds(n, 1)], min_val=0, max_val=3 * (NT - 1))
                v.wait_ge(s_ohu, n * GROUP + 2 * GROUP)
                v.wait_ge(s_ct, n + 2)
                v.tensor_tensor(CT[:, ds(r, 3), :], PS[0:T, 3 * par:3 * par + 3, 0:CHUNK], CT[:, ds(r, 3), :],
                                ALU.add).then_inc(s_ct, 1)
            v.sem_inc(s_ohu, GROUP)
            v.sem_inc(s_ct, 2)
            onehots(0)
            with v.Fori(0, NG // 2 - 1) as i:
                onehots(i * 2 + 1)
                add_counts(0, i * 2)
                onehots(i * 2 + 2)
                add_counts(1, i * 2 + 1)
            onehots(NG - 1)
            add_counts(0, NG - 2)
            add_counts(1, NG - 1)
            v.wait_ge(s_ct, NG + 2)
            for t in range(NT):
                c0 = t * CW + t * T
                v.tensor_tensor(CTf[:, c0:c0 + T], CTf[:, c0:c0 + T], ident[0:T, 0:T], ALU.add).then_inc(s_ct, 1)
            v.wait_ge(s_ct, NG + 2 + NT)
            v.wait_ge(s_x1, 3 * KT)
            v.wait_ge(s_lc, 1)
            link(v.tensor_copy(logitc[:, :, :], PS[0:T, 7, 0:240].rearrange("p (t c) -> p t c", c=24)))
            for s in range(NT + 1):
                if s < NT:
                    if s >= 2:
                        v.wait_ge(s_mt, 2 * (s - 1))
                    v.tensor_scalar(maskb[s % 2][:, :], CTf[:, s * CW:s * CW + N], 1.0, None, ALU.min).then_inc(s_mask, 1)
                if s >= 1:
                    for half in range(2):
                        v.wait_ge(s_mt, 2 * (s - 1) + half + 1)
                        v.tensor_scalar(NEG[:, 5 * half:5 * half + 5, (s - 1) * T:s * T],
                                        PSB[0:T, 6 + half, 0:630].rearrange("p (k n) -> p k n", k=5)[:, :, 0:T],
                                        1.0, BIG, ALU.subtract, ALU.mult).then_inc(s_neg, 1)
            v.wait_ge(s_neg, 2 * NT)
            for j in range(HEADS_ALL):
                v.wait_ge(s_asB[j % 2], 16 * (j // 2 + 1))
                for dt in range(NT):
                    if dt >= 2 or j >= 1:
                        v.wait_ge(s_mx, j * NT + dt - 1)
                    v.tensor_tensor_reduce(junk[dt % 2][:, :], asB[j % 2][0:T, :], NEG[:, dt, :], 1.0, -3.0e38,
                                           ALU.add, ALU.max, Mx[:, dt, j:j + 1]).then_inc(s_mx, 1)
            v.wait_ge(s_mx, NT * HEADS_ALL)
            lc = logitc[:, :, :].rearrange("p t (l s h) -> p t l s h", l=LAYERS, s=2)
            Mv = Mx[:, :, :].rearrange("p t (l h) -> p t l h", l=LAYERS)
            Zv = zz[:, :, :].rearrange("p t (l h) -> p t l h", l=LAYERS)
            Uv = UV[:, :, 0:HEADS_ALL].rearrange("p t (l h) -> p t l h", l=LAYERS)
            Vv = UV[:, :, HEADS_ALL:].rearrange("p t (l h) -> p t l h", l=LAYERS)
            for l in range(LAYERS):
                link(v.tensor_tensor(Zv[:, :, l, :], Mv[:, :, l, :], lc[:, :, l, 1, :], ALU.add))
                link(v.scalar_tensor_tensor(out=Zv[:, :, l, :], in0=Zv[:, :, l, :], scalar=SLOPE, in1=Zv[:, :, l, :],
                                            op0=ALU.mult, op1=ALU.max))
                link(v.tensor_tensor(Uv[:, :, l, :], lc[:, :, l, 1, :], Zv[:, :, l, :], ALU.subtract))
                link(v.scalar_tensor_tensor(out=Vv[:, :, l, :], in0=lc[:, :, l, 1, :], scalar=SLOPE, in1=Zv[:, :, l, :],
                                            op0=ALU.mult, op1=ALU.subtract))
                for dst_, f in ((as8, 1.0 - SLOPE), (as2, SLOPE)):
                    link(v.tensor_scalar(dst_[:, l * HEADS * NT:(l + 1) * HEADS * NT].rearrange("p (h t) -> p t h", h=HEADS),
                                         lc[:, :, l, 0, :], f, None, ALU.mult))
            v.sem_inc(s_uv, 1)
            v.drain()
            v.sem_inc(s_b1, 1)
            v.wait_ge(s_b1, 4)
            for q in range(2):
                v.memset(hs[q][:, :, C:CP], 1.0).then_inc(s_ones, 1)
            v.sem_inc(s_p, 2)
            with v.Fori(0, PAIRS) as i:
                def expo(hh, st):
                    u = hh * NT + st
                    if st == 0:
                        v.wait_ge(s_hs[hh], i * 80 + 80)
                    v.wait_ge(s_ex, i * 2 * NT + u + 1)
                    v.scalar_tensor_tensor(out=tt[st % 2][:, :], in0=uB[hh][0:T, :], scalar=col8[hh][:, st:st + 1],
                                           in1=vB[hh][0:T, :], op0=ALU.add, op1=ALU.max).then_inc(s_tt, 1)

                def probs(hh, st):
                    u = hh * NT + st
                    v.wait_ge(s_ex, i * 2 * NT + u + 3)
                    v.wait_ge(s_pu, i * 2 * NT + u + 1)
                    v.tensor_tensor(pr[st % 2][:, :], ex[st % 2][:, :], CTf[:, st * CW:st * CW + N],
                                    ALU.mult).then_inc(s_p, 1)

                def sums(hh):
                    for b in range(5):
                        if b < 4:
                            v.wait_ge(s_ob, i * 8 + hh * 4 + b + 1)
                        else:
                            v.wait_ge(s_pu, i * 2 * NT + hh * NT + NT + 2)
                        if b == 0:
                            v.wait_ge(s_oe, i * 2 * NT + hh * NT + NT)
                        v.tensor_scalar(den[:, 2 * b:2 * b + 2], PS[0:T, b, :].rearrange("p (r c) -> p r c", r=2)[:, :, C],
                                        1e-16, None, ALU.add).then_inc(s_den, 1)
                        v.wait_ge(s_den, i * 10 + hh * 5 + b + 1)
                        v.reciprocal(rs[:, 2 * b:2 * b + 2], den[:, 2 * b:2 * b + 2]).then_inc(s_rs, 1)
                expo(0, 0)
                for st in range(NT):
                    if st + 1 < NT:
                        expo(0, st + 1)
                    else:
                        expo(1, 0)
                    probs(0, st)
                expo(1, 1)
                probs(1, 0)
                sums(0)
                for st in range(1, NT):
                    if st + 1 < NT:
                        expo(1, st + 1)
                    probs(1, st)
                sums(1)
            v.drain()
            v.sem_inc(s_b2, 1)
            v.wait_ge(s_b2, 3)
            v.wait_ge(s_misc, 32)
            v.memset(zrow[:, :], 0.0).then_inc(s_zr, 1)
            for t in range(NT):
                v.wait_ge(s_xr[t % 2], 16 * (t // 2 + 1))
                for c in range(2):
                    f = slice(c * D // 2, (c + 1) * D // 2)
                    v.wait_ge(s_pj, 2 * t + c + 1)
                    link(v.tensor_tensor(rr[:, f], PS[0:T, 2 * (t % 2) + c, 0:D // 2], boB[0:T, f], ALU.add))
                    v.scalar_tensor_tensor(out=x2[:, t, f], in0=rr[:, f], scalar=0.0, in1=xr[t % 2][:, f],
                                           op0=ALU.max, op1=ALU.add).then_inc(s_pje, 1)
                    v.wait_ge(s_pje, 2 * t + c + 1)
                    link(v.bn_stats(st2[:, 6 * c:6 * c + 6], x2[:, t, f]))
                link(v.bn_aggr(mv2[:, 0:2], st2[:, :]))
                v.tensor_scalar(mv2[:, 2:3], mv2[:, 1:2], LN_EPS, None, ALU.add).then_inc(s_v2, 1)
                v.wait_ge(s_r2, t + 1)
                if t >= 2:
                    v.wait_ge(s_yd[t % 2], 16 * (t // 2))
                    v.wait_ge(s_yt, 2 * (t - 1))
                v.tensor_scalar(y[t % 2][:, :], x2[:, t, :], mv2[:, 0:1], rstd2[:, t % 2:t % 2 + 1], ALU.subtract,
                                ALU.mult).then_inc(s_y, 1)
                v.wait_ge(s_y, t + 1)
            v.wait_ge(s_lg, NT)
            link(v.tensor_copy(lg[:, :, :], PS[0:T, 6, 0:NT * EXPERTS].rearrange("p (t e) -> p t e", e=EXPERTS)))
            for t in range(NT):
                link(v.max(top[:, t, :], lg[:, t, :]))
                link(v.max_index(tidx[:, t, :], top[:, t, :], lg[:, t, :]))
            link(v.tensor_copy(idxF[:, :, :], tidx[:, :, 0:TOPK]))
            v.tensor_tensor(small[:, 0:NT], top[:, :, 1], top[:, :, 0], ALU.subtract).then_inc(s_sm, 1)
            v.wait_ge(s_sme, 1)
            link(v.tensor_scalar(small[:, NT:2 * NT], edt[:, :], 1.0, None, ALU.add))
            link(v.reciprocal(wk[:, :, 0], small[:, NT:2 * NT]))
            link(v.tensor_tensor(wk[:, :, 1], wk[:, :, 0], edt[:, :], ALU.mult))
            for t in range(NT):
                for k in range(TOPK):
                    link(v.tensor_scalar(ohp[:, t, k * EXPERTS:(k + 1) * EXPERTS], iota1[0:T, 0:EXPERTS], 1.0,
                                         idxF[:, t, k:k + 1], ALU.subtract, ALU.is_equal))
            v.tensor_copy(oh2[:, :, :], ohp[:, :, :]).then_inc(s_oh2, 1)
            v.wait_ge(s_cum, 1)
            link(v.tensor_tensor(ohp[:, :, :], ohp[:, :, :], PS[0:T, 7, 0:16 * NT].rearrange("p (t e) -> p t e", e=16),
                                 ALU.mult))
            link(v.tensor_reduce(posk[:, :, :], ohp[:, :, :].rearrange("p t (k e) -> p t k e", k=TOPK), AX.X, ALU.add))
            link(v.tensor_scalar(keep[:, :, :], posk[:, :, :], float(CAP), None, ALU.is_lt))
            link(v.tensor_tensor(wk[:, :, :], wk[:, :, :], keep[:, :, :], ALU.mult))
            link(v.tensor_copy(rk[:, :, 0], posk[:, :, 0]))
            link(v.tensor_scalar(rk[:, :, 1], posk[:, :, 1], float(CAP), None, ALU.add))
            link(v.tensor_scalar(rsub[:, :, :], rk[:, :, :], float(T), None, ALU.is_ge))
            link(v.scalar_tensor_tensor(out=rsub[:, :, :], in0=rk[:, :, :], scalar=float(2 * T), in1=rsub[:, :, :],
                                        op0=ALU.is_ge, op1=ALU.add))
            link(v.scalar_tensor_tensor(out=rslot[:, :, :], in0=rsub[:, :, :], scalar=-float(T), in1=rk[:, :, :],
                                        op0=ALU.mult, op1=ALU.add))
            link(v.scalar_tensor_tensor(out=rtile[:, :, :], in0=idxF[:, :, :], scalar=float(RT), in1=rsub[:, :, :],
                                        op0=ALU.mult, op1=ALU.add))
            link(v.tensor_scalar(tmpk[:, :, :], rk[:, :, :], float(ROWS - 1), None, ALU.subtract))
            link(v.tensor_tensor(tmpk[:, :, :], tmpk[:, :, :], keep[:, :, :], ALU.mult))
            link(v.tensor_scalar(tmpk[:, :, :], tmpk[:, :, :], float(ROWS - 1), None, ALU.add))
            link(v.scalar_tensor_tensor(out=rowF[:, :, :], in0=idxF[:, :, :], scalar=float(ROWS), in1=tmpk[:, :, :],
                                        op0=ALU.mult, op1=ALU.add))
            link(v.tensor_copy(rowI[:, :].rearrange("p (t k) -> p t k", k=TOPK), rowF[:, :, :]))
            link(v.tensor_scalar(tmpk[:, :, :], keep[:, :, :], -1000.0, 1001.0, ALU.mult, ALU.add))
            link(v.tensor_tensor(rslot[:, :, :], rslot[:, :, :], tmpk[:, :, :], ALU.add))
            link(v.tensor_scalar(rtile[:, :, :], rtile[:, :, :], 1.0, None, ALU.add))
            for u in range(TOPK * NT):
                t, k = divmod(u, TOPK)
                if u >= 2:
                    v.wait_ge(s_tku, u - 1)
                v.tensor_scalar(ohs[u % 2][:, :], iota1[0:T, 0:T], rslot[:, t, k:k + 1], None, ALU.is_equal)
                v.tensor_scalar(oht[u % 2][:, :], iota1[0:T, 0:EXPERTS * RT], rtile[:, t, k:k + 1], tokv[:, t:t + 1],
                                ALU.is_equal, ALU.mult).then_inc(s_tk, 1)
            v.wait_ge(s_tku, TOPK * NT)
            link(v.tensor_scalar(tokI[:, :], PS[0:T, 0, 0:EXPERTS * RT], float(N), None, ALU.add))
            v.drain()
            v.sem_inc(s_b3, 1)
            v.wait_ge(s_b3, 3)
            for e in range(EXPERTS):
                for m in range(2):
                    v.wait_ge(s_h1, 4 * e + 2 + m + 1)
                    v.wait_ge(s_sg, 2 * e + m + 1)
                    if e >= 1:
                        v.wait_ge(s_ye, RT * e)
                    v.tensor_tensor(actT[:, m, :], PS[:, 2 + m, 0:ROWS], sg[m][:, :], ALU.mult).then_inc(s_ac, 1)
            for t in range(NT):
                v.wait_ge(s_g0[t % 2], 16 * (t // 2 + 1))
                v.wait_ge(s_g1[t % 2], 16 * (t // 2 + 1))
                link(v.scalar_tensor_tensor(out=g0[t % 2][:, :], in0=g0[t % 2][:, :], scalar=wk[:, t, 0:1], in1=x2[:, t, :],
                                            op0=ALU.mult, op1=ALU.add))
                v.scalar_tensor_tensor(out=g1[t % 2][:, :], in0=g1[t % 2][:, :], scalar=wk[:, t, 1:2], in1=g0[t % 2][:, :],
                                       op0=ALU.mult, op1=ALU.add).then_inc(s_fin, 1)


_INS = ['x', 'src', 'dst', 'L0_gnn_W_ah', 'L0_gnn_b_ah', 'L0_gnn_W0', 'L0_gnn_a_src0', 'L0_gnn_a_dst0', 'L0_gnn_b0',
        'L0_gnn_W1', 'L0_gnn_a_src1', 'L0_gnn_a_dst1', 'L0_gnn_b1', 'L0_gnn_W2', 'L0_gnn_a_src2', 'L0_gnn_a_dst2',
        'L0_gnn_b2', 'L0_gnn_W_out', 'L0_gnn_b_out', 'L0_ffn_Wg', 'L0_ffn_W1', 'L0_ffn_W2']


def kernel(**inputs):
    import numpy as _np
    import concourse.bacc as _bacc
    from concourse import mybir as _mybir
    from concourse.bass_utils import run_bass_kernel_spmd as _run

    nc = _bacc.Bacc("TRN2", target_bir_lowering=False, num_devices=1)
    arrays, aps = {}, {}
    for name in _INS:
        a = _np.ascontiguousarray(inputs[name])
        arrays[f"in_{name}_dram"] = a
        aps[name.replace("L0_gnn_", "").replace("L0_", "")] = nc.dram_tensor(
            f"in_{name}_dram", a.shape, _mybir.dt.from_np(a.dtype), kind="ExternalInput").ap()
    out = nc.dram_tensor("out_0_dram", (N, D), F32, kind="ExternalOutput").ap()
    gnn_moe(nc, aps["x"], aps["src"], aps["dst"], aps["W_ah"], aps["b_ah"],
            [aps[f"W{l}"] for l in range(LAYERS)], [aps[f"a_src{l}"] for l in range(LAYERS)],
            [aps[f"a_dst{l}"] for l in range(LAYERS)], [aps[f"b{l}"] for l in range(LAYERS)],
            aps["W_out"], aps["b_out"], aps["ffn_Wg"], aps["ffn_W1"], aps["ffn_W2"], out)
    r = _run(nc, [arrays], core_ids=[0])
    return r.results[0]["out_0_dram"]
```

```python
from contextlib import ExitStack

import concourse.bass as bass
from concourse import mybir

F32 = mybir.dt.float32
F16 = mybir.dt.float16
BF16 = mybir.dt.bfloat16
I32 = mybir.dt.int32
U32 = mybir.dt.uint32
I16 = mybir.dt.int16
ALU = mybir.AluOpType
ACT = mybir.ActivationFunctionType
AX = mybir.AxisListType
ds = bass.ds

N = 1250
T = 125
NT = N // T
D = 768
P = 128
KT = D // P
LAYERS = 3
HEADS = 4
C = D // HEADS
CP = C + 1
HEADS_ALL = LAYERS * HEADS
PAIRS = HEADS_ALL // 2
SLOPE = 0.2
LN_EPS = 1e-5
BIG = 1.0e30

E = 20000
ET = E // T
GROUP = 4
SLOTS = GROUP * P
NG = (E + NT * (SLOTS - 1)) // SLOTS
NG += NG % 2
ST = NG * GROUP
CHUNK = 417
CW = 3 * CHUNK
CHUNKS = [(0, CHUNK), (CHUNK, CHUNK), (2 * CHUNK, N - 2 * CHUNK)]

EXPERTS = 8
TOPK = 2
HID = 256
CAP = int(1.2 * N / EXPERTS)
RT = 3
ROWS = RT * T
assert TOPK * CAP < ROWS and NG * SLOTS >= E + NT * (SLOTS - 1) - SLOTS


def gnn_moe(nc, x, src, dst, W_ah, b_ah, Wl, a_src, a_dst, bl, W_out, b_out, Wg, W1, W2, out):
    h_dram = nc.dram_tensor("h_rows", (HEADS_ALL, N, C), F32, kind="Internal").ap()
    logit_rows = nc.dram_tensor("logit_rows", (2 * HEADS_ALL, N), F32, kind="Internal").ap()
    uv_rows = nc.dram_tensor("uv_rows", (2 * HEADS_ALL, N), F32, kind="Internal").ap()
    emb_dram = nc.dram_tensor("emb_t", (LAYERS * D, N), F32, kind="Internal").ap()
    y_dram = nc.dram_tensor("y_rows", (N + 1, D), F32, kind="Internal").ap()
    ye_dram = nc.dram_tensor("expert_rows", (EXPERTS * ROWS, D), F32, kind="Internal").ap()

    with ExitStack() as ctx:
        ctx.enter_context(nc.allow_non_contiguous_dma("bias columns and node tiles"))

        def sem(name):
            return ctx.enter_context(nc.semaphore(name))

        def alloc(stack):
            return lambda name, shape, dt: stack.enter_context(nc.sbuf_tensor(name, shape, dt))

        sb = alloc(ctx)
        PS = ctx.enter_context(nc.psum_tensor("PS", [P, 8, 512], F32))
        PSB = PS[:, :, :].rearrange("p b c -> p (b c)").bitcast(BF16).rearrange("p (b c) -> p b c", b=8)

        ident = sb("ident", [P, P], F32)
        identb = sb("identb", [P, P], BF16)
        iota1 = sb("iota1", [P, CW], F16)
        tri = sb("tri", [T, T], F16)
        ones = sb("ones", [T, T], F16)
        CT = sb("CT", [T, 3 * NT, CHUNK], I16)
        CTf = CT[:, :, :].rearrange("p a b -> p (a b)")
        b_ahT = sb("b_ahT", [P, KT], F32)
        blT = sb("blT", [P, LAYERS * KT], F32)
        as8 = sb("as8", [T, HEADS_ALL * NT], F32)
        as2 = sb("as2", [T, HEADS_ALL * NT], F32)
        small = sb("small", [T, 64], F32)
        tokv = sb("tokv", [T, NT], F32)

        tensors = {}

        def region(name, *sets, stack=ctx):
            width = {F32: 4, I32: 4, U32: 4, F16: 2, BF16: 2, I16: 2}
            total = 0
            for tset in sets:
                inner, size = ExitStack(), 0
                for entry in tset:
                    if len(entry) == 2:
                        size += region(entry[0], *entry[1], stack=inner)
                        continue
                    tname, shape, dt = entry
                    tensors[tname] = alloc(inner)(tname, shape, dt)
                    n = width[dt]
                    for d_ in shape[1:]:
                        n *= d_
                    size += (n + 31) // 32 * 32
                inner.close()
                total = max(total, size)
            alloc(stack)(name, [P, total // 4], F32)
            return total

        region("region_a",
               [("x1T", [P, KT, N], F32), ("W0", [P, KT, D], F32), ("W1", [P, KT, D], F32)],
               [("emb", [T, NT, 2 * C], F32), ("embT", [P, 3, N], F32), ("hs1", [T, NT, CP], F32),
                ("uB1", [P, N], F32), ("vB1", [P, N], F32)],
               [("x2", [T, NT, D], F32), ("EB0", [P, LAYERS * KT, T], F32), ("EB1", [P, LAYERS * KT, T], F32),
                ("y0", [T, D], F32), ("y1", [T, D], F32), ("boB", [P, D], F32), ("xr0", [T, D], F32),
                ("rr0", [T, D // 2], F32), ("rr1", [T, D // 2], F32), ("zrow", [1, D // 2], F32)],
               [("x2_", [T, NT, D], F32), ("g0_0", [T, D], F32), ("g0_1", [T, D], F32), ("g0_2", [T, D], F32),
                ("g1_0", [T, D], F32), ("g1_1", [T, D], F32), ("g1_2", [T, D], F32)])
        region("region_b",
               [("X", [T, NT, D], F32), ("xnT", [P, KT, N], F32)],
               [("vB0", [P, N], F32), ("NEG", [T, NT, N], BF16), ("asB0", [P, N], F32), ("asB1", [P, N], F32),
                ("junk0", [T, N], BF16), ("junk1", [T, N], BF16), ("maskb0", [T, N], BF16), ("maskb1", [T, N], BF16),
                ("Lr", [2 * HEADS_ALL, N], F32), ("UVr", [2 * HEADS, N], F32)],
               [("vB0_", [P, N], F32), ("Wo", [P, LAYERS * KT, D], F32)],
               [("W1s1", [P, KT, 2 * HID], F32), ("W2s1", [P, 2, D], F32), ("XgT0", [P, KT, ROWS], F32),
                ("XgT1", [P, KT, ROWS], F32), ("Xg0", [T, D], F32), ("Xg1", [T, D], F32), ("Xg2", [T, D], F32)])
        hsb = [sb(f"hsb{i}", [T, D // 2], F32) for i in range(4)]
        mx_all = sb("mx_all", [T, NT, HEADS_ALL], F32)
        logitc = sb("logitc", [T, NT, 2 * HEADS_ALL], F32)
        UV = [sb(f"UV{i}", [T, NT, 2 * HEADS], F32) for i in range(2)]
        zz = sb("zz", [T, NT, HEADS], F32)
        region("region_c",
               [("aB", [P, 2, D], F32), ("wa", [P, KT, 2 * HEADS_ALL], F32), ("wjunk", [P, 2, C], F32),
                ("one_row", [T, ET], F16), ("local1", [T, ET], F32), ("other1", [T, ET], F32), ("slot1", [T, ET], F32),
                ("tile1", [T, ET], F32), ("cols", [T, 8, NT], F32), ("gbF", [1, NG], F32), ("gbI", [1, NG], I32),
                ("sorted", [P, 2 * ST], F32),
                ("sort_or_count",
                 ([("xn0", [T, D], F32), ("xn1", [T, D], F32), ("sumx", [T, NT], F32), ("nmean", [T, NT], F32),
                   ("sumsq", [T, NT], F32), ("ve", [T, NT], F32), ("mhalf", [T, NT], F32), ("rstd", [T, NT], F32),
                   ("sjunk", [T, D], BF16), ("srcI", [T, ET], I32), ("dstI", [T, ET], I32), ("key", [T, ET], F32),
                   ("bucket", [T, ET], F32), ("inb", [T, NT, ET], F16), ("cum", [T, NT, ET], F16),
                   ("tot16", [T, NT], F16), ("colsI", [T, 2, NT], I32), ("tmpj", [T, ET], F32), ("pos", [T, ET], F32),
                   ("posI", [T, 3, ET], I32)]
                  + [(f"pick{i}", [T, P], F16) for i in range(4)] + [(f"put{i}", [T, 2 * ST], F16) for i in range(4)],
                  [(f"oh_src{i}", [P, T], F16) for i in range(4)]
                  + [(f"oh_dst{i}", [P, CW], F16) for i in range(4)]))],
               [("tt0", [T, N], F32), ("tt1", [T, N], F32), ("ex0", [T, N], F32), ("ex1", [T, N], F32),
                ("pr0", [T, N], F32), ("pr1", [T, N], F32), ("hs0", [T, NT, CP], F32), ("uB0", [P, N], F32),
                ("den", [T, NT], F32), ("rs", [T, NT], F32)],
               [("W1s0", [P, KT, 2 * HID], F32), ("W2s0", [P, 2, D], F32), ("sg0", [P, ROWS], F32), ("sg1", [P, ROWS], F32),
                ("actT", [P, 2, ROWS], F32), ("ye0", [T, D], F32), ("ye1", [T, D], F32), ("xr1", [T, D], F32),
                ("yT0", [P, KT, T], F32), ("yT1", [P, KT, T], F32),
                ("WgS", [P, KT, EXPERTS], F32), ("st2", [T, 12], F32), ("mv2", [T, 4], F32),
                ("rstd2", [T, NT], F32), ("mh2", [T, 1], F32), ("lg", [T, NT, EXPERTS], F32), ("top", [T, NT, 8], F32),
                ("tidx", [T, NT, 8], U32), ("idxF", [T, NT, TOPK], F32), ("oh2", [T, NT, TOPK * EXPERTS], F16),
                ("ohp", [T, NT, TOPK * EXPERTS], F32), ("posk", [T, NT, TOPK], F32), ("keep", [T, NT, TOPK], F32),
                ("rk", [T, NT, TOPK], F32), ("rsub", [T, NT, TOPK], F32), ("rtile", [T, NT, TOPK], F32),
                ("rslot", [T, NT, TOPK], F32), ("tmpk", [T, NT, TOPK], F32), ("rowF", [T, NT, TOPK], F32),
                ("ohs0", [T, T], F16), ("ohs1", [T, T], F16), ("oht0", [T, EXPERTS * RT], F16),
                ("oht1", [T, EXPERTS * RT], F16), ("edt", [T, NT], F32)])
        x1T, xnT, X, NEG, Lr, Wo, emb, embT = (tensors[k] for k in ("x1T", "xnT", "X", "NEG", "Lr", "Wo", "emb", "embT"))
        W, asB, junk, maskb, hs, uB, vB, tt, ex, pr, xn = (
            [tensors[f"{k}{i}"] for i in range(2)]
            for k in ("W", "asB", "junk", "maskb", "hs", "uB", "vB", "tt", "ex", "pr", "xn"))
        pick, put, oh_src, oh_dst = ([tensors[f"{k}{i}"] for i in range(4)] for k in ("pick", "put", "oh_src", "oh_dst"))
        (aB, wa, wjunk, sumx, nmean, sumsq, ve, mhalf, rstd, sjunk, srcI, dstI, key, other1, bucket, local1, inb, cum,
         one_row, tot16, cols, colsI, tmpj, pos, posI, slot1, tile1, gbF, gbI, sorted_, UVr, den, rs) = (
            tensors[k] for k in ("aB", "wa", "wjunk", "sumx", "nmean", "sumsq", "ve", "mhalf", "rstd", "sjunk", "srcI",
                                 "dstI", "key", "other1", "bucket", "local1", "inb", "cum", "one_row", "tot16", "cols",
                                 "colsI", "tmpj", "pos", "posI", "slot1", "tile1", "gbF", "gbI", "sorted", "UVr", "den",
                                 "rs"))

        rowI = sb("rowI", [T, NT * TOPK], I32)
        tokI = sb("tokI", [T, EXPERTS * RT], I32)
        wk = sb("wk", [T, NT, TOPK], F32)
        x2, boB, zrow, WgS, st2, mv2, rstd2, mh2, lg, top, tidx, idxF, oh2, ohp, posk, keep, rk, rsub, rtile = (
            tensors[k] for k in ("x2", "boB", "zrow", "WgS", "st2", "mv2", "rstd2", "mh2", "lg", "top", "tidx", "idxF",
                                 "oh2", "ohp", "posk", "keep", "rk", "rsub", "rtile"))
        rslot, tmpk, rowF, edt, actT = (tensors[k] for k in ("rslot", "tmpk", "rowF", "edt", "actT"))
        EB, xr, rr, y, yT, ohs, oht, W1s, W2s, XgT, sg, ye = (
            [tensors[f"{k}{i}"] for i in range(2)]
            for k in ("EB", "xr", "rr", "y", "yT", "ohs", "oht", "W1s", "W2s", "XgT", "sg", "ye"))
        g0, g1 = ([tensors[f"{k}{i}"] for i in range(3)] for k in ("g0_", "g1_"))
        Xg = [tensors[f"Xg{i}"] for i in range(3)]

        def sems(name, n):
            return [sem(f"{name}{i}") for i in range(n)]

        s_x = sems("x_tile", NT)
        s_wah, s_small, s_edges, s_aB, s_lrd, s_uvd, s_wo, s_misc, s_zr, s_ed = (sem(n) for n in (
            "wah_loaded", "small_loaded", "edges_loaded", "a_rows_loaded", "logit_rows_written", "uv_rows_written",
            "wout_loaded", "stage6_small_loaded", "zero_row_written", "embT_written"))
        s_w, s_asB, s_hs, s_eb, s_xr, s_yd, s_w1, s_w2, s_yed = (sems(n, 2) for n in (
            "w_loaded", "source_row_loaded", "head_loaded", "emb_tile_loaded", "residual_loaded", "y_written",
            "expert_w1_loaded", "expert_w2_loaded", "expert_rows_written"))
        s_hd = sems("h_written", 4)
        s_xg, s_g0, s_g1, s_od = (sems(n, 3) for n in (
            "rows_gathered", "first_rows_gathered", "second_rows_gathered", "result_written"))
        s_c, s_ctz, s_ssq, s_rstd, s_xn, s_tp, s_tpe, s_x1, s_x1e = (sem(n) for n in (
            "constants", "counts_cleared", "squares_summed", "rstd_ready", "xn_ready", "xn_transposed", "xnT_stored",
            "x1_banks", "x1T_stored"))
        s_h, s_he, s_wj, s_wa, s_lr, s_lre, s_lc = (sem(n) for n in (
            "h_banks", "h_evacuated", "logit_weight_column", "wa_ready", "logit_row_banks", "logit_rows_stored",
            "logit_columns"))
        s_tot, s_pre, s_pick, s_perm, s_oh, s_ohu, s_ct = (sem(n) for n in (
            "bucket_totals", "bucket_prefixes", "permutation_ready", "permutation_used", "count_onehots_ready",
            "count_onehots_used", "counts_added"))
        s_mask, s_mt, s_neg, s_mx, s_uv, s_uvt, s_uvr = (sem(n) for n in (
            "mask_ready", "mask_transposed", "neg_stored", "neighbour_max", "uv_columns", "uv_transposed",
            "uv_rows_stored"))
        s_ones, s_tt, s_ex, s_p, s_pu, s_ob, s_den, s_rs, s_oe, s_tr, s_te = (sem(n) for n in (
            "ones_column", "exponent_ready", "exp_ready", "probs_ready", "probs_used", "head_banks_full",
            "row_sums_guarded", "row_sums_inverted", "head_tiles_stored", "emb_transposed", "embT_stored"))
        s_pj, s_pje, s_v2, s_r2, s_y, s_yt, s_yte, s_lg, s_oh2, s_cum, s_sm, s_sme, s_tk, s_tku, s_tok = (
            sem(n) for n in (
                "projection_banks", "projection_evacuated", "variance2_ready", "rstd2_ready", "y_ready", "y_transposed",
                "yT_stored", "gate_logits", "expert_onehots", "expert_counts", "gate_differences", "gate_exp",
                "token_onehots", "token_onehots_used", "token_table"))
        s_xt, s_xte, s_h1, s_sg, s_ac, s_yb, s_yee, s_fin = (sem(n) for n in (
            "rows_transposed", "rows_transposed_stored", "hidden_banks", "silu_ready", "hidden_act_ready",
            "expert_out_banks", "expert_out_stored", "result_ready"))
        s_dch, s_ach, s_gch = (sem(n) for n in ("vector_chain", "scalar_chain", "pool_chain"))

        HALF = D // 2
        HU = LAYERS * NT * 2
        COUNT_H = NG // 2
        UNITS = HEADS_ALL * NT
        PERM = 9
        M2_STEPS = 60
        M2 = HEADS * NT
        UV2_STEP = M2_STEPS + 6
        PAIR_GROUPS = [(0, 4), (4, 8), (8, NT)]

        def row(ap):
            return ap.rearrange("(o n) -> o n", o=1)

        def half_tile(i):
            return i // (2 * NT), (i // 2) % NT, i % 2

        block = ctx.enter_context(nc.Block())

        @block.sync
        def _(sp):
            for t in range(NT):
                sp.dma_start(X[:, t, :], x[t * T:(t + 1) * T, :]).then_inc(s_x[t], 16)
            sp.dma_start(W[0][:, :, :], W_ah.rearrange("(k p) n -> p k n", p=P)).then_inc(s_wah, 16)
            sp.dma_start(b_ahT[:, :], b_ah.rearrange("(k p) -> p k", p=P)).then_inc(s_small, 16)
            for l in range(LAYERS):
                sp.dma_start(blT[:, l * KT:(l + 1) * KT],
                             bl[l].rearrange("(k p) -> p k", p=P)).then_inc(s_small, 16)
            for l in range(LAYERS):
                b = (l + 1) % 2
                if l == 1:
                    sp.wait_ge(s_x1, 3 * KT)
                if l == 2:
                    sp.wait_ge(s_h, 2 * NT)
                if l >= 1:
                    sp.wait_ge(s_wa, l)
                sp.dma_start(W[b][:, :, :], Wl[l].rearrange("(k p) n -> p k n", p=P)).then_inc(s_w[b], 16)
                for i, a in enumerate((a_src[l], a_dst[l])):
                    sp.dma_start(aB[:, i, :], row(a.rearrange("h c -> (h c)")).broadcast_to([P, D])).then_inc(s_aB, 16)
            sp.wait_ge(s_lre, 3)
            sp.dma_start(logit_rows[:, :], Lr[:, :]).then_inc(s_lrd, 16)
            sp.wait_ge(s_lrd, 16)

            def load_row(j):
                l, h = divmod(j, HEADS)
                if j >= 2:
                    sp.wait_ge(s_mx, NT * (j - 1))
                r0 = l * 2 * HEADS + h
                sp.dma_start(asB[j % 2][:, :], logit_rows[r0:r0 + 1, :].broadcast_to([P, N])).then_inc(s_asB[j % 2], 16)

            def store_uv(l):
                sp.wait_ge(s_uvr, 3 * (l + 1))
                sp.dma_start(uv_rows[l * 2 * HEADS:(l + 1) * 2 * HEADS, :], UVr[:, :]).then_inc(s_uvd, 16)

            def load_head(head):
                l, h = divmod(head, HEADS)
                q = head % 2
                if head >= 2:
                    sp.wait_ge(s_pu, 2 + (head - 1) * NT)
                sp.wait_ge(s_uvd, 16 * (l + 1))
                sp.dma_start(hs[q][:, :, 0:C], h_dram[head].rearrange("(t p) c -> p t c", p=T)).then_inc(s_hs[q], 16)
                for k, buf in enumerate((uB, vB)):
                    r0 = l * 2 * HEADS + k * HEADS + h
                    sp.dma_start(buf[q][:, :], uv_rows[r0:r0 + 1, :].broadcast_to([P, N])).then_inc(s_hs[q], 16)

            def store_pair(pair):
                sp.wait_ge(s_te, 3 + 9 * pair + 9)
                sp.dma_start(emb_dram[pair * 3 * P:(pair + 1) * 3 * P, :].rearrange("(k p) n -> p k n", p=P),
                             embT[:, :, :]).then_inc(s_ed, 16)
            for j in range(HEADS + 2):
                load_row(j)
            store_uv(0)
            for q in range(4):
                sp.wait_ge(s_hd[q], 16 * (2 * NT // 4))
            load_head(0)
            for j in range(HEADS + 2, 2 * HEADS):
                load_row(j)
            store_uv(1)
            for q in range(4):
                sp.wait_ge(s_hd[q], 16 * (HU // 4))
            load_row(2 * HEADS)
            load_row(2 * HEADS + 1)
            sp.wait_ge(s_h, HU)
            sp.wait_ge(s_pu, 3)
            load_head(1)
            for head in range(2, HEADS_ALL):
                if head == 2 * HEADS:
                    store_uv(2)
                load_head(head)
                if head in (3, 5):
                    load_row(2 * HEADS + head // 2 + 1)
                if head % 2 == 0 and head >= 4:
                    store_pair(head // 2 - 2)
                if head == 2 * HEADS:
                    sp.wait_ge(s_uv, 3)
                    sp.dma_start(Wo[:, :, :], W_out.rearrange("(k p) n -> p k n", p=P)).then_inc(s_wo, 16)
            store_pair(PAIRS - 2)
            store_pair(PAIRS - 1)
            sp.wait_ge(s_ed, 16 * PAIRS)
            sp.dma_start(boB[:, :], row(b_out).broadcast_to([P, D])).then_inc(s_misc, 16)
            sp.dma_start(WgS[:, :, :], Wg.rearrange("(k p) e -> p k e", p=P)).then_inc(s_misc, 16)

            def load_expert(e):
                if e >= 2:
                    sp.wait_ge(s_h1, 4 * (e - 1))
                    sp.wait_ge(s_yb, 2 * RT * (e - 1))
                sp.dma_start(W1s[e % 2][:, :, :], W1[e].rearrange("(k p) n -> p k n", p=P)).then_inc(s_w1[e % 2], 16)
                sp.dma_start(W2s[e % 2][:, :, :], W2[e].rearrange("(k p) n -> p k n", p=P)).then_inc(s_w2[e % 2], 16)
            for t in range(NT):
                if t >= 2:
                    sp.wait_ge(s_pje, 2 * (t - 1))
                sp.dma_start(EB[t % 2][:, :, :], emb_dram.rearrange("(k p) n -> p k n", p=P)[:, :, t * T:(t + 1) * T]
                             ).then_inc(s_eb[t % 2], 16)
                sp.dma_start(xr[t % 2][:, :], x[t * T:(t + 1) * T, :]).then_inc(s_xr[t % 2], 16)
                if t == 1:
                    load_expert(0)
                if t >= 1:
                    sp.wait_ge(s_y, t)
                    sp.dma_start(y_dram[(t - 1) * T:t * T, :], y[(t - 1) % 2][:, :]).then_inc(s_yd[(t - 1) % 2], 16)
            sp.wait_ge(s_zr, 1)
            for c in range(2):
                sp.dma_start(y_dram[N:N + 1, c * HALF:(c + 1) * HALF], zrow[:, :]).then_inc(s_zr, 16)
            sp.wait_ge(s_pj, 2 * NT)
            load_expert(1)
            sp.wait_ge(s_y, NT)
            sp.dma_start(y_dram[(NT - 1) * T:NT * T, :], y[(NT - 1) % 2][:, :]).then_inc(s_yd[(NT - 1) % 2], 16)
            for e in range(2, EXPERTS):
                load_expert(e)
            for t in range(NT):
                sp.wait_ge(s_fin, t + 1)
                sp.dma_start(out[t * T:(t + 1) * T, :], g1[t % 3][:, :]).then_inc(s_od[t % 3], 16)
            for q in range(3):
                sp.wait_ge(s_od[q], 16 * len(range(q, NT, 3)))

        @block.gpsimd
        def _(g):
            chain = [0]

            def link(ins):
                chain[0] += 1
                ins.then_inc(s_gch, 1)
                g.wait_ge(s_gch, chain[0])

            g.dma_start(srcI[:, :], src.rearrange("(p t) -> p t", p=T)).then_inc(s_edges, 16)
            g.dma_start(dstI[:, :], dst.rearrange("(p t) -> p t", p=T)).then_inc(s_edges, 16)
            link(g.memset(tri[:, :], 1.0))
            g.affine_select(out=tri[:, :], in_=tri[:, :], compare_op=ALU.is_gt, fill=0.0, base=0,
                            pattern=[[1, T]], channel_multiplier=-1).then_inc(s_c, 1)
            g.memset(ones[:, :], 1.0).then_inc(s_c, 1)
            link(g.memset(ident[:, :], 0.0))
            g.affine_select(out=ident[:, :], in_=ident[:, :], compare_op=ALU.not_equal, fill=1.0, base=0,
                            pattern=[[-1, P]], channel_multiplier=1).then_inc(s_c, 1)
            g.iota(iota1[:, :], [[1, CW]], base=1, channel_multiplier=0,
                   allow_small_or_imprecise_dtypes=True).then_inc(s_c, 1)
            link(g.memset(mhalf[:, :], -0.5))
            for t in range(NT):
                g.wait_ge(s_ssq, t + 1)
                link(g.tensor_scalar(ve[:, t:t + 1], sumsq[:, t:t + 1], 1.0 / D, LN_EPS, ALU.mult, ALU.add))
                g.tensor_tensor(rstd[:, t:t + 1], ve[:, t:t + 1], mhalf[:, 0:1], ALU.pow).then_inc(s_rstd, 1)
            g.iota(tokv[:, :], [[T, NT]], base=-N, channel_multiplier=1,
                   allow_small_or_imprecise_dtypes=True).then_inc(s_c, 1)
            g.memset(CTf, 0).then_inc(s_ctz, 1)
            g.wait_ge(s_zr, 1)
            link(g.memset(mh2[:, :], -0.5))
            for t in range(NT):
                g.wait_ge(s_v2, t + 1)
                g.tensor_tensor(rstd2[:, t:t + 1], mv2[:, 2:3], mh2[:, :], ALU.pow).then_inc(s_r2, 1)
            g.wait_ge(s_tok, 1)
            for q in range(2):
                g.wait_ge(s_yd[q], 16 * NT // 2)
            g.wait_ge(s_zr, 33)
            for u in range(EXPERTS * RT):
                if u >= RT:
                    g.wait_ge(s_xt, 2 * (u - RT + 1))
                g.indirect_dma_start(out=Xg[u % 3][:, :], out_offset=None, in_=y_dram[:, :],
                                     in_offset=bass.IndirectOffsetOnAxis(ap=tokI[:, u:u + 1], axis=0)
                                     ).then_inc(s_xg[u % 3], 16)
            for q in range(2):
                g.wait_ge(s_yed[q], 16 * EXPERTS * RT // 2)
            for t in range(NT):
                if t >= 3:
                    g.wait_ge(s_od[t % 3], 16 * (t // 3))
                for k, (gb, s_g) in enumerate(((g0, s_g0), (g1, s_g1))):
                    g.indirect_dma_start(out=gb[t % 3][:, :], out_offset=None, in_=ye_dram[:, :],
                                         in_offset=bass.IndirectOffsetOnAxis(
                                             ap=rowI[:, TOPK * t + k:TOPK * t + k + 1], axis=0)
                                         ).then_inc(s_g[t % 3], 16)

        @block.tensor
        def _(pe):
            pe.wait_ge(s_c, 4)
            pe.wait_ge(s_tot, 1)
            pe.matmul(PS[0:T, 5, 0:NT], tri[:, :], tot16[:, :], start=True, stop=True)
            pe.matmul(PS[0:T, 5, 16:16 + NT], ones[:, :], tot16[:, :], start=True, stop=True).then_inc(s_pre, 1)
            for t in range(NT):
                pe.wait_ge(s_xn, t + 1)
                for half in range(2):
                    u = 2 * t + half
                    if u >= 4:
                        pe.wait_ge(s_tpe, u - 3)
                    for k in range(3):
                        mm = pe.transpose(PS[:, u % 4, k * T:(k + 1) * T],
                                          xn[t % 2][:, (3 * half + k) * P:(3 * half + k + 1) * P], ident[0:T, 0:T])
                    mm.then_inc(s_tp, 1)
            pe.wait_ge(s_wah, 16)
            for c, (c0, cn) in enumerate(CHUNKS):
                pe.wait_ge(s_tpe, 2 * -(-(c0 + cn) // T))
                for m in range(KT):
                    u = KT * c + m
                    if u >= 2:
                        pe.wait_ge(s_x1e, u - 1)
                    for k in range(KT):
                        mm = pe.matmul(PS[:, 6 + u % 2, 0:cn], W[0][:, k, m * P:(m + 1) * P], xnT[:, k, c0:c0 + cn],
                                       start=(k == 0), stop=(k == KT - 1))
                    mm.then_inc(s_x1, 1)
                    for n in range(PERM * u, min(PERM * (u + 1), ET)):
                        pe.wait_ge(s_pick, n + 1)
                        pe.matmul(PS[:, 4, 0:2 * ST], pick[n % 4][:, :], put[n % 4][:, :], start=(n == 0),
                                  stop=(n == ET - 1)).then_inc(s_perm, 1)
            def h_half(i):
                l, t, c = half_tile(i)
                b = (l + 1) % 2
                if t == 0 and c == 0:
                    pe.wait_ge(s_w[b], 16 * (l // 2 + 1))
                if i >= 2:
                    pe.wait_ge(s_he, i - 1)
                for k in range(KT):
                    mm = pe.matmul(PS[0:T, 6 + i % 2, 0:HALF], x1T[:, k, t * T:(t + 1) * T],
                                   W[b][:, k, c * HALF:(c + 1) * HALF], start=(k == 0), stop=(k == KT - 1))
                mm.then_inc(s_h, 1)
            pe.wait_ge(s_x1e, 3 * KT)
            for i in range(COUNT_H):
                h_half(i)
                for g in (2 * i, 2 * i + 1):
                    pe.wait_ge(s_ct, g + 1)
                    for q in range(GROUP):
                        pe.wait_ge(s_oh, g * GROUP + q + 1)
                        for c in range(3):
                            mm = pe.matmul(PS[0:T, 3 * (g % 2) + c, 0:CHUNK], oh_src[q][:, :],
                                           oh_dst[q][:, c * CHUNK:(c + 1) * CHUNK], start=(q == 0), stop=(q == GROUP - 1))
                        mm.then_inc(s_ohu, 1)
            for i in range(COUNT_H, COUNT_H + 3):
                h_half(i)
            pe.wait_ge(s_ct, NG + 2)
            pe.wait_ge(s_wa, LAYERS)
            for c, (c0, cn) in enumerate(CHUNKS):
                for k in range(KT):
                    mm = pe.matmul(PS[0:2 * HEADS_ALL, c, 0:cn], wa[:, k, :], x1T[:, k, c0:c0 + cn],
                                   start=(k == 0), stop=(k == KT - 1))
                mm.then_inc(s_lr, 1)
            for t in range(NT):
                for k in range(KT):
                    mm = pe.matmul(PS[0:T, 3, t * 24:(t + 1) * 24], x1T[:, k, t * T:(t + 1) * T], wa[:, k, :],
                                   start=(k == 0), stop=(k == KT - 1))
            mm.then_inc(s_lc, 1)
            i = COUNT_H + 3
            for s in range(NT):
                pe.wait_ge(s_mask, s + 1)
                for half in range(2):
                    u = 2 * s + half
                    if u >= 2:
                        pe.wait_ge(s_neg, u - 1)
                    for k in range(5):
                        mm = pe.transpose(PSB[0:T, 4 + half, k * 126:k * 126 + T],
                                          maskb[s % 2][:, (5 * half + k) * T:(5 * half + k + 1) * T], identb[0:T, 0:T])
                    mm.then_inc(s_mt, 1)
                if s % 2:
                    h_half(i)
                    i += 1

            def uv_transposes(l, b0):
                pe.wait_ge(s_uv, l + 1)
                for q, (t0, t1) in enumerate(PAIR_GROUPS):
                    for t in range(t0, t1):
                        mm = pe.transpose(PS[0:2 * HEADS, b0 + q, (t - t0) * T:(t - t0 + 1) * T], UV[l % 2][:, t, :],
                                          ident[0:T, 0:T])
                    mm.then_inc(s_uvt, 1)
            while i < 3 * HU // 4 + 3:
                h_half(i)
                i += 1
            uv_transposes(0, 0)
            while i < HU:
                h_half(i)
                i += 1
            pe.wait_ge(s_uvr, 3)
            uv_transposes(1, 0)
            pe.wait_ge(s_uvr, 6)

            def pair_transposes(pair, k):
                pe.wait_ge(s_oe, (2 * pair + 2) * NT)
                for q, (t0, t1) in enumerate(PAIR_GROUPS):
                    pe.wait_ge(s_te, 9 * pair + 3 * k + q + 1)
                    for t in range(t0, t1):
                        mm = pe.transpose(PS[:, 5 + q, (t - t0) * T:(t - t0 + 1) * T], emb[:, t, k * P:(k + 1) * P],
                                          ident[0:T, 0:T])
                    mm.then_inc(s_tr, 1)
            pe.sem_inc(s_pu, 2)
            for u in range(UNITS):
                head, st = divmod(u, NT)
                if st == 0:
                    pe.wait_ge(s_hs[head % 2], 48 * (head // 2 + 1))
                    pe.wait_ge(s_ones, head % 2 + 1)
                pe.wait_ge(s_p, u + 1)
                for dt in range(NT):
                    b, r = divmod(dt, 2)
                    if st == 0 and r == 0 and head > 0:
                        pe.wait_ge(s_oe, (head - 1) * NT + 2 * (b + 1))
                    mm = pe.matmul(PS[0:T, b, r * 256:r * 256 + CP], pr[st % 2][:, dt * T:(dt + 1) * T],
                                   hs[head % 2][:, st, :], start=(st == 0 and r == 0), stop=(st == NT - 1),
                                   skip_group_check=True)
                    if st == NT - 1 and r == 1 and b < 4:
                        mm.then_inc(s_ob, 1)
                mm.then_inc(s_pu, 1)
                if head % 2 == 0 and head >= 2 and 3 <= st < 6:
                    pair_transposes(head // 2 - 1, st - 3)
                if u == UV2_STEP:
                    pe.wait_ge(s_te, 9 * (head // 2) + 3)
                    uv_transposes(2, 5)
            for k in range(3):
                pair_transposes(PAIRS - 1, k)
            pe.wait_ge(s_wo, 16)
            pe.wait_ge(s_misc, 32)

            def gate_transposes(t):
                pe.wait_ge(s_y, t + 1)
                for half in range(2):
                    if t >= 1:
                        pe.wait_ge(s_yte, 2 * (t - 1) + half + 1)
                    for k in range(3):
                        mm = pe.transpose(PS[:, 4 + half, k * T:(k + 1) * T],
                                          y[t % 2][:, (3 * half + k) * P:(3 * half + k + 1) * P], ident[0:T, 0:T])
                    mm.then_inc(s_yt, 1)

            def gate_logits(t):
                pe.wait_ge(s_yte, 2 * t + 2)
                if t >= 2:
                    pe.wait_ge(s_oh2, t - 1)
                for k in range(KT):
                    mm = pe.matmul(PS[0:T, 6 + t % 2, 0:EXPERTS], yT[t % 2][:, k, :], WgS[:, k, :],
                                   start=(k == 0), stop=(k == KT - 1))
                mm.then_inc(s_lg, 1)
            for t in range(NT + 1):
                if t < NT:
                    pe.wait_ge(s_eb[t % 2], 16 * (t // 2 + 1))
                    if t == 0:
                        pe.wait_ge(s_oe, UNITS)
                    if t >= 2:
                        pe.wait_ge(s_pje, 2 * (t - 1))
                    for c in range(2):
                        for k in range(LAYERS * KT):
                            mm = pe.matmul(PS[0:T, 2 * (t % 2) + c, 0:HALF], EB[t % 2][:, k, :],
                                           Wo[:, k, c * HALF:(c + 1) * HALF], start=(k == 0),
                                           stop=(k == LAYERS * KT - 1))
                        mm.then_inc(s_pj, 1)
                if t >= 2:
                    gate_logits(t - 2)
                if t >= 1:
                    gate_transposes(t - 1)
            gate_logits(NT - 1)
            for t in range(NT):
                pe.wait_ge(s_oh2, t + 1)
                for q in range(t):
                    pe.matmul(PS[0:T, 0, t * 16:(t + 1) * 16], ones[:, :], oh2[:, q, :], start=(q == 0), stop=False)
                mm = pe.matmul(PS[0:T, 0, t * 16:(t + 1) * 16], tri[:, :], oh2[:, t, :], start=(t == 0), stop=True)
            mm.then_inc(s_cum, 1)
            for u in range(TOPK * NT):
                pe.wait_ge(s_tk, u + 1)
                pe.matmul(PS[0:T, 2, 0:EXPERTS * RT], ohs[u % 2][:, :], oht[u % 2][:, :], start=(u == 0),
                          stop=(u == TOPK * NT - 1)).then_inc(s_tku, 1)

            def row_transposes(e):
                for j in range(RT):
                    u = e * RT + j
                    pe.wait_ge(s_xg[u % 3], 16 * (u // 3 + 1))
                    for half in range(2):
                        v = 2 * u + half
                        if v >= 2:
                            pe.wait_ge(s_xte, v - 1)
                        for k in range(3):
                            mm = pe.transpose(PS[:, half, k * T:(k + 1) * T],
                                              Xg[u % 3][:, (3 * half + k) * P:(3 * half + k + 1) * P], ident[0:T, 0:T])
                        mm.then_inc(s_xt, 1)
            row_transposes(0)
            for e in range(EXPERTS):
                pe.wait_ge(s_xte, 2 * RT * (e + 1))
                pe.wait_ge(s_w1[e % 2], 16 * (e // 2 + 1))
                if e == 0:
                    pe.wait_ge(s_tok, 1)
                if e >= 1:
                    pe.wait_ge(s_ac, 2 * e)
                for m in (2, 3, 0, 1):
                    for k in range(KT):
                        mm = pe.matmul(PS[:, 2 + m, 0:ROWS], W1s[e % 2][:, k, m * P:(m + 1) * P], XgT[e % 2][:, k, :],
                                       start=(k == 0), stop=(k == KT - 1))
                    mm.then_inc(s_h1, 1)
                if e + 1 < EXPERTS:
                    row_transposes(e + 1)
                pe.wait_ge(s_w2[e % 2], 16 * (e // 2 + 1))
                pe.wait_ge(s_ac, 2 * (e + 1))
                for j in range(RT):
                    u = e * RT + j
                    for c in range(2):
                        if u >= 1:
                            pe.wait_ge(s_yee, 2 * (u - 1) + c + 1)
                        for k in range(2):
                            mm = pe.matmul(PS[0:T, 6 + c, 0:HALF], actT[:, k, j * T:(j + 1) * T],
                                           W2s[e % 2][:, k, c * HALF:(c + 1) * HALF], start=(k == 0), stop=(k == 1))
                        mm.then_inc(s_yb, 1)

        @block.scalar
        def _(act):
            chain = [0]

            def link(ins):
                chain[0] += 1
                ins.then_inc(s_ach, 1)
                act.wait_ge(s_ach, chain[0])

            for t in range(NT):
                act.wait_ge(s_x[t], 16)
                link(act.activation(sjunk[:, :], X[:, t, :], ACT.Copy, accum_out=sumx[:, t:t + 1]))
                link(act.activation(nmean[:, t:t + 1], sumx[:, t:t + 1], ACT.Copy, scale=-1.0 / D))
                act.activation(sjunk[:, :], X[:, t, :], ACT.Square, bias=nmean[:, t:t + 1],
                               accum_out=sumsq[:, t:t + 1]).then_inc(s_ssq, 1)
                act.wait_ge(s_ssq, t + 1)
            for u in range(2 * NT):
                t, half = divmod(u, 2)
                act.wait_ge(s_tp, u + 1)
                act.activation(xnT[:, 3 * half:3 * half + 3, t * T:(t + 1) * T],
                               PS[:, u % 4, 0:3 * T].rearrange("p (k n) -> p k n", k=3), ACT.Copy).then_inc(s_tpe, 1)
            act.wait_ge(s_small, 64)
            for c, (c0, cn) in enumerate(CHUNKS):
                for m in range(KT):
                    u = KT * c + m
                    act.wait_ge(s_x1, u + 1)
                    act.activation(x1T[:, m, c0:c0 + cn], PS[:, 6 + u % 2, 0:cn], ACT.Relu,
                                   bias=b_ahT[:, m:m + 1]).then_inc(s_x1e, 1)

            def h_store(i):
                l, t, c = half_tile(i)
                act.wait_ge(s_h, i + 1)
                if i >= 4:
                    act.wait_ge(s_hd[i % 4], 16 * (i // 4))
                act.activation(hsb[i % 4][:, :], PS[0:T, 6 + i % 2, 0:HALF], ACT.Copy).then_inc(s_he, 1)
                act.wait_ge(s_he, i + 1)
                q0 = l * HEADS + c * HEADS // 2
                act.dma_start(h_dram[q0:q0 + HEADS // 2, t * T:(t + 1) * T, :].rearrange("q p c -> p q c"),
                              hsb[i % 4][:, :].rearrange("p (q c) -> p q c", q=HEADS // 2)).then_inc(s_hd[i % 4], 16)

            def uv_store(l, b0):
                if l >= 1:
                    act.wait_ge(s_uvd, 16 * l)
                for q, (t0, t1) in enumerate(PAIR_GROUPS):
                    act.wait_ge(s_uvt, 3 * l + q + 1)
                    act.activation(UVr[:, t0 * T:t1 * T], PS[0:2 * HEADS, b0 + q, 0:(t1 - t0) * T],
                                   ACT.Copy).then_inc(s_uvr, 1)
            for i in range(COUNT_H + 3):
                h_store(i)
            for c, (c0, cn) in enumerate(CHUNKS):
                act.wait_ge(s_lr, c + 1)
                act.activation(Lr[:, c0:c0 + cn], PS[0:2 * HEADS_ALL, c, 0:cn], ACT.Copy).then_inc(s_lre, 1)
            for i in range(COUNT_H + 3, 3 * HU // 4 + 3):
                h_store(i)
            uv_store(0, 0)
            for i in range(3 * HU // 4 + 3, HU):
                h_store(i)
            uv_store(1, 0)

            def head_store(head):
                for dt in range(NT):
                    b, r = divmod(dt, 2)
                    if r == 0:
                        act.wait_ge(s_rs, head * 5 + b + 1)
                    if dt == 0 and head % 2 == 0 and head >= 2:
                        act.wait_ge(s_tr, 9 * (head // 2))
                    if dt == 0 and head == 0:
                        act.wait_ge(s_pu, 2 + NT)
                    act.activation(emb[:, dt, (head % 2) * C:(head % 2 + 1) * C], PS[0:T, b, r * 256:r * 256 + C],
                                   ACT.Copy, scale=rs[:, dt:dt + 1]).then_inc(s_oe, 1)

            def pair_store(pair, k):
                if k == 0 and pair >= 1:
                    act.wait_ge(s_ed, 16 * pair)
                for q, (t0, t1) in enumerate(PAIR_GROUPS):
                    act.wait_ge(s_tr, 9 * pair + 3 * k + q + 1)
                    act.activation(embT[:, k, t0 * T:t1 * T], PS[:, 5 + q, 0:(t1 - t0) * T], ACT.Relu,
                                   bias=blT[:, pair * 3 + k:pair * 3 + k + 1]).then_inc(s_te, 1)
            act.sem_inc(s_te, 3)
            for u in range(UNITS):
                head, st = divmod(u, NT)
                act.wait_ge(s_tt, u + 1)
                if u >= 2:
                    act.wait_ge(s_p, u - 1)
                act.activation(ex[st % 2][:, :], tt[st % 2][:, :], ACT.Exp, bias=as2[:, u:u + 1]).then_inc(s_ex, 1)
                if st == 1 and head >= 1:
                    head_store(head - 1)
                if head % 2 == 0 and head >= 2 and 5 <= st < 8:
                    pair_store(head // 2 - 1, st - 5)
                if u == UV2_STEP + 1:
                    uv_store(2, 5)
            head_store(HEADS_ALL - 1)
            for k in range(3):
                pair_store(PAIRS - 1, k)
            for t in range(NT):
                for half in range(2):
                    act.wait_ge(s_yt, 2 * t + half + 1)
                    if t >= 2 and half == 0:
                        act.wait_ge(s_lg, t - 1)
                    act.activation(yT[t % 2][:, 3 * half:3 * half + 3, :],
                                   PS[:, 4 + half, 0:3 * T].rearrange("p (k n) -> p k n", k=3), ACT.Copy).then_inc(s_yte, 1)
            act.wait_ge(s_sm, 1)
            act.activation(edt[:, :], small[:, 0:NT], ACT.Exp).then_inc(s_sme, 1)

            def rows_store(e):
                for j in range(RT):
                    for half in range(2):
                        v = 2 * (e * RT + j) + half
                        act.wait_ge(s_xt, v + 1)
                        if e >= 2 and j == 0 and half == 0:
                            act.wait_ge(s_h1, 4 * (e - 1))
                        act.activation(XgT[e % 2][:, 3 * half:3 * half + 3, j * T:(j + 1) * T],
                                       PS[:, half, 0:3 * T].rearrange("p (k n) -> p k n", k=3), ACT.Copy).then_inc(s_xte, 1)
            rows_store(0)
            for e in range(EXPERTS):
                for m in range(2):
                    act.wait_ge(s_h1, 4 * e + m + 1)
                    if e >= 1:
                        act.wait_ge(s_ac, 2 * (e - 1) + m + 1)
                    act.activation(sg[m][:, :], PS[:, 4 + m, 0:ROWS], ACT.Silu).then_inc(s_sg, 1)
                if e + 1 < EXPERTS:
                    rows_store(e + 1)
                for j in range(RT):
                    u = e * RT + j
                    for c in range(2):
                        act.wait_ge(s_yb, 2 * u + c + 1)
                        if u >= 2 and c == 0:
                            act.wait_ge(s_yed[u % 2], 16 * (u // 2))
                        act.activation(ye[u % 2][:, c * HALF:(c + 1) * HALF], PS[0:T, 6 + c, 0:HALF],
                                       ACT.Copy).then_inc(s_yee, 1)
                    act.wait_ge(s_yee, 2 * u + 2)
                    act.dma_start(ye_dram[u * T:(u + 1) * T, :], ye[u % 2][:, :]).then_inc(s_yed[u % 2], 16)

        @block.vector
        def _(v):
            chain = [0]

            def link(ins):
                chain[0] += 1
                ins.then_inc(s_dch, 1)
                v.wait_ge(s_dch, chain[0])

            link(v.memset(one_row[:, :], 1.0))
            v.wait_ge(s_edges, 32)
            link(v.tensor_copy(key[:, :], srcI[:, :]))
            link(v.tensor_scalar(other1[:, :], dstI[:, :], 1.0, None, ALU.add))
            link(v.tensor_scalar(bucket[:, :], key[:, :], float(T), None, ALU.is_ge))
            for j in range(2, NT):
                link(v.scalar_tensor_tensor(out=bucket[:, :], in0=key[:, :], scalar=float(T * j), in1=bucket[:, :],
                                            op0=ALU.is_ge, op1=ALU.add))
            link(v.scalar_tensor_tensor(out=local1[:, :], in0=bucket[:, :], scalar=-float(T), in1=key[:, :],
                                        op0=ALU.mult, op1=ALU.add))
            link(v.tensor_scalar(local1[:, :], local1[:, :], 1.0, None, ALU.add))
            for j in range(NT):
                ins = v.tensor_scalar(inb[:, j, :], bucket[:, :], float(j), None, ALU.is_equal)
            link(ins)
            for j in range(NT):
                ins = v.tensor_tensor_scan(cum[:, j, :], one_row[:, :], inb[:, j, :], 0.0, ALU.mult, ALU.add)
            link(ins)
            v.tensor_copy(tot16[:, :], cum[:, :, ET - 1]).then_inc(s_tot, 1)
            v.wait_ge(s_pre, 1)
            link(v.tensor_scalar(colsI[:, 0, :], PS[0:T, 5, 16:16 + NT], float(SLOTS - 1), None, ALU.add))
            link(v.tensor_scalar(colsI[:, 1, :], colsI[:, 0, :], SLOTS.bit_length() - 1, None, ALU.arith_shift_right))
            link(v.tensor_copy(cols[:, 0, :], colsI[:, 1, :]))
            link(v.tensor_tensor_scan(cols[:, 1, :], one_row[:, 0:NT], cols[:, 0, :], 0.0, ALU.mult, ALU.add))
            link(v.tensor_tensor(cols[:, 2, :], cols[:, 1, :], cols[:, 0, :], ALU.subtract))
            link(v.scalar_tensor_tensor(out=cols[:, 3, :], in0=cols[:, 2, :], scalar=float(SLOTS), in1=PS[0:T, 5, 0:NT],
                                        op0=ALU.mult, op1=ALU.add))
            link(v.tensor_scalar(cols[:, 4, :], cols[:, 3, :], -1.0, None, ALU.add))
            for j in range(NT):
                dstt = pos if j == 0 else tmpj
                link(v.scalar_tensor_tensor(out=dstt[:, :], in0=cum[:, j, :], scalar=cols[:, 4, j:j + 1], in1=inb[:, j, :],
                                            op0=ALU.add, op1=ALU.mult))
                if j:
                    link(v.tensor_tensor(pos[:, :], pos[:, :], tmpj[:, :], ALU.add))
            link(v.tensor_copy(posI[:, 0, :], pos[:, :]))
            link(v.tensor_scalar(posI[:, 1, :], posI[:, 0, :], P - 1, None, ALU.bitwise_and))
            link(v.tensor_scalar(posI[:, 2, :], posI[:, 0, :], P.bit_length() - 1, None, ALU.arith_shift_right))
            link(v.tensor_scalar(slot1[:, :], posI[:, 1, :], 1.0, None, ALU.add))
            link(v.tensor_scalar(tile1[:, :], posI[:, 2, :], 1.0, None, ALU.add))
            for t in range(NT):
                v.wait_ge(s_rstd, t + 1)
                if t >= 2:
                    v.wait_ge(s_tp, 2 * (t - 1))
                v.tensor_scalar(xn[t % 2][:, :], X[:, t, :], nmean[:, t:t + 1], rstd[:, t:t + 1], ALU.add,
                                ALU.mult).then_inc(s_xn, 1)

            def place(q, t, free=None):
                if free is not None:
                    v.wait_ge(s_perm, free)
                v.tensor_scalar(pick[q][:, :], iota1[0:T, 0:P], slot1[:, ds(t, 1)], None, ALU.is_equal)
                v.tensor_scalar(put[q][:, 0:ST], iota1[0:T, 0:ST], tile1[:, ds(t, 1)], local1[:, ds(t, 1)],
                                ALU.is_equal, ALU.mult)
                v.tensor_scalar(put[q][:, ST:2 * ST], iota1[0:T, 0:ST], tile1[:, ds(t, 1)], other1[:, ds(t, 1)],
                                ALU.is_equal, ALU.mult).then_inc(s_pick, 1)
            v.wait_ge(s_c, 4)
            for q in range(4):
                place(q, q)
            with v.Fori(1, ET // 4) as i:
                for q in range(4):
                    place(q, i * 4 + q, i * 4 + q - 3)
            link(v.tensor_copy(identb[:, :], ident[:, :]))
            link(v.tensor_scalar(gbF[:, :], iota1[0:1, 0:NG], cols[0:1, 2, 1:2], None, ALU.is_gt))
            for j in range(2, NT):
                link(v.scalar_tensor_tensor(out=gbF[:, :], in0=iota1[0:1, 0:NG], scalar=cols[0:1, 2, j:j + 1],
                                            in1=gbF[:, :], op0=ALU.is_gt, op1=ALU.add))
            link(v.tensor_scalar(gbI[:, :], gbF[:, :], 3.0, None, ALU.mult))
            v.wait_ge(s_perm, ET)
            link(v.tensor_copy(sorted_[:, :], PS[:, 4, 0:2 * ST]))

            wcols = [0]

            def logit_weights(l, k):
                b = (l + 1) % 2
                if k == 0:
                    v.wait_ge(s_w[b], 16 * (l // 2 + 1))
                    v.wait_ge(s_aB, 32 * (l + 1))
                for sd in range(2):
                    for h in range(HEADS):
                        col = l * 2 * HEADS + sd * HEADS + h
                        v.tensor_tensor_reduce(wjunk[:, h % 2, :], W[b][:, k, h * C:(h + 1) * C],
                                               aB[:, sd, h * C:(h + 1) * C], 1.0, 0.0, ALU.mult, ALU.add,
                                               wa[:, k, col:col + 1]).then_inc(s_wj, 1)
                        wcols[0] += 1
                        if wcols[0] >= 2:
                            v.wait_ge(s_wj, wcols[0] - 1)
                if k == KT - 1:
                    v.wait_ge(s_wj, wcols[0])
                    v.sem_inc(s_wa, 1)

            def onehots(n):
                for q in range(GROUP):
                    col = n * GROUP + q
                    v.wait_ge(s_ohu, col + 1)
                    v.tensor_scalar(oh_src[q][:, :], iota1[:, 0:T], sorted_[:, ds(col, 1)], None, ALU.is_equal)
                    v.tensor_scalar(oh_dst[q][:, :], iota1[:, :], sorted_[:, ds(col + ST, 1)], None,
                                    ALU.is_equal).then_inc(s_oh, 1)

            def add_counts(par, n):
                r = v.value_load(gbI[0:1, ds(n, 1)], min_val=0, max_val=3 * (NT - 1))
                v.wait_ge(s_ohu, n * GROUP + 2 * GROUP)
                v.wait_ge(s_ct, n + 2)
                v.tensor_tensor(CT[:, ds(r, 3), :], PS[0:T, 3 * par:3 * par + 3, 0:CHUNK], CT[:, ds(r, 3), :],
                                ALU.add).then_inc(s_ct, 1)
            v.wait_ge(s_ctz, 1)
            v.sem_inc(s_ohu, GROUP)
            v.sem_inc(s_ct, 2)
            onehots(0)
            pending = [(l, k) for l in range(2) for k in range(KT)]
            for seg in range(NG // 4):
                with v.Fori(seg * 2, seg * 2 + 2) as i:
                    onehots(i * 2 + 1)
                    add_counts(0, i * 2)
                    onehots(i * 2 + 2)
                    add_counts(1, i * 2 + 1)
                if pending:
                    logit_weights(*pending.pop(0))
            onehots(NG - 1)
            add_counts(0, NG - 2)
            add_counts(1, NG - 1)
            for k in range(KT):
                logit_weights(2, k)
            v.wait_ge(s_ct, NG + 2)
            for t in range(NT):
                c0 = t * CW + t * T
                v.tensor_tensor(CTf[:, c0:c0 + T], CTf[:, c0:c0 + T], ident[0:T, 0:T], ALU.add).then_inc(s_ct, 1)
            v.wait_ge(s_ct, NG + 2 + NT)
            for s in range(NT + 1):
                if s < NT:
                    if s >= 2:
                        v.wait_ge(s_mt, 2 * (s - 1))
                    v.tensor_scalar(maskb[s % 2][:, :], CTf[:, s * CW:s * CW + N], 1.0, None, ALU.min).then_inc(s_mask, 1)
                if s >= 1:
                    for half in range(2):
                        v.wait_ge(s_mt, 2 * (s - 1) + half + 1)
                        v.tensor_scalar(NEG[:, 5 * half:5 * half + 5, (s - 1) * T:s * T],
                                        PSB[0:T, 4 + half, 0:630].rearrange("p (k n) -> p k n", k=5)[:, :, 0:T],
                                        1.0, BIG, ALU.subtract, ALU.mult).then_inc(s_neg, 1)
            v.wait_ge(s_neg, 2 * NT)
            v.wait_ge(s_lc, 1)
            link(v.tensor_copy(logitc[:, :, :], PS[0:T, 3, 0:240].rearrange("p (t c) -> p t c", c=24)))

            def neighbour_max(n):
                j, dt = divmod(n, NT)
                if dt == 0:
                    v.wait_ge(s_asB[j % 2], 16 * (j // 2 + 1))
                if n >= 2:
                    v.wait_ge(s_mx, n - 1)
                v.tensor_tensor_reduce(junk[n % 2][:, :], asB[j % 2][0:T, :], NEG[:, dt, :], 1.0, -3.0e38,
                                       ALU.add, ALU.max, mx_all[:, dt, j:j + 1]).then_inc(s_mx, 1)

            def uv_columns(l):
                v.wait_ge(s_mx, NT * HEADS * (l + 1))
                ad = logitc[:, :, (2 * l + 1) * HEADS:(2 * l + 2) * HEADS]
                link(v.tensor_tensor(zz[:, :, :], mx_all[:, :, l * HEADS:(l + 1) * HEADS], ad, ALU.add))
                link(v.scalar_tensor_tensor(out=zz[:, :, :], in0=zz[:, :, :], scalar=SLOPE, in1=zz[:, :, :],
                                            op0=ALU.mult, op1=ALU.max))
                link(v.tensor_tensor(UV[l % 2][:, :, 0:HEADS], ad, zz[:, :, :], ALU.subtract))
                link(v.scalar_tensor_tensor(out=UV[l % 2][:, :, HEADS:], in0=ad, scalar=SLOPE, in1=zz[:, :, :],
                                            op0=ALU.mult, op1=ALU.subtract))
                for dst_, f in ((as8, 1.0 - SLOPE), (as2, SLOPE)):
                    link(v.tensor_scalar(dst_[:, l * HEADS * NT:(l + 1) * HEADS * NT].rearrange("p (h t) -> p t h", h=HEADS),
                                         logitc[:, :, 2 * l * HEADS:(2 * l + 1) * HEADS], f, None, ALU.mult))
                v.sem_inc(s_uv, 1)
            for l in range(2):
                for n in range(l * M2, (l + 1) * M2):
                    neighbour_max(n)
                uv_columns(l)
            v.memset(hs[0][:, :, C:CP], 1.0).then_inc(s_ones, 1)

            def exponent(u):
                head, st = divmod(u, NT)
                if st == 0:
                    v.wait_ge(s_hs[head % 2], 48 * (head // 2 + 1))
                if u >= 2:
                    v.wait_ge(s_ex, u - 1)
                v.scalar_tensor_tensor(out=tt[st % 2][:, :], in0=uB[head % 2][0:T, :], scalar=as8[:, u:u + 1],
                                       in1=vB[head % 2][0:T, :], op0=ALU.add, op1=ALU.max).then_inc(s_tt, 1)

            def probs(u):
                st = u % NT
                v.wait_ge(s_ex, u + 1)
                v.wait_ge(s_pu, u + 1)
                v.tensor_tensor(pr[st % 2][:, :], ex[st % 2][:, :], CTf[:, st * CW:st * CW + N], ALU.mult).then_inc(s_p, 1)

            def sums(head):
                for b in range(5):
                    if b < 4:
                        v.wait_ge(s_ob, head * 4 + b + 1)
                    else:
                        v.wait_ge(s_pu, head * NT + NT + 2)
                    if b == 0 and head:
                        v.wait_ge(s_oe, head * NT)
                    v.tensor_scalar(den[:, 2 * b:2 * b + 2], PS[0:T, b, :].rearrange("p (r c) -> p r c", r=2)[:, :, C],
                                    1e-16, None, ALU.add).then_inc(s_den, 1)
                    v.wait_ge(s_den, head * 5 + b + 1)
                    v.reciprocal(rs[:, 2 * b:2 * b + 2], den[:, 2 * b:2 * b + 2]).then_inc(s_rs, 1)
            exponent(0)
            done = 0
            for u in range(UNITS):
                head, st = divmod(u, NT)
                if u + 1 < UNITS:
                    exponent(u + 1)
                while done < min(M2, (u + 1) * M2 // M2_STEPS):
                    neighbour_max(2 * M2 + done)
                    done += 1
                    if done == M2:
                        uv_columns(2)
                probs(u)
                if u == 1:
                    v.wait_ge(s_pu, 3)
                    v.memset(hs[1][:, :, C:CP], 1.0).then_inc(s_ones, 1)
                if st == 0 and head:
                    sums(head - 1)
            sums(HEADS_ALL - 1)
            v.wait_ge(s_oe, UNITS)
            v.memset(zrow[:, :], 0.0).then_inc(s_zr, 1)
            v.wait_ge(s_misc, 32)

            def gate(t):
                v.wait_ge(s_lg, t + 1)
                link(v.tensor_copy(lg[:, t, :], PS[0:T, 6 + t % 2, 0:EXPERTS]))
                link(v.max(top[:, t, :], lg[:, t, :]))
                link(v.max_index(tidx[:, t, :], top[:, t, :], lg[:, t, :]))
                link(v.tensor_copy(idxF[:, t, :], tidx[:, t, 0:TOPK]))
                for k in range(TOPK):
                    ins = v.tensor_scalar(ohp[:, t, k * EXPERTS:(k + 1) * EXPERTS], iota1[0:T, 0:EXPERTS], 1.0,
                                          idxF[:, t, k:k + 1], ALU.subtract, ALU.is_equal)
                link(ins)
                v.tensor_copy(oh2[:, t, :], ohp[:, t, :]).then_inc(s_oh2, 1)
            for t in range(NT):
                v.wait_ge(s_xr[t % 2], 16 * (t // 2 + 1))
                for c in range(2):
                    f = slice(c * HALF, (c + 1) * HALF)
                    v.wait_ge(s_pj, 2 * t + c + 1)
                    link(v.tensor_tensor(rr[c][:, :], PS[0:T, 2 * (t % 2) + c, 0:HALF], boB[0:T, f], ALU.add))
                    v.scalar_tensor_tensor(out=x2[:, t, f], in0=rr[c][:, :], scalar=0.0, in1=xr[t % 2][:, f],
                                           op0=ALU.max, op1=ALU.add).then_inc(s_pje, 1)
                    v.wait_ge(s_pje, 2 * t + c + 1)
                    link(v.bn_stats(st2[:, 6 * c:6 * c + 6], x2[:, t, f]))
                link(v.bn_aggr(mv2[:, 0:2], st2[:, :]))
                v.tensor_scalar(mv2[:, 2:3], mv2[:, 1:2], LN_EPS, None, ALU.add).then_inc(s_v2, 1)
                v.wait_ge(s_r2, t + 1)
                if t >= 2:
                    v.wait_ge(s_yd[t % 2], 16 * (t // 2))
                    v.wait_ge(s_yt, 2 * (t - 1))
                v.tensor_scalar(y[t % 2][:, :], x2[:, t, :], mv2[:, 0:1], rstd2[:, t:t + 1], ALU.subtract,
                                ALU.mult).then_inc(s_y, 1)
                v.wait_ge(s_y, t + 1)
                if t >= 2:
                    gate(t - 2)
            gate(NT - 2)
            gate(NT - 1)
            v.tensor_tensor(small[:, 0:NT], top[:, :, 1], top[:, :, 0], ALU.subtract).then_inc(s_sm, 1)
            v.wait_ge(s_sme, 1)
            link(v.tensor_scalar(small[:, NT:2 * NT], edt[:, :], 1.0, None, ALU.add))
            link(v.reciprocal(wk[:, :, 0], small[:, NT:2 * NT]))
            link(v.tensor_tensor(wk[:, :, 1], wk[:, :, 0], edt[:, :], ALU.mult))
            v.wait_ge(s_cum, 1)
            link(v.tensor_tensor(ohp[:, :, :], ohp[:, :, :], PS[0:T, 0, 0:16 * NT].rearrange("p (t e) -> p t e", e=16),
                                 ALU.mult))
            link(v.tensor_reduce(posk[:, :, :], ohp[:, :, :].rearrange("p t (k e) -> p t k e", k=TOPK), AX.X, ALU.add))
            link(v.tensor_scalar(keep[:, :, :], posk[:, :, :], float(CAP), None, ALU.is_lt))
            link(v.tensor_copy(rk[:, :, 0], posk[:, :, 0]))
            link(v.tensor_scalar(rk[:, :, 1], posk[:, :, 1], float(CAP), None, ALU.add))
            link(v.tensor_scalar(rsub[:, :, :], rk[:, :, :], float(T), None, ALU.is_ge))
            link(v.scalar_tensor_tensor(out=rsub[:, :, :], in0=rk[:, :, :], scalar=float(2 * T), in1=rsub[:, :, :],
                                        op0=ALU.is_ge, op1=ALU.add))
            link(v.scalar_tensor_tensor(out=rslot[:, :, :], in0=rsub[:, :, :], scalar=-float(T), in1=rk[:, :, :],
                                        op0=ALU.mult, op1=ALU.add))
            link(v.scalar_tensor_tensor(out=rtile[:, :, :], in0=idxF[:, :, :], scalar=float(RT), in1=rsub[:, :, :],
                                        op0=ALU.mult, op1=ALU.add))
            link(v.tensor_scalar(tmpk[:, :, :], keep[:, :, :], -1000.0, 1001.0, ALU.mult, ALU.add))
            link(v.tensor_tensor(rslot[:, :, :], rslot[:, :, :], tmpk[:, :, :], ALU.add))
            link(v.tensor_scalar(rtile[:, :, :], rtile[:, :, :], 1.0, None, ALU.add))
            for u in range(TOPK * NT):
                t, k = divmod(u, TOPK)
                if u >= 2:
                    v.wait_ge(s_tku, u - 1)
                v.tensor_scalar(ohs[u % 2][:, :], iota1[0:T, 0:T], rslot[:, t, k:k + 1], None, ALU.is_equal)
                v.tensor_scalar(oht[u % 2][:, :], iota1[0:T, 0:EXPERTS * RT], rtile[:, t, k:k + 1], tokv[:, t:t + 1],
                                ALU.is_equal, ALU.mult).then_inc(s_tk, 1)
            v.wait_ge(s_tku, TOPK * NT)
            v.tensor_scalar(tokI[:, :], PS[0:T, 2, 0:EXPERTS * RT], float(N), None, ALU.add).then_inc(s_tok, 1)
            link(v.tensor_tensor(wk[:, :, :], wk[:, :, :], keep[:, :, :], ALU.mult))
            link(v.tensor_scalar(tmpk[:, :, :], rk[:, :, :], float(ROWS - 1), None, ALU.subtract))
            link(v.tensor_tensor(tmpk[:, :, :], tmpk[:, :, :], keep[:, :, :], ALU.mult))
            link(v.tensor_scalar(tmpk[:, :, :], tmpk[:, :, :], float(ROWS - 1), None, ALU.add))
            link(v.scalar_tensor_tensor(out=rowF[:, :, :], in0=idxF[:, :, :], scalar=float(ROWS), in1=tmpk[:, :, :],
                                        op0=ALU.mult, op1=ALU.add))
            v.tensor_copy(rowI[:, :].rearrange("p (t k) -> p t k", k=TOPK), rowF[:, :, :]).then_inc(s_tok, 1)
            for e in range(EXPERTS):
                for m in range(2):
                    v.wait_ge(s_h1, 4 * e + 2 + m + 1)
                    v.wait_ge(s_sg, 2 * e + m + 1)
                    if e >= 1:
                        v.wait_ge(s_yb, 2 * RT * e)
                    v.tensor_tensor(actT[:, m, :], PS[:, 2 + m, 0:ROWS], sg[m][:, :], ALU.mult).then_inc(s_ac, 1)
            for t in range(NT):
                v.wait_ge(s_g0[t % 3], 16 * (t // 3 + 1))
                link(v.scalar_tensor_tensor(out=g0[t % 3][:, :], in0=g0[t % 3][:, :], scalar=wk[:, t, 0:1], in1=x2[:, t, :],
                                            op0=ALU.mult, op1=ALU.add))
                v.wait_ge(s_g1[t % 3], 16 * (t // 3 + 1))
                v.scalar_tensor_tensor(out=g1[t % 3][:, :], in0=g1[t % 3][:, :], scalar=wk[:, t, 1:2], in1=g0[t % 3][:, :],
                                       op0=ALU.mult, op1=ALU.add).then_inc(s_fin, 1)


_INS = ['x', 'src', 'dst', 'L0_gnn_W_ah', 'L0_gnn_b_ah', 'L0_gnn_W0', 'L0_gnn_a_src0', 'L0_gnn_a_dst0', 'L0_gnn_b0',
        'L0_gnn_W1', 'L0_gnn_a_src1', 'L0_gnn_a_dst1', 'L0_gnn_b1', 'L0_gnn_W2', 'L0_gnn_a_src2', 'L0_gnn_a_dst2',
        'L0_gnn_b2', 'L0_gnn_W_out', 'L0_gnn_b_out', 'L0_ffn_Wg', 'L0_ffn_W1', 'L0_ffn_W2']


def kernel(**inputs):
    import numpy as _np
    import concourse.bacc as _bacc
    from concourse import mybir as _mybir
    from concourse.bass_utils import run_bass_kernel_spmd as _run

    nc = _bacc.Bacc("TRN2", target_bir_lowering=False, num_devices=1)
    arrays, aps = {}, {}
    for name in _INS:
        a = _np.ascontiguousarray(inputs[name])
        arrays[f"in_{name}_dram"] = a
        aps[name.replace("L0_gnn_", "").replace("L0_", "")] = nc.dram_tensor(
            f"in_{name}_dram", a.shape, _mybir.dt.from_np(a.dtype), kind="ExternalInput").ap()
    out = nc.dram_tensor("out_0_dram", (N, D), F32, kind="ExternalOutput").ap()
    gnn_moe(nc, aps["x"], aps["src"], aps["dst"], aps["W_ah"], aps["b_ah"],
            [aps[f"W{l}"] for l in range(LAYERS)], [aps[f"a_src{l}"] for l in range(LAYERS)],
            [aps[f"a_dst{l}"] for l in range(LAYERS)], [aps[f"b{l}"] for l in range(LAYERS)],
            aps["W_out"], aps["b_out"], aps["ffn_Wg"], aps["ffn_W1"], aps["ffn_W2"], out)
    r = _run(nc, [arrays], core_ids=[0])
    return r.results[0]["out_0_dram"]
```

```python
from contextlib import ExitStack

import concourse.bass as bass
from concourse import mybir

F32 = mybir.dt.float32
F16 = mybir.dt.float16
BF16 = mybir.dt.bfloat16
F32R = mybir.dt.float32r
I32 = mybir.dt.int32
U32 = mybir.dt.uint32
I16 = mybir.dt.int16
ALU = mybir.AluOpType
ACT = mybir.ActivationFunctionType
AX = mybir.AxisListType
ds = bass.ds

N = 1250
T = 125
NT = N // T
D = 768
P = 128
KT = D // P
LAYERS = 3
HEADS = 4
C = D // HEADS
CP = C + 1
HEADS_ALL = LAYERS * HEADS
PAIRS = HEADS_ALL // 2
SLOPE = 0.2
LN_EPS = 1e-5
BIG = 1.0e30

E = 20000
ET = E // T
GROUP = 4
SLOTS = GROUP * P
NG = (E + NT * (SLOTS - 1)) // SLOTS
NG += NG % 2
ST = NG * GROUP
CHUNK = 417
CW = 3 * CHUNK
CHUNKS = [(0, CHUNK), (CHUNK, CHUNK), (2 * CHUNK, N - 2 * CHUNK)]

EXPERTS = 8
TOPK = 2
HID = 256
CAP = int(1.2 * N / EXPERTS)
RT = 3
ROWS = RT * T
assert TOPK * CAP < ROWS and NG * SLOTS >= E + NT * (SLOTS - 1) - SLOTS


def gnn_moe(nc, x, src, dst, W_ah, b_ah, Wl, a_src, a_dst, bl, W_out, b_out, Wg, W1, W2, out):
    h_dram = nc.dram_tensor("h_rows", (HEADS_ALL, N, C), F32, kind="Internal").ap()
    logit_rows = nc.dram_tensor("logit_rows", (2 * HEADS_ALL, N), F32, kind="Internal").ap()
    uv_rows = nc.dram_tensor("uv_rows", (2 * HEADS_ALL, N), F32, kind="Internal").ap()
    emb_dram = nc.dram_tensor("emb_t", (LAYERS * D, N), F32, kind="Internal").ap()
    y_dram = nc.dram_tensor("y_rows", (N + 1, D), F32, kind="Internal").ap()
    ye_dram = nc.dram_tensor("expert_rows", (EXPERTS * ROWS, D), F32, kind="Internal").ap()

    with ExitStack() as ctx:
        ctx.enter_context(nc.allow_non_contiguous_dma("bias columns and node tiles"))

        def sem(name):
            return ctx.enter_context(nc.semaphore(name))

        def alloc(stack):
            return lambda name, shape, dt: stack.enter_context(nc.sbuf_tensor(name, shape, dt))

        sb = alloc(ctx)
        PS = ctx.enter_context(nc.psum_tensor("PS", [P, 8, 512], F32))
        PSB = PS[:, :, :].rearrange("p b c -> p (b c)").bitcast(BF16).rearrange("p (b c) -> p b c", b=8)

        ident = sb("ident", [P, P], F32)
        identb = sb("identb", [P, P], BF16)
        iota1 = sb("iota1", [P, CW], F16)
        tri = sb("tri", [T, T], F16)
        ones = sb("ones", [T, T], F16)
        b_ahT = sb("b_ahT", [P, KT], F32)
        blT = sb("blT", [P, LAYERS * KT], F32)
        as8 = sb("as8", [T, HEADS_ALL * NT], F32)
        as2 = sb("as2", [T, HEADS_ALL * NT], F32)
        small = sb("small", [T, 64], F32)
        tokv = sb("tokv", [T, NT], F32)

        RING = 8
        DEPTH = 3
        tensors = {}

        def region(name, *sets, stack=ctx):
            width = {F32: 4, F32R: 4, I32: 4, U32: 4, F16: 2, BF16: 2, I16: 2}
            total = 0
            for tset in sets:
                inner, size = ExitStack(), 0
                for entry in tset:
                    if len(entry) == 2:
                        size += region(entry[0], *entry[1], stack=inner)
                        continue
                    tname, shape, dt = entry
                    tensors[tname] = alloc(inner)(tname, shape, dt)
                    n = width[dt]
                    for d_ in shape[1:]:
                        n *= d_
                    size += (n + 31) // 32 * 32
                inner.close()
                total = max(total, size)
            alloc(stack)(name, [P, total // 4], F32)
            return total

        WO_D = 8
        region("region_d",
               [("CT", [T, 3 * NT, CHUNK], I16)],
               [("Woh_d", [P, WO_D, D], F32R)],
               [("W1h0", [P, KT, 2 * HID], F32R), ("W1l0", [P, KT, 2 * HID], F32R)])
        CT = tensors["CT"]
        CTf = CT[:, :, :].rearrange("p a b -> p (a b)")
        region("region_a",
               [("x1T", [P, KT, N], F32), ("W0", [P, KT, D], F32), ("W1", [P, KT, D], F32)],
               [("emb", [T, NT, 2 * C], F32), ("embT", [P, 3, N], F32), ("hs1", [T, NT, CP], F32),
                ("uB1", [P, N], F32), ("vB1", [P, N], F32), ("tt2", [T, N], F32), ("ex2", [T, N], F32),
                ("pr2", [T, N], F32)],
               [("x2", [T, NT, D], F32), ("EBs", [P, 3, 3, T], F32), ("EBh", [P, 3, 3, T], F32R), ("EBl", [P, 3, 3, T], F32R),
                ("y0", [T, D], F32), ("y1", [T, D], F32), ("boB", [P, D], F32), ("xr0", [T, D], F32),
                ("yT0", [P, KT, T], F32), ("yT1", [P, KT, T], F32), ("zrow", [1, D // 2], F32)],
               [("x2_kept", [T, NT, D], F32), ("gg9", [T, TOPK, D], F32),
                ("sg0", [P, ROWS], F32), ("sg1", [P, ROWS], F32), ("actT", [P, 2, ROWS], F32),
                ("acth", [P, 2, ROWS], F32R), ("actl", [P, 2, ROWS], F32R)])
        region("region_b",
               [("X", [T, NT, D], F32), ("xnT", [P, KT, N], F32)],
               [("vB0", [P, N], F32),
                ("neg_or_w", ([("NEG", [T, NT, N], BF16)],
                              [("Wt", [P, KT, D], F32), ("cnt0", [T, 3, CHUNK], I16), ("cnt1", [T, 3, CHUNK], I16)])),
                ("asB0", [P, N], F32), ("asB1", [P, N], F32),
                ("junk0", [T, N], BF16), ("junk1", [T, N], BF16), ("maskb0", [T, N], BF16), ("maskb1", [T, N], BF16),
                ("Lr", [2 * HEADS_ALL, N], F32), ("UVr", [2 * HEADS, N], F32)],
               [("vB0_under_wout", [P, N], F32), ("Wo", [P, LAYERS * KT, D], F32)],
               [("vB0_under_low", [P, N], F32), ("Wol", [P, LAYERS * KT, D], F32R)],
               [("W1h1", [P, KT, 2 * HID], F32R), ("W1l1", [P, KT, 2 * HID], F32R), ("XgTh", [P, KT, ROWS + 1], F32R),
                ("XgTl", [P, KT, ROWS + 1], F32R), ("ye0", [T, D], F32), ("ye1", [T, D], F32),
                ("Xg0", [T, D], F32), ("Xg1", [T, D], F32), ("Xg2", [T, D], F32)],
               [(f"gg{t}", [T, TOPK, D], F32) for t in range(NT - 1)])
        hsbuf = sb("hsbuf", [T, 4, D // 2], F32)
        hsb = [hsbuf[:, i, :] for i in range(4)]
        mx_all = sb("mx_all", [T, NT, HEADS_ALL], F32)
        logitc = sb("logitc", [T, NT, 2 * HEADS_ALL], F32)
        UV = [sb(f"UV{i}", [T, NT, 2 * HEADS], F32) for i in range(2)]
        zz = sb("zz", [T, NT, HEADS], F32)
        region("region_c",
               [("aB", [P, 2, D], F32), ("wa", [P, KT, 2 * HEADS_ALL], F32), ("wjunk", [P, 2, C], F32),
                ("one_row", [T, ET], F16), ("local1", [T, ET], F32), ("other1", [T, ET], F32), ("slot1", [T, ET], F32),
                ("tile1", [T, ET], F32), ("cols", [T, 8, NT], F32), ("gbF", [1, NG], F32), ("gbI", [1, NG], I32),
                ("sorted", [P, 2 * ST], F32),
                ("sort_or_count",
                 ([("xn0", [T, D], F32), ("xn1", [T, D], F32), ("sumx", [T, NT], F32), ("nmean", [T, NT], F32),
                   ("sumsq", [T, NT], F32), ("ve", [T, NT], F32), ("mhalf", [T, NT], F32), ("rstd", [T, NT], F32),
                   ("sjunk", [T, D], BF16), ("srcI", [T, ET], I32), ("dstI", [T, ET], I32), ("key", [T, ET], F32),
                   ("bucket", [T, ET], F32), ("inb", [T, NT, ET], F16), ("cum", [T, NT, ET], F16),
                   ("tot16", [T, NT], F16), ("colsI", [T, 2, NT], I32), ("tmpj", [T, ET], F32), ("pos", [T, ET], F32),
                   ("posI", [T, 3, ET], I32)]
                  + [(f"pick{i}", [T, 2, P], F16) for i in range(RING)] + [(f"put{i}", [T, ST], F16) for i in range(RING)],
                  [(f"oh_src{i}", [P, T], F16) for i in range(2 * GROUP)]
                  + [(f"oh_dst{i}", [P, CW], F16) for i in range(2 * GROUP)]))],
               [("tt0", [T, N], F32), ("tt1", [T, N], F32), ("ex0", [T, N], F32), ("ex1", [T, N], F32),
                ("pr0", [T, N], F32), ("pr1", [T, N], F32), ("hs0", [T, NT, CP], F32), ("uB0", [P, N], F32),
                ("den", [T, NT], F32), ("rs", [T, NT], F32)],
               [("wout_or_expert",
                 ([("Woh_c", [P, LAYERS * KT - WO_D, D], F32R)],
                  [("W1s", [P, KT, 2 * HID], F32), ("W2s", [P, 2, D], F32), ("W2h", [P, 2, D], F32R),
                   ("W2l", [P, 2, D], F32R)])),
                ("WgS", [P, KT, EXPERTS], F32), ("st2", [T, 12], F32), ("mv2", [T, 4], F32),
                ("rstd2", [T, NT], F32), ("mh2", [T, 1], F32), ("lg", [T, NT, EXPERTS], F32), ("top", [T, NT, 8], F32),
                ("tidx", [T, NT, 8], U32), ("idxF", [T, NT, TOPK], F32), ("oh2", [T, NT, TOPK * EXPERTS], F16),
                ("ohp", [T, NT, TOPK * EXPERTS], F32), ("posk", [T, NT, TOPK], F32), ("keep", [T, NT, TOPK], F32),
                ("rk", [T, NT, TOPK], F32), ("rsub", [T, NT, TOPK], F32), ("rtile", [T, NT, TOPK], F32),
                ("rslot", [T, NT, TOPK], F32), ("tmpk", [T, NT, TOPK], F32), ("rowF", [T, NT, TOPK], F32),
                ("ohs", [T, TOPK * NT, T], F16), ("oht", [T, TOPK * NT, EXPERTS * RT], F16), ("edt", [T, NT], F32)])
        Wt, cnt = tensors["Wt"], [tensors["cnt0"], tensors["cnt1"]]
        x1T, xnT, X, NEG, Lr, Wo, emb, embT = (tensors[k] for k in ("x1T", "xnT", "X", "NEG", "Lr", "Wo", "emb", "embT"))
        W, asB, junk, maskb, hs, uB, vB, xn = (
            [tensors[f"{k}{i}"] for i in range(2)]
            for k in ("W", "asB", "junk", "maskb", "hs", "uB", "vB", "xn"))
        tt, ex, pr = ([tensors[f"{k}{i}"] for i in range(DEPTH)] for k in ("tt", "ex", "pr"))
        pick, put = ([tensors[f"{k}{i}"] for i in range(RING)] for k in ("pick", "put"))
        oh_src, oh_dst = ([tensors[f"{k}{i}"] for i in range(2 * GROUP)] for k in ("oh_src", "oh_dst"))
        (aB, wa, wjunk, sumx, nmean, sumsq, ve, mhalf, rstd, sjunk, srcI, dstI, key, other1, bucket, local1, inb, cum,
         one_row, tot16, cols, colsI, tmpj, pos, posI, slot1, tile1, gbF, gbI, sorted_, UVr, den, rs) = (
            tensors[k] for k in ("aB", "wa", "wjunk", "sumx", "nmean", "sumsq", "ve", "mhalf", "rstd", "sjunk", "srcI",
                                 "dstI", "key", "other1", "bucket", "local1", "inb", "cum", "one_row", "tot16", "cols",
                                 "colsI", "tmpj", "pos", "posI", "slot1", "tile1", "gbF", "gbI", "sorted", "UVr", "den",
                                 "rs"))

        rowI = sb("rowI", [T, NT * TOPK], I32)
        tokI = sb("tokI", [T, EXPERTS * RT], I32)
        wk = sb("wk", [T, NT, TOPK], F32)
        x2, boB, zrow, WgS, st2, mv2, rstd2, mh2, lg, top, tidx, idxF, oh2, ohp, posk, keep, rk, rsub, rtile = (
            tensors[k] for k in ("x2", "boB", "zrow", "WgS", "st2", "mv2", "rstd2", "mh2", "lg", "top", "tidx", "idxF",
                                 "oh2", "ohp", "posk", "keep", "rk", "rsub", "rtile"))
        rslot, tmpk, rowF, edt, actT = (tensors[k] for k in ("rslot", "tmpk", "rowF", "edt", "actT"))
        EBs, EBh, EBl, Wol = (tensors[k] for k in ("EBs", "EBh", "EBl", "Wol"))
        Woh = [tensors["Woh_d"][:, k, :] if k < WO_D else tensors["Woh_c"][:, k - WO_D, :] for k in range(LAYERS * KT)]
        ohs, oht = tensors["ohs"], tensors["oht"]
        y, yT, W1h, W1l, sg, ye = (
            [tensors[f"{k}{i}"] for i in range(2)] for k in ("y", "yT", "W1h", "W1l", "sg", "ye"))
        W1s, W2s, W2h, W2l, XgTh, XgTl, acth, actl = (
            tensors[k] for k in ("W1s", "W2s", "W2h", "W2l", "XgTh", "XgTl", "acth", "actl"))
        rr = hsb[0:2]
        xr = [tensors["xr0"][:, :], hsbuf[:, 2:4, :].rearrange("p a b -> p (a b)")]
        gg = [tensors[f"gg{t}"] for t in range(NT)]
        Xg = [tensors[f"Xg{i}"] for i in range(3)]

        def sems(name, n):
            return [sem(f"{name}{i}") for i in range(n)]

        s_x = sems("x_tile", NT)
        s_wah, s_small, s_edges, s_aB, s_lrd, s_uvd, s_wo, s_misc, s_zr, s_ed = (sem(n) for n in (
            "wah_loaded", "small_loaded", "edges_loaded", "a_rows_loaded", "logit_rows_written", "uv_rows_written",
            "wout_loaded", "stage6_small_loaded", "zero_row_written", "embT_written"))
        s_w, s_asB, s_hs, s_xr, s_yd, s_yed = (sems(n, 2) for n in (
            "w_loaded", "source_row_loaded", "head_loaded", "residual_loaded", "y_written", "expert_rows_written"))
        s_eb = sems("emb_chunk_loaded", 3)
        s_woh, s_wol, s_ebh, s_ebl, s_ec = (sem(n) for n in (
            "wout_high_parts", "wout_low_parts", "emb_high_parts", "emb_low_parts", "emb_chunk_used"))
        s_wt = sem("w2_for_logits_loaded")
        s_hd = sems("h_written", 4)
        s_xg, s_od = (sems(n, 3) for n in ("rows_gathered", "result_written"))
        s_g = sems("expert_rows_gathered", NT)
        s_c, s_ctz, s_ssq, s_rstd, s_xn, s_tp, s_tpe, s_x1, s_x1e = (sem(n) for n in (
            "constants", "counts_cleared", "squares_summed", "rstd_ready", "xn_ready", "xn_transposed", "xnT_stored",
            "x1_banks", "x1T_stored"))
        s_h, s_he, s_wj, s_wa, s_lr, s_lre, s_lc = (sem(n) for n in (
            "h_banks", "h_evacuated", "logit_weight_column", "wa_ready", "logit_row_banks", "logit_rows_stored",
            "logit_columns"))
        s_tot, s_pre, s_pick, s_perm, s_oh, s_ohu, s_ct = (sem(n) for n in (
            "bucket_totals", "bucket_prefixes", "permutation_ready", "permutation_used", "count_onehots_ready",
            "count_onehots_used", "counts_added"))
        s_cev = sem("group_counts_stored")
        s_mask, s_mt, s_neg, s_mx, s_uv, s_uvt, s_uvr = (sem(n) for n in (
            "mask_ready", "mask_transposed", "neg_stored", "neighbour_max", "uv_columns", "uv_transposed",
            "uv_rows_stored"))
        s_ones, s_tt, s_ex, s_p, s_pu, s_ob, s_den, s_rs, s_oe, s_tr, s_te = (sem(n) for n in (
            "ones_column", "exponent_ready", "exp_ready", "probs_ready", "probs_used", "head_banks_full",
            "row_sums_guarded", "row_sums_inverted", "head_tiles_stored", "emb_transposed", "embT_stored"))
        s_pj, s_pje, s_v2, s_r2, s_y, s_yt, s_yte, s_lg, s_oh2, s_cum, s_sm, s_sme, s_tk, s_tku, s_tok = (
            sem(n) for n in (
                "projection_banks", "projection_evacuated", "variance2_ready", "rstd2_ready", "y_ready", "y_transposed",
                "yT_stored", "gate_logits", "expert_onehots", "expert_counts", "gate_differences", "gate_exp",
                "token_onehots", "token_onehots_used", "token_table"))
        s_w1, s_w2, s_w1h, s_w1l, s_w2h, s_w2l, s_pad, s_xtl, s_am, s_ah, s_al = (sem(n) for n in (
            "expert_w1_loaded", "expert_w2_loaded", "w1_high_parts", "w1_low_parts", "w2_high_parts", "w2_low_parts",
            "pad_column", "rows_low_parts", "act_full", "act_high_parts", "act_low_parts"))
        s_xt, s_xth, s_h1, s_sg, s_yb, s_yee, s_fin = (sem(n) for n in (
            "rows_transposed", "rows_high_parts", "hidden_banks", "silu_ready",
            "expert_out_banks", "expert_out_stored", "result_ready"))
        s_dch, s_ach, s_gch = (sem(n) for n in ("vector_chain", "scalar_chain", "pool_chain"))

        HALF = D // 2
        HU = LAYERS * NT * 2
        COUNT_H = NG // 2
        H_FIRST = 1
        H_BEFORE_LOGITS = 0
        H_COUNTED = H_FIRST + COUNT_H
        UNITS = HEADS_ALL * NT
        ROUTED = NT - 2
        X_LAG = 4
        PERM_FROM, PERM = 2, 10
        M2_STEPS = 66
        M2 = HEADS * NT
        M2_BEFORE = 8
        UV2_STEP = M2_STEPS + 3
        PAIR_GROUPS = [(0, 4), (4, 8), (8, NT)]

        def row(ap):
            return ap.rearrange("(o n) -> o n", o=1)

        def half_tile(i):
            return i // (2 * NT), (i // 2) % NT, i % 2

        block = ctx.enter_context(nc.Block())

        @block.sync
        def _(sp):
            for t in range(NT):
                sp.dma_start(X[:, t, :], x[t * T:(t + 1) * T, :]).then_inc(s_x[t], 16)
            sp.dma_start(W[0][:, :, :], W_ah.rearrange("(k p) n -> p k n", p=P)).then_inc(s_wah, 16)
            sp.dma_start(b_ahT[:, :], b_ah.rearrange("(k p) -> p k", p=P)).then_inc(s_small, 16)
            for l in range(LAYERS):
                sp.dma_start(blT[:, l * KT:(l + 1) * KT],
                             bl[l].rearrange("(k p) -> p k", p=P)).then_inc(s_small, 16)
            for l in range(LAYERS):
                b = (l + 1) % 2
                if l >= 1:
                    sp.wait_ge(s_wa, l)
                for i, a in enumerate((a_src[l], a_dst[l])):
                    sp.dma_start(aB[:, i, :], row(a.rearrange("h c -> (h c)")).broadcast_to([P, D])).then_inc(s_aB, 16)
                if l == 1:
                    sp.wait_ge(s_x1, 3 * KT)
                if l == 2:
                    sp.wait_ge(s_h, 2 * NT)
                sp.dma_start(W[b][:, :, :], Wl[l].rearrange("(k p) n -> p k n", p=P)).then_inc(s_w[b], 16)
                if l == 1:
                    sp.dma_start(Wt[:, :, :], Wl[2].rearrange("(k p) n -> p k n", p=P)).then_inc(s_wt, 16)
            sp.wait_ge(s_lre, 3)
            sp.dma_start(logit_rows[:, :], Lr[:, :]).then_inc(s_lrd, 16)
            sp.wait_ge(s_lrd, 16)

            def load_row(j):
                l, h = divmod(j, HEADS)
                if j >= 2:
                    sp.wait_ge(s_mx, NT * (j - 1))
                r0 = l * 2 * HEADS + h
                sp.dma_start(asB[j % 2][:, :], logit_rows[r0:r0 + 1, :].broadcast_to([P, N])).then_inc(s_asB[j % 2], 16)

            def store_uv(l):
                sp.wait_ge(s_uvr, 3 * (l + 1))
                sp.dma_start(uv_rows[l * 2 * HEADS:(l + 1) * 2 * HEADS, :], UVr[:, :]).then_inc(s_uvd, 16)

            def load_head(head):
                l, h = divmod(head, HEADS)
                q = head % 2
                if head >= 2:
                    sp.wait_ge(s_pu, DEPTH + (head - 1) * NT)
                sp.wait_ge(s_uvd, 16 * (l + 1))
                sp.dma_start(hs[q][:, :, 0:C], h_dram[head].rearrange("(t p) c -> p t c", p=T)).then_inc(s_hs[q], 16)
                for k, buf in enumerate((uB, vB)):
                    r0 = l * 2 * HEADS + k * HEADS + h
                    sp.dma_start(buf[q][:, :], uv_rows[r0:r0 + 1, :].broadcast_to([P, N])).then_inc(s_hs[q], 16)

            def store_pair(pair):
                sp.wait_ge(s_te, 3 + 9 * pair + 9)
                sp.dma_start(emb_dram[pair * 3 * P:(pair + 1) * 3 * P, :].rearrange("(k p) n -> p k n", p=P),
                             embT[:, :, :]).then_inc(s_ed, 16)
            for j in range(HEADS + 3):
                load_row(j)
            store_uv(0)
            for q in range(4):
                sp.wait_ge(s_hd[q], 16 * (2 * NT // 4))
            load_head(0)
            for j in range(HEADS + 3, 2 * HEADS + 2):
                load_row(j)
            for q in range(4):
                sp.wait_ge(s_hd[q], 16 * (HU // 4))
            sp.wait_ge(s_h, HU)
            load_head(1)
            for head in range(2, HEADS_ALL):
                if head == 2:
                    store_uv(1)
                if head == 2 * HEADS:
                    store_uv(2)
                load_head(head)
                if head in (3, 5):
                    load_row(2 * HEADS + head // 2 + 1)
                if head % 2 == 0 and head >= 4:
                    store_pair(head // 2 - 2)
                if head == 2 * HEADS:
                    sp.wait_ge(s_uv, 3)
                    sp.dma_start(Wo[:, :, :], W_out.rearrange("(k p) n -> p k n", p=P)).then_inc(s_wo, 16)
            store_pair(PAIRS - 2)
            def load_chunk(n):
                t, pair = divmod(n, PAIRS)
                if n >= 3:
                    sp.wait_ge(s_ebl, n - 2)
                if n == PAIRS - 1:
                    sp.wait_ge(s_ed, 16 * PAIRS)
                sp.dma_start(EBs[:, n % 3, :, :], emb_dram.rearrange("(k p) n -> p k n", p=P)[
                    :, 3 * pair:3 * pair + 3, t * T:(t + 1) * T]).then_inc(s_eb[n % 3], 16)
            sp.wait_ge(s_ed, 16 * (PAIRS - 1))
            sp.wait_ge(s_pu, UNITS + DEPTH)
            for n in range(4):
                load_chunk(n)
            store_pair(PAIRS - 1)
            load_chunk(4)
            sp.dma_start(boB[:, :], row(b_out).broadcast_to([P, D])).then_inc(s_misc, 16)
            sp.dma_start(WgS[:, :, :], Wg.rearrange("(k p) e -> p k e", p=P)).then_inc(s_misc, 16)

            def load_expert(e):
                if e >= 1:
                    sp.wait_ge(s_w1l, KT * e)
                sp.dma_start(W1s[:, :, :], W1[e].rearrange("(k p) n -> p k n", p=P)).then_inc(s_w1, 16)
                if e >= 1:
                    sp.wait_ge(s_w2l, 2 * e)
                sp.dma_start(W2s[:, :, :], W2[e].rearrange("(k p) n -> p k n", p=P)).then_inc(s_w2, 16)
            for n in range(NT * PAIRS):
                t, pair = divmod(n, PAIRS)
                if n >= 5:
                    load_chunk(n)
                if pair == 0:
                    if t >= 2:
                        sp.wait_ge(s_pje, 2 * (t - 1))
                    sp.dma_start(xr[t % 2], x[t * T:(t + 1) * T, :]).then_inc(s_xr[t % 2], 16)
                if pair == PAIRS - 1 and t >= 1:
                    sp.wait_ge(s_y, t)
                    sp.dma_start(y_dram[(t - 1) * T:t * T, :], y[(t - 1) % 2][:, :]).then_inc(s_yd[(t - 1) % 2], 16)
            sp.wait_ge(s_zr, 1)
            for c in range(2):
                sp.dma_start(y_dram[N:N + 1, c * HALF:(c + 1) * HALF], zrow[:, :]).then_inc(s_zr, 16)
            sp.wait_ge(s_pj, 2 * NT)
            load_expert(0)
            sp.wait_ge(s_y, NT)
            sp.dma_start(y_dram[(NT - 1) * T:NT * T, :], y[(NT - 1) % 2][:, :]).then_inc(s_yd[(NT - 1) % 2], 16)
            for e in range(1, EXPERTS):
                load_expert(e)
            for t in range(NT):
                sp.wait_ge(s_fin, t + 1)
                sp.dma_start(out[t * T:(t + 1) * T, :], gg[t][:, 1, :]).then_inc(s_od[t % 3], 16)
            for q in range(3):
                sp.wait_ge(s_od[q], 16 * len(range(q, NT, 3)))

        @block.gpsimd
        def _(g):
            chain = [0]

            def link(ins):
                chain[0] += 1
                ins.then_inc(s_gch, 1)
                g.wait_ge(s_gch, chain[0])

            g.dma_start(srcI[:, :], src.rearrange("(p t) -> p t", p=T)).then_inc(s_edges, 16)
            g.dma_start(dstI[:, :], dst.rearrange("(p t) -> p t", p=T)).then_inc(s_edges, 16)
            link(g.memset(tri[:, :], 1.0))
            g.affine_select(out=tri[:, :], in_=tri[:, :], compare_op=ALU.is_gt, fill=0.0, base=0,
                            pattern=[[1, T]], channel_multiplier=-1).then_inc(s_c, 1)
            g.memset(ones[:, :], 1.0).then_inc(s_c, 1)
            link(g.memset(ident[:, :], 0.0))
            g.affine_select(out=ident[:, :], in_=ident[:, :], compare_op=ALU.not_equal, fill=1.0, base=0,
                            pattern=[[-1, P]], channel_multiplier=1).then_inc(s_c, 1)
            g.iota(iota1[:, :], [[1, CW]], base=1, channel_multiplier=0,
                   allow_small_or_imprecise_dtypes=True).then_inc(s_c, 1)
            link(g.memset(mhalf[:, :], -0.5))
            for t in range(NT):
                g.wait_ge(s_ssq, t + 1)
                link(g.tensor_scalar(ve[:, t:t + 1], sumsq[:, t:t + 1], 1.0 / D, LN_EPS, ALU.mult, ALU.add))
                g.tensor_tensor(rstd[:, t:t + 1], ve[:, t:t + 1], mhalf[:, 0:1], ALU.pow).then_inc(s_rstd, 1)
            g.iota(tokv[:, :], [[T, NT]], base=-N, channel_multiplier=1,
                   allow_small_or_imprecise_dtypes=True).then_inc(s_c, 1)
            g.memset(CTf, 0).then_inc(s_ctz, 1)
            g.wait_ge(s_zr, 1)
            link(g.memset(mh2[:, :], -0.5))
            for t in range(NT):
                g.wait_ge(s_v2, t + 1)
                g.tensor_tensor(rstd2[:, t:t + 1], mv2[:, 2:3], mh2[:, :], ALU.pow).then_inc(s_r2, 1)
            g.wait_ge(s_tok, 1)
            for q in range(2):
                g.wait_ge(s_yd[q], 16 * NT // 2)
            g.wait_ge(s_zr, 33)
            for u in range(EXPERTS * RT):
                if u >= RT:
                    g.wait_ge(s_xt, 2 * (u - RT + 1))
                g.indirect_dma_start(out=Xg[u % 3][:, :], out_offset=None, in_=y_dram[:, :],
                                     in_offset=bass.IndirectOffsetOnAxis(ap=tokI[:, u:u + 1], axis=0)
                                     ).then_inc(s_xg[u % 3], 16)
            for q in range(2):
                g.wait_ge(s_yed[q], 16 * EXPERTS * RT // 2)
            for t in range(NT):
                for k in range(TOPK):
                    g.indirect_dma_start(out=gg[t][:, k, :], out_offset=None, in_=ye_dram[:, :],
                                         in_offset=bass.IndirectOffsetOnAxis(
                                             ap=rowI[:, TOPK * t + k:TOPK * t + k + 1], axis=0)).then_inc(s_g[t], 16)

        @block.tensor
        def _(pe):
            pe.wait_ge(s_c, 4)
            def xn_transposes(t):
                pe.wait_ge(s_xn, t + 1)
                for half in range(2):
                    u = 2 * t + half
                    if u >= 4:
                        pe.wait_ge(s_tpe, u - 3)
                    for k in range(3):
                        mm = pe.transpose(PS[:, u % 4, k * T:(k + 1) * T],
                                          xn[t % 2][:, (3 * half + k) * P:(3 * half + k + 1) * P], ident[0:T, 0:T])
                    mm.then_inc(s_tp, 1)
            permuted, transposed = 0, 6
            for t in range(transposed):
                xn_transposes(t)
                if t == 1:
                    pe.wait_ge(s_tot, 1)
                    pe.matmul(PS[0:T, 5, 0:NT], tri[:, :], tot16[:, :], start=True, stop=True)
                    pe.matmul(PS[0:T, 5, 16:16 + NT], ones[:, :], tot16[:, :], start=True, stop=True).then_inc(s_pre, 1)
            pe.wait_ge(s_wah, 16)
            for c, (c0, cn) in enumerate(CHUNKS):
                pe.wait_ge(s_tpe, 2 * -(-(c0 + cn) // T))
                for m in range(KT):
                    u = KT * c + m
                    if u >= 2:
                        pe.wait_ge(s_x1e, u - 1)
                    for k in range(KT):
                        mm = pe.matmul(PS[:, 6 + u % 2, 0:cn], W[0][:, k, m * P:(m + 1) * P], xnT[:, k, c0:c0 + cn],
                                       start=(k == 0), stop=(k == KT - 1))
                        if k == KT - 1:
                            mm.then_inc(s_x1, 1)
                        if u < 3 and k % 2 and transposed < NT:
                            xn_transposes(transposed)
                            transposed += 1
                        while permuted < min(ET, PERM * (u - PERM_FROM) + -(-PERM * (k + 1) // KT)):
                            n = permuted
                            permuted += 1
                            pe.wait_ge(s_pick, n + 1)
                            for i in range(2):
                                mp = pe.matmul(PS[:, 4 + i, 0:ST], pick[n % RING][:, i, :], put[n % RING][:, :],
                                               start=(n == 0), stop=(n == ET - 1))
                            mp.then_inc(s_perm, 1)
            def h_half(i, ks=range(KT)):
                l, t, c = half_tile(i)
                b = (l + 1) % 2
                if t == 0 and c == 0:
                    pe.wait_ge(s_w[b], 16 * (l // 2 + 1))
                if i >= 2 and 0 in ks:
                    pe.wait_ge(s_he, i - 1)
                for k in ks:
                    mm = pe.matmul(PS[0:T, 6 + i % 2, 0:HALF], x1T[:, k, t * T:(t + 1) * T],
                                   W[b][:, k, c * HALF:(c + 1) * HALF], start=(k == 0), stop=(k == KT - 1))
                    if k == KT - 1:
                        mm.then_inc(s_h, 1)
            pe.wait_ge(s_x1e, 3 * KT)
            for i in range(H_FIRST):
                h_half(i)
            for i in range(COUNT_H):
                for g in (2 * i, 2 * i + 1):
                    if g >= 2:
                        pe.wait_ge(s_cev, g - 1)
                    for q in range(GROUP):
                        b = g % 2 * GROUP + q
                        h_half(H_FIRST + i, range(b, min(b + 1, KT)))
                        pe.wait_ge(s_oh, g * GROUP + q + 1)
                        for c in range(3):
                            mm = pe.matmul(PS[0:T, 3 * (g % 2) + c, 0:CHUNK], oh_src[b][:, :],
                                           oh_dst[b][:, c * CHUNK:(c + 1) * CHUNK], start=(q == 0), stop=(q == GROUP - 1))
                        mm.then_inc(s_ohu, 1)
            for i in range(H_COUNTED, H_COUNTED + H_BEFORE_LOGITS):
                h_half(i)

            def mask_transposes(s):
                pe.wait_ge(s_mask, s + 1)
                for half in range(2):
                    u = 2 * s + half
                    if u >= 2:
                        pe.wait_ge(s_neg, u - 1)
                    for k in range(5):
                        mm = pe.transpose(PSB[0:T, 4 + half, k * 126:k * 126 + T],
                                          maskb[s % 2][:, (5 * half + k) * T:(5 * half + k + 1) * T], identb[0:T, 0:T])
                    mm.then_inc(s_mt, 1)
            pe.wait_ge(s_cev, NG)
            pe.wait_ge(s_wa, LAYERS)
            masked = 0
            for c, (c0, cn) in enumerate(CHUNKS):
                for k in range(KT):
                    mm = pe.matmul(PS[0:2 * HEADS_ALL, c, 0:cn], wa[:, k, :], x1T[:, k, c0:c0 + cn],
                                   start=(k == 0), stop=(k == KT - 1))
                    if k == KT - 1:
                        mm.then_inc(s_lr, 1)
                    if k % 2:
                        mask_transposes(masked)
                        masked += 1
            for s in range(masked, NT):
                mask_transposes(s)
            pe.wait_ge(s_lre, 3)
            for t in range(NT):
                mm = pe.transpose(PS[0:T, 3, t * 24:(t + 1) * 24], Lr[:, t * T:(t + 1) * T],
                                  ident[0:2 * HEADS_ALL, 0:2 * HEADS_ALL])
            mm.then_inc(s_lc, 1)
            i = H_COUNTED + H_BEFORE_LOGITS

            def uv_transposes(l, b0):
                pe.wait_ge(s_uv, l + 1)
                for q, (t0, t1) in enumerate(PAIR_GROUPS):
                    for t in range(t0, t1):
                        mm = pe.transpose(PS[0:2 * HEADS, b0 + q, (t - t0) * T:(t - t0 + 1) * T], UV[l % 2][:, t, :],
                                          ident[0:T, 0:T])
                    mm.then_inc(s_uvt, 1)
            while i < 3 * HU // 4 + 3:
                h_half(i)
                i += 1
            uv_transposes(0, 0)
            while i < HU:
                h_half(i)
                i += 1
            pe.wait_ge(s_uvr, 3)

            def pair_transposes(pair, k):
                pe.wait_ge(s_oe, (2 * pair + 2) * NT)
                for q, (t0, t1) in enumerate(PAIR_GROUPS):
                    pe.wait_ge(s_te, 9 * pair + 3 * k + q + 1)
                    for t in range(t0, t1):
                        mm = pe.transpose(PS[:, 5 + q, (t - t0) * T:(t - t0 + 1) * T], emb[:, t, k * P:(k + 1) * P],
                                          ident[0:T, 0:T])
                    mm.then_inc(s_tr, 1)
            pe.sem_inc(s_pu, DEPTH)
            for u in range(UNITS):
                head, st = divmod(u, NT)
                if st == 0:
                    pe.wait_ge(s_hs[head % 2], 48 * (head // 2 + 1))
                    pe.wait_ge(s_ones, head % 2 + 1)
                pe.wait_ge(s_p, u + 1)
                for dt in range(NT):
                    b, r = divmod(dt, 2)
                    if st == 0 and r == 0 and head > 0:
                        pe.wait_ge(s_oe, (head - 1) * NT + 2 * (b + 1))
                    mm = pe.matmul(PS[0:T, b, r * 256:r * 256 + CP], pr[u % DEPTH][:, dt * T:(dt + 1) * T],
                                   hs[head % 2][:, st, :], start=(st == 0 and r == 0), stop=(st == NT - 1),
                                   skip_group_check=True)
                    if st == NT - 1 and r == 1 and b < 4:
                        mm.then_inc(s_ob, 1)
                mm.then_inc(s_pu, 1)
                if u == 0:
                    pe.wait_ge(s_he, HU)
                    uv_transposes(1, 5)
                if head == 2 and st == 3:
                    pe.wait_ge(s_uvr, 6)
                if head % 2 == 0 and head >= 2 and 3 <= st < 6:
                    pair_transposes(head // 2 - 1, st - 3)
                if u == UV2_STEP:
                    pe.wait_ge(s_te, 9 * (head // 2) + 3)
                    uv_transposes(2, 5)
            for k in range(3):
                pair_transposes(PAIRS - 1, k)
            def gate_transposes(t):
                pe.wait_ge(s_y, t + 1)
                for half in range(2):
                    if t >= 1:
                        pe.wait_ge(s_yte, 2 * (t - 1) + half + 1)
                    for k in range(3):
                        mm = pe.transpose(PS[:, 4 + half, k * T:(k + 1) * T],
                                          y[t % 2][:, (3 * half + k) * P:(3 * half + k + 1) * P], ident[0:T, 0:T])
                    mm.then_inc(s_yt, 1)

            def gate_logits(t):
                pe.wait_ge(s_misc, 32)
                pe.wait_ge(s_yte, 2 * t + 2)
                if t >= 2:
                    pe.wait_ge(s_oh2, t - 1)
                for k in range(KT):
                    mm = pe.matmul(PS[0:T, 6 + t % 2, 0:EXPERTS], yT[t % 2][:, k, :], WgS[:, k, :],
                                   start=(k == 0), stop=(k == KT - 1))
                mm.then_inc(s_lg, 1)

            def expert_counts(t0, t1, q0, q1):
                pe.wait_ge(s_oh2, min(t1, q1))
                for t in range(t0, t1):
                    for q in range(q0, min(t, q1)):
                        pe.matmul(PS[0:T, 0, t * 16:(t + 1) * 16], ones[:, :], oh2[:, q, :],
                                  start=(q == 0 and (t < ROUTED or t == t0)), stop=False,
                                  skip_group_check=True)
                    if t < q1:
                        mm = pe.matmul(PS[0:T, 0, t * 16:(t + 1) * 16], tri[:, :], oh2[:, t, :], start=(t == 0), stop=True,
                                       skip_group_check=True)
                        if t == q1 - 1:
                            mm.then_inc(s_cum, 1)

            def token_table(t0, t1):
                for u in range(TOPK * t0, TOPK * t1):
                    pe.wait_ge(s_tk, u + 1)
                    mm = pe.matmul(PS[0:T, 1, 0:EXPERTS * RT], ohs[:, u, :], oht[:, u, :], start=(u == 0),
                                   stop=(u == TOPK * NT - 1))
                mm.then_inc(s_tku, 1)
            for n in range(NT * PAIRS):
                t, pair = divmod(n, PAIRS)
                if pair == 0 and t >= 2:
                    pe.wait_ge(s_pje, 2 * (t - 1))
                pe.wait_ge(s_ebl, n + 1)
                for q in range(3):
                    k = 3 * pair + q
                    if t == 0:
                        pe.wait_ge(s_wol, k + 1)
                    h, l = EBh[:, n % 3, q, :], EBl[:, n % 3, q, :]
                    for stationary, moving in ((h, Woh[k]), (h, Wol[:, k, :]), (l, Woh[k])):
                        for c in range(2):
                            last = k == LAYERS * KT - 1 and stationary is l
                            mm = pe.matmul(PS[0:T, 2 * (t % 2) + c, 0:HALF], stationary, moving[:, c * HALF:(c + 1) * HALF],
                                           start=(k == 0 and moving is Woh[k] and stationary is h), stop=last)
                            if last:
                                mm.then_inc(s_pj, 1)
                if k < LAYERS * KT - 1:
                    mm.then_inc(s_ec, 1)
                if pair == 3 and t == NT - 1:
                    pe.wait_ge(s_pje, 2 * (NT - 1))
                    expert_counts(0, ROUTED, 0, ROUTED)
                if pair == 4 and t >= 1:
                    gate_transposes(t - 1)
                if pair == 5 and t >= 1:
                    gate_logits(t - 1)
            token_table(0, ROUTED)
            expert_counts(ROUTED, NT, 0, ROUTED)
            gate_transposes(NT - 1)
            gate_logits(NT - 1)
            expert_counts(ROUTED, NT, ROUTED, NT)
            token_table(ROUTED, NT)

            def row_transposes(v):
                u, half = divmod(v, 2)
                if half == 0:
                    pe.wait_ge(s_xg[u % 3], 16 * (u // 3 + 1))
                if v >= 2:
                    pe.wait_ge(s_xtl, v - 1)
                for k in range(3):
                    mm = pe.transpose(PS[:, half, k * T:(k + 1) * T],
                                      Xg[u % 3][:, (3 * half + k) * P:(3 * half + k + 1) * P], ident[0:T, 0:T])
                mm.then_inc(s_xt, 1)

            def split_product(out_, wh, wl, xh, xl, first, last):
                pe.matmul(out_, wh, xh, start=first, stop=False)
                pe.matmul(out_, wh, xl, start=False, stop=False)
                return pe.matmul(out_, wl, xh, start=False, stop=last)
            for v in range(2 * RT):
                row_transposes(v)
            for e in range(EXPERTS):
                pe.wait_ge(s_xtl, 2 * RT * (e + 1))
                for n, m in enumerate((2, 3, 0, 1)):
                    for k in range(KT):
                        if n == 0:
                            pe.wait_ge(s_w1l, KT * e + k + 1)
                        if k == 0 and e >= 1:
                            pe.wait_ge(s_sg if n < 2 else s_am, 2 * (e - 1) + n % 2 + 1)
                        f = slice(m * P, (m + 1) * P)
                        mm = split_product(PS[:, 2 + m, 0:ROWS + 1], W1h[e % 2][:, k, f], W1l[e % 2][:, k, f],
                                           XgTh[:, k, :], XgTl[:, k, :], k == 0, k == KT - 1)
                    mm.then_inc(s_h1, 1)
                if e + 1 < EXPERTS:
                    for v in range(2):
                        row_transposes(2 * RT * (e + 1) + v)
                pe.wait_ge(s_w2l, 2 * (e + 1))
                pe.wait_ge(s_al, 2 * (e + 1))
                for j in range(RT):
                    u = e * RT + j
                    for c in range(2):
                        if u >= 1:
                            pe.wait_ge(s_yee, 2 * (u - 1) + c + 1)
                        f, r = slice(c * HALF, (c + 1) * HALF), slice(j * T, (j + 1) * T)
                        for k in range(2):
                            mm = split_product(PS[0:T, 6 + c, 0:HALF], acth[:, k, r], actl[:, k, r], W2h[:, k, f],
                                               W2l[:, k, f], k == 0, k == 1)
                        mm.then_inc(s_yb, 1)
                        if e + 1 < EXPERTS and 2 * j + c < 2 * RT - 2:
                            row_transposes(2 * RT * (e + 1) + 2 * j + c + 2)

        @block.scalar
        def _(act):
            chain = [0]

            def link(ins):
                chain[0] += 1
                ins.then_inc(s_ach, 1)
                act.wait_ge(s_ach, chain[0])

            def xn_store(t):
                for half in range(2):
                    u = 2 * t + half
                    act.wait_ge(s_tp, u + 1)
                    act.activation(xnT[:, 3 * half:3 * half + 3, t * T:(t + 1) * T],
                                   PS[:, u % 4, 0:3 * T].rearrange("p (k n) -> p k n", k=3), ACT.Copy).then_inc(s_tpe, 1)

            for t in range(NT):
                if t >= X_LAG:
                    xn_store(t - X_LAG)
                act.wait_ge(s_x[t], 16)
                link(act.activation(sjunk[:, :], X[:, t, :], ACT.Copy, accum_out=sumx[:, t:t + 1]))
                link(act.activation(nmean[:, t:t + 1], sumx[:, t:t + 1], ACT.Copy, scale=-1.0 / D))
                act.activation(sjunk[:, :], X[:, t, :], ACT.Square, bias=nmean[:, t:t + 1],
                               accum_out=sumsq[:, t:t + 1]).then_inc(s_ssq, 1)
                act.wait_ge(s_ssq, t + 1)
            for t in range(NT - X_LAG, NT):
                xn_store(t)
            act.wait_ge(s_small, 64)
            for c, (c0, cn) in enumerate(CHUNKS):
                for m in range(KT):
                    u = KT * c + m
                    act.wait_ge(s_x1, u + 1)
                    act.activation(x1T[:, m, c0:c0 + cn], PS[:, 6 + u % 2, 0:cn], ACT.Relu,
                                   bias=b_ahT[:, m:m + 1]).then_inc(s_x1e, 1)

            def h_store(i):
                l, t, c = half_tile(i)
                act.wait_ge(s_h, i + 1)
                if i >= 4:
                    act.wait_ge(s_hd[i % 4], 16 * (i // 4))
                act.activation(hsb[i % 4], PS[0:T, 6 + i % 2, 0:HALF], ACT.Copy).then_inc(s_he, 1)
                act.wait_ge(s_he, i + 1)
                q0 = l * HEADS + c * HEADS // 2
                act.dma_start(h_dram[q0:q0 + HEADS // 2, t * T:(t + 1) * T, :].rearrange("q p c -> p q c"),
                              hsb[i % 4].rearrange("p (q c) -> p q c", q=HEADS // 2)).then_inc(s_hd[i % 4], 16)

            def count_store(g):
                act.wait_ge(s_ohu, (g + 3) * GROUP)
                if g >= 2:
                    act.wait_ge(s_ct, g)
                act.activation(cnt[g % 2][:, :, :], PS[0:T, 3 * (g % 2):3 * (g % 2) + 3, 0:CHUNK],
                               ACT.Copy).then_inc(s_cev, 1)

            def uv_store(l, b0):
                if l >= 1:
                    act.wait_ge(s_uvd, 16 * l)
                for q, (t0, t1) in enumerate(PAIR_GROUPS):
                    act.wait_ge(s_uvt, 3 * l + q + 1)
                    act.activation(UVr[:, t0 * T:t1 * T], PS[0:2 * HEADS, b0 + q, 0:(t1 - t0) * T],
                                   ACT.Copy).then_inc(s_uvr, 1)
            for i in range(H_FIRST):
                h_store(i)
            for i in range(COUNT_H):
                count_store(2 * i)
                h_store(H_FIRST + i)
                count_store(2 * i + 1)
            for i in range(H_COUNTED, H_COUNTED + H_BEFORE_LOGITS):
                h_store(i)
            for c, (c0, cn) in enumerate(CHUNKS):
                act.wait_ge(s_lr, c + 1)
                act.activation(Lr[:, c0:c0 + cn], PS[0:2 * HEADS_ALL, c, 0:cn], ACT.Copy).then_inc(s_lre, 1)
            for i in range(H_COUNTED + H_BEFORE_LOGITS, 3 * HU // 4 + 3):
                h_store(i)
            uv_store(0, 0)
            for i in range(3 * HU // 4 + 3, HU - 3):
                h_store(i)

            def exponential(u):
                act.wait_ge(s_tt, u + 1)
                if u >= DEPTH:
                    act.wait_ge(s_p, u - DEPTH + 1)
                act.activation(ex[u % DEPTH][:, :], tt[u % DEPTH][:, :], ACT.Exp, bias=as2[:, u:u + 1]).then_inc(s_ex, 1)
            exponential(0)
            for i in range(HU - 3, HU):
                h_store(i)

            def head_store(head):
                for dt in range(NT):
                    b, r = divmod(dt, 2)
                    if r == 0:
                        act.wait_ge(s_rs, head * 5 + b + 1)
                    if dt == 0 and head % 2 == 0 and head >= 2:
                        act.wait_ge(s_tr, 9 * (head // 2))
                    if dt == 0 and head == 0:
                        act.wait_ge(s_pu, DEPTH + NT)
                    act.activation(emb[:, dt, (head % 2) * C:(head % 2 + 1) * C], PS[0:T, b, r * 256:r * 256 + C],
                                   ACT.Copy, scale=rs[:, dt:dt + 1]).then_inc(s_oe, 1)

            def pair_store(pair, k):
                if k == 0 and pair >= 1:
                    act.wait_ge(s_ed, 16 * pair)
                for q, (t0, t1) in enumerate(PAIR_GROUPS):
                    act.wait_ge(s_tr, 9 * pair + 3 * k + q + 1)
                    act.activation(embT[:, k, t0 * T:t1 * T], PS[:, 5 + q, 0:(t1 - t0) * T], ACT.Relu,
                                   bias=blT[:, pair * 3 + k:pair * 3 + k + 1]).then_inc(s_te, 1)
            act.sem_inc(s_te, 3)
            for u in range(UNITS):
                head, st = divmod(u, NT)
                if u >= 1:
                    exponential(u)
                if st == 1 and head >= 1:
                    head_store(head - 1)
                if head % 2 == 0 and head >= 2 and 5 <= st < 8:
                    pair_store(head // 2 - 1, st - 5)
                if u == 1:
                    uv_store(1, 5)
                if u == UV2_STEP + 1:
                    uv_store(2, 5)
            head_store(HEADS_ALL - 1)

            def wout_high(k):
                if k == 0:
                    act.wait_ge(s_wo, 16)
                    act.wait_ge(s_pu, UNITS + DEPTH)
                act.activation(Woh[k], Wo[:, k, :], ACT.Copy).then_inc(s_woh, 1)

            def emb_high(n):
                act.wait_ge(s_eb[n % 3], 16 * (n // 3 + 1))
                if n >= 3:
                    t, pair = divmod(n - 3, PAIRS)
                    if pair == PAIRS - 1:
                        act.wait_ge(s_pj, 2 * (t + 1))
                    else:
                        act.wait_ge(s_ec, (PAIRS - 1) * t + pair + 1)
                act.activation(EBh[:, n % 3, :, :], EBs[:, n % 3, :, :], ACT.Copy).then_inc(s_ebh, 1)

            for k in range(3):
                wout_high(k)
                if k == 2:
                    emb_high(0)
                pair_store(PAIRS - 1, k)
            def w1_high(e):
                act.wait_ge(s_w1, 16 * (e + 1))
                if e >= 2:
                    act.wait_ge(s_h1, 4 * (e - 1))
                if e == 1:
                    act.wait_ge(s_pj, 2 * NT)
                for k in range(KT):
                    act.activation(W1h[e % 2][:, k, :], W1s[:, k, :], ACT.Copy).then_inc(s_w1h, 1)

            def y_store(t):
                for half in range(2):
                    act.wait_ge(s_yt, 2 * t + half + 1)
                    if t >= 2 and half == 0:
                        act.wait_ge(s_lg, t - 1)
                    act.activation(yT[t % 2][:, 3 * half:3 * half + 3, :],
                                   PS[:, 4 + half, 0:3 * T].rearrange("p (k n) -> p k n", k=3), ACT.Copy).then_inc(s_yte, 1)
            for n in range(NT * PAIRS):
                if n >= 1:
                    emb_high(n)
                if 1 <= n < PAIRS:
                    for k in range(3 * n, 3 * n + 3):
                        wout_high(k)
                if n % PAIRS == 1 and n > 2 * PAIRS:
                    y_store(n // PAIRS - 2)
            y_store(NT - 2)
            y_store(NT - 1)
            act.wait_ge(s_sm, 1)
            act.activation(edt[:, :], small[:, 0:NT], ACT.Exp).then_inc(s_sme, 1)
            w1_high(0)

            def rows_high(v):
                u, half = divmod(v, 2)
                j = u % RT
                act.wait_ge(s_xt, v + 1)
                act.activation(XgTh[:, 3 * half:3 * half + 3, j * T:(j + 1) * T],
                               PS[:, half, 0:3 * T].rearrange("p (k n) -> p k n", k=3), ACT.Copy).then_inc(s_xth, 1)

            for part in (XgTh, XgTl):
                act.activation(part[:, :, ROWS:ROWS + 1], ident[:, 0:KT].rearrange("p (k o) -> p k o", o=1),
                               ACT.Copy).then_inc(s_pad, 1)
            for v in range(2 * RT):
                rows_high(v)
            for e in range(EXPERTS):
                act.wait_ge(s_w2, 16 * (e + 1))
                if e >= 1:
                    act.wait_ge(s_yb, 2 * RT * e)
                for k in range(2):
                    act.activation(W2h[:, k, :], W2s[:, k, :], ACT.Copy).then_inc(s_w2h, 1)
                if e + 1 < EXPERTS:
                    w1_high(e + 1)
                for m in range(2):
                    act.wait_ge(s_h1, 4 * e + m + 1)
                    if e >= 1:
                        act.wait_ge(s_am, 2 * (e - 1) + m + 1)
                    act.activation(sg[m][:, :], PS[:, 4 + m, 0:ROWS], ACT.Silu).then_inc(s_sg, 1)
                for m in range(2):
                    act.wait_ge(s_am, 2 * e + m + 1)
                    act.activation(acth[:, m, :], actT[:, m, :], ACT.Copy).then_inc(s_ah, 1)
                if e + 1 < EXPERTS:
                    for v in range(2):
                        rows_high(2 * RT * (e + 1) + v)
                for j in range(RT):
                    u = e * RT + j
                    for c in range(2):
                        act.wait_ge(s_yb, 2 * u + c + 1)
                        if u >= 2 and c == 0:
                            act.wait_ge(s_yed[u % 2], 16 * (u // 2))
                        act.activation(ye[u % 2][:, c * HALF:(c + 1) * HALF], PS[0:T, 6 + c, 0:HALF],
                                       ACT.Copy).then_inc(s_yee, 1)
                        if e + 1 < EXPERTS and 2 * j + c < 2 * RT - 2:
                            rows_high(2 * RT * (e + 1) + 2 * j + c + 2)
                    act.wait_ge(s_yee, 2 * u + 2)
                    act.dma_start(ye_dram[u * T:(u + 1) * T, :], ye[u % 2][:, :]).then_inc(s_yed[u % 2], 16)

        @block.vector
        def _(v):
            chain = [0]

            def link(ins):
                chain[0] += 1
                ins.then_inc(s_dch, 1)
                v.wait_ge(s_dch, chain[0])

            def normalise(t):
                v.wait_ge(s_rstd, t + 1)
                if t >= 2:
                    v.wait_ge(s_tp, 2 * (t - 1))
                v.tensor_scalar(xn[t % 2][:, :], X[:, t, :], nmean[:, t:t + 1], rstd[:, t:t + 1], ALU.add,
                                ALU.mult).then_inc(s_xn, 1)
            link(v.memset(one_row[:, :], 1.0))
            v.wait_ge(s_edges, 32)
            link(v.tensor_copy(key[:, :], srcI[:, :]))
            link(v.tensor_scalar(other1[:, :], dstI[:, :], 1.0, None, ALU.add))
            link(v.tensor_scalar(bucket[:, :], key[:, :], float(T), None, ALU.is_ge))
            for j in range(2, NT):
                link(v.scalar_tensor_tensor(out=bucket[:, :], in0=key[:, :], scalar=float(T * j), in1=bucket[:, :],
                                            op0=ALU.is_ge, op1=ALU.add))
            normalise(0)
            link(v.scalar_tensor_tensor(out=local1[:, :], in0=bucket[:, :], scalar=-float(T), in1=key[:, :],
                                        op0=ALU.mult, op1=ALU.add))
            link(v.tensor_scalar(local1[:, :], local1[:, :], 1.0, None, ALU.add))
            for j in range(NT):
                ins = v.tensor_scalar(inb[:, j, :], bucket[:, :], float(j), None, ALU.is_equal)
            link(ins)
            normalise(1)
            for j in range(NT):
                ins = v.tensor_tensor_scan(cum[:, j, :], one_row[:, :], inb[:, j, :], 0.0, ALU.mult, ALU.add)
            link(ins)
            v.tensor_copy(tot16[:, :], cum[:, :, ET - 1]).then_inc(s_tot, 1)
            normalise(2)
            v.wait_ge(s_pre, 1)
            link(v.tensor_scalar(colsI[:, 0, :], PS[0:T, 5, 16:16 + NT], float(SLOTS - 1), None, ALU.add))
            link(v.tensor_scalar(colsI[:, 1, :], colsI[:, 0, :], SLOTS.bit_length() - 1, None, ALU.arith_shift_right))
            link(v.tensor_copy(cols[:, 0, :], colsI[:, 1, :]))
            link(v.tensor_tensor_scan(cols[:, 1, :], one_row[:, 0:NT], cols[:, 0, :], 0.0, ALU.mult, ALU.add))
            link(v.tensor_tensor(cols[:, 2, :], cols[:, 1, :], cols[:, 0, :], ALU.subtract))
            link(v.scalar_tensor_tensor(out=cols[:, 3, :], in0=cols[:, 2, :], scalar=float(SLOTS), in1=PS[0:T, 5, 0:NT],
                                        op0=ALU.mult, op1=ALU.add))
            link(v.tensor_scalar(cols[:, 4, :], cols[:, 3, :], -1.0, None, ALU.add))

            for j in range(NT):
                dstt = pos if j == 0 else tmpj
                link(v.scalar_tensor_tensor(out=dstt[:, :], in0=cum[:, j, :], scalar=cols[:, 4, j:j + 1], in1=inb[:, j, :],
                                            op0=ALU.add, op1=ALU.mult))
                if j:
                    link(v.tensor_tensor(pos[:, :], pos[:, :], tmpj[:, :], ALU.add))
                if j + 3 < NT:
                    normalise(j + 3)
            link(v.tensor_copy(posI[:, 0, :], pos[:, :]))
            link(v.tensor_scalar(posI[:, 1, :], posI[:, 0, :], P - 1, None, ALU.bitwise_and))
            link(v.tensor_scalar(posI[:, 2, :], posI[:, 0, :], P.bit_length() - 1, None, ALU.arith_shift_right))
            link(v.tensor_scalar(slot1[:, :], posI[:, 1, :], 1.0, None, ALU.add))
            link(v.tensor_scalar(tile1[:, :], posI[:, 2, :], 1.0, None, ALU.add))

            def place(q, t, free=None):
                if free is not None:
                    v.wait_ge(s_perm, free)
                for i, end in enumerate((local1, other1)):
                    v.tensor_scalar(pick[q][:, i, :], iota1[0:T, 0:P], slot1[:, ds(t, 1)], end[:, ds(t, 1)],
                                    ALU.is_equal, ALU.mult)
                v.tensor_scalar(put[q][:, :], iota1[0:T, 0:ST], tile1[:, ds(t, 1)], None,
                                ALU.is_equal).then_inc(s_pick, 1)
            v.wait_ge(s_c, 4)
            for q in range(RING):
                place(q, q)
            with v.Fori(1, ET // RING) as i:
                for q in range(RING):
                    place(q, i * RING + q, i * RING + q - RING + 1)
            link(v.tensor_copy(identb[:, :], ident[:, :]))
            link(v.tensor_scalar(gbF[:, :], iota1[0:1, 0:NG], cols[0:1, 2, 1:2], None, ALU.is_gt))
            for j in range(2, NT):
                link(v.scalar_tensor_tensor(out=gbF[:, :], in0=iota1[0:1, 0:NG], scalar=cols[0:1, 2, j:j + 1],
                                            in1=gbF[:, :], op0=ALU.is_gt, op1=ALU.add))
            link(v.tensor_scalar(gbI[:, :], gbF[:, :], 3.0, None, ALU.mult))
            v.wait_ge(s_perm, ET)
            link(v.tensor_copy(sorted_[:, :].rearrange("p (i n) -> p i n", i=2), PS[:, 4:6, 0:ST]))

            wcols = [0]

            def logit_weights(l, k, sd):
                Wk = Wt if l == 2 else W[(l + 1) % 2]
                if k == 0 and sd == 0:
                    v.wait_ge(s_wt if l == 2 else s_w[(l + 1) % 2], 16)
                    v.wait_ge(s_aB, 32 * (l + 1))
                for h in range(HEADS):
                    col = l * 2 * HEADS + sd * HEADS + h
                    v.tensor_tensor_reduce(wjunk[:, h % 2, :], Wk[:, k, h * C:(h + 1) * C], aB[:, sd, h * C:(h + 1) * C],
                                           1.0, 0.0, ALU.mult, ALU.add, wa[:, k, col:col + 1]).then_inc(s_wj, 1)
                    wcols[0] += 1
                    if wcols[0] >= 2:
                        v.wait_ge(s_wj, wcols[0] - 1)
                if k == KT - 1 and sd == 1:
                    v.wait_ge(s_wj, wcols[0])
                    v.sem_inc(s_wa, 1)

            def onehots(par, n):
                for q in range(GROUP):
                    col = n * GROUP + q
                    b = par * GROUP + q
                    v.wait_ge(s_ohu, col + 1)
                    v.tensor_scalar(oh_src[b][:, :], iota1[:, 0:T], sorted_[:, ds(col, 1)], None, ALU.is_equal)
                    v.tensor_scalar(oh_dst[b][:, :], iota1[:, :], sorted_[:, ds(col + ST, 1)], None,
                                    ALU.is_equal).then_inc(s_oh, 1)

            def add_counts(par, n):
                r = v.value_load(gbI[0:1, ds(n, 1)], min_val=0, max_val=3 * (NT - 1))
                v.wait_ge(s_cev, n + 1)
                v.wait_ge(s_ct, n + 1)
                v.tensor_tensor(CT[:, ds(r, 3), :], cnt[par][:, :, :], CT[:, ds(r, 3), :], ALU.add).then_inc(s_ct, 1)
            v.wait_ge(s_ctz, 1)
            v.sem_inc(s_ohu, 2 * GROUP)
            v.sem_inc(s_ct, 1)
            onehots(0, 0)
            pending = [(l, k, sd) for l in range(LAYERS) for k in range(KT) for sd in range(2)]
            for seg in range(NG // 4):
                with v.Fori(seg * 2, seg * 2 + 2) as i:
                    onehots(1, i * 2 + 1)
                    add_counts(0, i * 2)
                    onehots(0, i * 2 + 2)
                    add_counts(1, i * 2 + 1)
                while len(pending) > 2 * LAYERS * KT * (NG // 4 - 1 - seg) // (NG // 4):
                    logit_weights(*pending.pop(0))
            onehots(1, NG - 1)
            add_counts(0, NG - 2)
            add_counts(1, NG - 1)
            v.wait_ge(s_ct, NG + 1)
            for t in range(NT):
                c0 = t * CW + t * T
                v.tensor_tensor(CTf[:, c0:c0 + T], CTf[:, c0:c0 + T], ident[0:T, 0:T], ALU.add).then_inc(s_ct, 1)
            v.wait_ge(s_ct, NG + 1 + NT)
            for s in range(NT + 1):
                if s < NT:
                    if s >= 2:
                        v.wait_ge(s_mt, 2 * (s - 1))
                    v.tensor_scalar(maskb[s % 2][:, :], CTf[:, s * CW:s * CW + N], 1.0, None, ALU.min).then_inc(s_mask, 1)
                if s >= 1:
                    for half in range(2):
                        v.wait_ge(s_mt, 2 * (s - 1) + half + 1)
                        v.tensor_scalar(NEG[:, 5 * half:5 * half + 5, (s - 1) * T:s * T],
                                        PSB[0:T, 4 + half, 0:630].rearrange("p (k n) -> p k n", k=5)[:, :, 0:T],
                                        1.0, BIG, ALU.subtract, ALU.mult).then_inc(s_neg, 1)
            v.wait_ge(s_neg, 2 * NT)

            def neighbour_max(n):
                j, dt = divmod(n, NT)
                if dt == 0:
                    v.wait_ge(s_asB[j % 2], 16 * (j // 2 + 1))
                if n >= 2:
                    v.wait_ge(s_mx, n - 1)
                v.tensor_tensor_reduce(junk[n % 2][:, :], asB[j % 2][0:T, :], NEG[:, dt, :], 1.0, -3.0e38,
                                       ALU.add, ALU.max, mx_all[:, dt, j:j + 1]).then_inc(s_mx, 1)

            def uv_columns(l):
                v.wait_ge(s_mx, NT * HEADS * (l + 1))
                if l == 0:
                    v.wait_ge(s_lc, 1)
                    link(v.tensor_copy(logitc[:, :, :], PS[0:T, 3, 0:240].rearrange("p (t c) -> p t c", c=24)))
                ad = logitc[:, :, (2 * l + 1) * HEADS:(2 * l + 2) * HEADS]
                link(v.tensor_tensor(zz[:, :, :], mx_all[:, :, l * HEADS:(l + 1) * HEADS], ad, ALU.add))
                link(v.scalar_tensor_tensor(out=zz[:, :, :], in0=zz[:, :, :], scalar=SLOPE, in1=zz[:, :, :],
                                            op0=ALU.mult, op1=ALU.max))
                link(v.tensor_tensor(UV[l % 2][:, :, 0:HEADS], ad, zz[:, :, :], ALU.subtract))
                link(v.scalar_tensor_tensor(out=UV[l % 2][:, :, HEADS:], in0=ad, scalar=SLOPE, in1=zz[:, :, :],
                                            op0=ALU.mult, op1=ALU.subtract))
                for dst_, f in ((as8, 1.0 - SLOPE), (as2, SLOPE)):
                    link(v.tensor_scalar(dst_[:, l * HEADS * NT:(l + 1) * HEADS * NT].rearrange("p (h t) -> p t h", h=HEADS),
                                         logitc[:, :, 2 * l * HEADS:(2 * l + 1) * HEADS], f, None, ALU.mult))
                v.sem_inc(s_uv, 1)
            for l in range(2):
                for n in range(l * M2, (l + 1) * M2):
                    neighbour_max(n)
                uv_columns(l)
            v.memset(hs[0][:, :, C:CP], 1.0).then_inc(s_ones, 1)

            def exponent(u):
                head, st = divmod(u, NT)
                if st == 0:
                    v.wait_ge(s_hs[head % 2], 48 * (head // 2 + 1))
                if u == 2:
                    v.wait_ge(s_h, HU)
                if u >= DEPTH:
                    v.wait_ge(s_ex, u - DEPTH + 1)
                v.scalar_tensor_tensor(out=tt[u % DEPTH][:, :], in0=uB[head % 2][0:T, :], scalar=as8[:, u:u + 1],
                                       in1=vB[head % 2][0:T, :], op0=ALU.add, op1=ALU.max).then_inc(s_tt, 1)

            def probs(u):
                st = u % NT
                v.wait_ge(s_ex, u + 1)
                v.wait_ge(s_pu, u + 1)
                v.scalar_tensor_tensor(out=pr[u % DEPTH][:, :], in0=ex[u % DEPTH][:, :], scalar=3.0e38,
                                       in1=CTf[:, st * CW:st * CW + N], op0=ALU.min, op1=ALU.mult).then_inc(s_p, 1)

            def sums(head):
                for b in range(5):
                    if b < 4:
                        v.wait_ge(s_ob, head * 4 + b + 1)
                    else:
                        v.wait_ge(s_pu, head * NT + NT + DEPTH)
                    if b == 0 and head:
                        v.wait_ge(s_oe, head * NT)
                    v.tensor_scalar(den[:, 2 * b:2 * b + 2], PS[0:T, b, :].rearrange("p (r c) -> p r c", r=2)[:, :, C],
                                    1e-16, None, ALU.add).then_inc(s_den, 1)
                    v.wait_ge(s_den, head * 5 + b + 1)
                    v.reciprocal(rs[:, 2 * b:2 * b + 2], den[:, 2 * b:2 * b + 2]).then_inc(s_rs, 1)
            exponent(0)
            issued = 1
            for n in range(M2_BEFORE):
                neighbour_max(2 * M2 + n)
            done = M2_BEFORE
            for u in range(UNITS):
                head, st = divmod(u, NT)
                while issued < min(UNITS, u + (2 if u < 2 else 3)):
                    exponent(issued)
                    issued += 1
                while done < min(M2, M2_BEFORE + (u + 1) * (M2 - M2_BEFORE) // M2_STEPS):
                    neighbour_max(2 * M2 + done)
                    done += 1
                    if done == M2:
                        uv_columns(2)
                probs(u)
                if u == 1:
                    v.memset(hs[1][:, :, C:CP], 1.0).then_inc(s_ones, 1)
                if st == 0 and head:
                    sums(head - 1)
            sums(HEADS_ALL - 1)
            v.wait_ge(s_oe, UNITS)
            v.memset(zrow[:, :], 0.0).then_inc(s_zr, 1)

            def gate(t):
                v.wait_ge(s_lg, t + 1)
                link(v.tensor_copy(lg[:, t, :], PS[0:T, 6 + t % 2, 0:EXPERTS]))
                link(v.max(top[:, t, :], lg[:, t, :]))
                link(v.max_index(tidx[:, t, :], top[:, t, :], lg[:, t, :]))
                link(v.tensor_copy(idxF[:, t, :], tidx[:, t, 0:TOPK]))
                for k in range(TOPK):
                    ins = v.tensor_scalar(ohp[:, t, k * EXPERTS:(k + 1) * EXPERTS], iota1[0:T, 0:EXPERTS], 1.0,
                                          idxF[:, t, k:k + 1], ALU.subtract, ALU.is_equal)
                link(ins)
                v.tensor_copy(oh2[:, t, :], ohp[:, t, :]).then_inc(s_oh2, 1)

            def w1_low(e):
                for k in range(KT):
                    v.wait_ge(s_w1h, KT * e + k + 1)
                    v.tensor_tensor(W1l[e % 2][:, k, :], W1s[:, k, :], W1h[e % 2][:, k, :].bitcast(F32),
                                    ALU.subtract).then_inc(s_w1l, 1)

            def rows_out(t):
                v.wait_ge(s_misc, 32)
                v.wait_ge(s_xr[t % 2], 16 * (t // 2 + 1))
                for c in range(2):
                    f = slice(c * HALF, (c + 1) * HALF)
                    v.wait_ge(s_pj, 2 * t + c + 1)
                    link(v.tensor_tensor(rr[c], PS[0:T, 2 * (t % 2) + c, 0:HALF], boB[0:T, f], ALU.add))
                    v.scalar_tensor_tensor(out=x2[:, t, f], in0=rr[c], scalar=0.0, in1=xr[t % 2][:, f],
                                           op0=ALU.max, op1=ALU.add).then_inc(s_pje, 1)
                    v.wait_ge(s_pje, 2 * t + c + 1)
                    link(v.bn_stats(st2[:, 6 * c:6 * c + 6], x2[:, t, f]))
                link(v.bn_aggr(mv2[:, 0:2], st2[:, :]))
                v.tensor_scalar(mv2[:, 2:3], mv2[:, 1:2], LN_EPS, None, ALU.add).then_inc(s_v2, 1)
                v.wait_ge(s_r2, t + 1)
                if t >= 2:
                    v.wait_ge(s_yd[t % 2], 16 * (t // 2))
                    v.wait_ge(s_yt, 2 * (t - 1))
                v.tensor_scalar(y[t % 2][:, :], x2[:, t, :], mv2[:, 0:1], rstd2[:, t:t + 1], ALU.subtract,
                                ALU.mult).then_inc(s_y, 1)
                v.wait_ge(s_y, t + 1)

            def wout_low(k):
                v.wait_ge(s_woh, k + 1)
                v.tensor_tensor(Wol[:, k, :], Wo[:, k, :], Woh[k].bitcast(F32), ALU.subtract).then_inc(s_wol, 1)
            for n in range(NT * PAIRS):
                t = n // PAIRS
                if n == 0:
                    wout_low(0)
                v.wait_ge(s_ebh, n + 1)
                v.tensor_tensor(EBl[:, n % 3, :, :], EBs[:, n % 3, :, :], EBh[:, n % 3, :, :].bitcast(F32),
                                ALU.subtract).then_inc(s_ebl, 1)
                if n < PAIRS:
                    for k in range(max(1, 3 * n), 3 * n + 3):
                        wout_low(k)
                if n % PAIRS == 2 and t >= 1:
                    rows_out(t - 1)
                if n % PAIRS == 4 and t >= 2:
                    gate(t - 2)

            def route(t0, t1):
                v.wait_ge(s_cum, 1 if t0 == 0 else 2)
                r = slice(t0, t1)
                link(v.tensor_tensor(ohp[:, r, :], ohp[:, r, :],
                                     PS[0:T, 0, 16 * t0:16 * t1].rearrange("p (t e) -> p t e", e=16), ALU.mult))
                link(v.tensor_reduce(posk[:, r, :], ohp[:, r, :].rearrange("p t (k e) -> p t k e", k=TOPK), AX.X, ALU.add))
                v.tensor_scalar(keep[:, r, :], posk[:, r, :], float(CAP), None, ALU.is_lt)
                v.tensor_copy(rk[:, r, 0], posk[:, r, 0])
                link(v.tensor_scalar(rk[:, r, 1], posk[:, r, 1], float(CAP), None, ALU.add))
                v.tensor_scalar(tmpk[:, r, :], keep[:, r, :], -1000.0, 1001.0, ALU.mult, ALU.add)
                link(v.tensor_scalar(rsub[:, r, :], rk[:, r, :], float(T), None, ALU.is_ge))
                link(v.scalar_tensor_tensor(out=rsub[:, r, :], in0=rk[:, r, :], scalar=float(2 * T), in1=rsub[:, r, :],
                                            op0=ALU.is_ge, op1=ALU.add))
                link(v.scalar_tensor_tensor(out=rslot[:, r, :], in0=rsub[:, r, :], scalar=-float(T), in1=rk[:, r, :],
                                            op0=ALU.mult, op1=ALU.add))
                v.tensor_tensor(rslot[:, r, :], rslot[:, r, :], tmpk[:, r, :], ALU.add)
                link(v.scalar_tensor_tensor(out=rtile[:, r, :], in0=idxF[:, r, :], scalar=float(RT), in1=rsub[:, r, :],
                                            op0=ALU.mult, op1=ALU.add))
                link(v.tensor_scalar(rtile[:, r, :], rtile[:, r, :], 1.0, None, ALU.add))
                for u in range(TOPK * t0, TOPK * t1):
                    t, k = divmod(u, TOPK)
                    v.tensor_scalar(ohs[:, u, :], iota1[0:T, 0:T], rslot[:, t, k:k + 1], None, ALU.is_equal)
                    v.tensor_scalar(oht[:, u, :], iota1[0:T, 0:EXPERTS * RT], rtile[:, t, k:k + 1], tokv[:, t:t + 1],
                                    ALU.is_equal, ALU.mult).then_inc(s_tk, 1)
            route(0, ROUTED)
            rows_out(NT - 1)
            gate(NT - 2)
            gate(NT - 1)
            route(ROUTED, NT)
            v.wait_ge(s_tku, 2)
            v.tensor_scalar(tokI[:, :], PS[0:T, 1, 0:EXPERTS * RT], float(N), None, ALU.add).then_inc(s_tok, 1)
            v.tensor_tensor(small[:, 0:NT], top[:, :, 1], top[:, :, 0], ALU.subtract).then_inc(s_sm, 1)
            v.wait_ge(s_sme, 1)
            link(v.tensor_scalar(small[:, NT:2 * NT], edt[:, :], 1.0, None, ALU.add))
            link(v.reciprocal(wk[:, :, 0], small[:, NT:2 * NT]))
            link(v.tensor_tensor(wk[:, :, 1], wk[:, :, 0], edt[:, :], ALU.mult))
            link(v.tensor_tensor(wk[:, :, :], wk[:, :, :], keep[:, :, :], ALU.mult))
            link(v.tensor_scalar(tmpk[:, :, :], rk[:, :, :], float(ROWS - 1), None, ALU.subtract))
            link(v.tensor_tensor(tmpk[:, :, :], tmpk[:, :, :], keep[:, :, :], ALU.mult))
            link(v.tensor_scalar(tmpk[:, :, :], tmpk[:, :, :], float(ROWS - 1), None, ALU.add))
            link(v.scalar_tensor_tensor(out=rowF[:, :, :], in0=idxF[:, :, :], scalar=float(ROWS), in1=tmpk[:, :, :],
                                        op0=ALU.mult, op1=ALU.add))
            v.tensor_copy(rowI[:, :].rearrange("p (t k) -> p t k", k=TOPK), rowF[:, :, :]).then_inc(s_tok, 1)
            w1_low(0)
            def rows_low(w):
                u, half = divmod(w, 2)
                j = u % RT
                v.wait_ge(s_xth, w + 1)
                f, r = slice(3 * half, 3 * half + 3), slice(j * T, (j + 1) * T)
                v.tensor_tensor(XgTl[:, f, r], PS[:, half, 0:3 * T].rearrange("p (k n) -> p k n", k=3),
                                XgTh[:, f, r].bitcast(F32), ALU.subtract).then_inc(s_xtl, 1)
            v.wait_ge(s_pad, 2)
            for w in range(2 * RT):
                rows_low(w)
            for e in range(EXPERTS):
                for k in range(2):
                    v.wait_ge(s_w2h, 2 * e + k + 1)
                    v.tensor_tensor(W2l[:, k, :], W2s[:, k, :], W2h[:, k, :].bitcast(F32), ALU.subtract).then_inc(s_w2l, 1)
                if e + 1 < EXPERTS:
                    w1_low(e + 1)
                for m in range(2):
                    v.wait_ge(s_h1, 4 * e + 2 + m + 1)
                    v.wait_ge(s_sg, 2 * e + m + 1)
                    v.tensor_tensor(actT[:, m, :], PS[:, 2 + m, 0:ROWS], sg[m][:, :], ALU.mult).then_inc(s_am, 1)
                for m in range(2):
                    v.wait_ge(s_ah, 2 * e + m + 1)
                    if e >= 1:
                        v.wait_ge(s_yb, 2 * RT * e)
                    v.tensor_tensor(actl[:, m, :], actT[:, m, :], acth[:, m, :].bitcast(F32), ALU.subtract).then_inc(s_al, 1)
                if e + 1 < EXPERTS:
                    for w in range(2 * RT):
                        rows_low(2 * RT * (e + 1) + w)
            for t in range(NT):
                v.wait_ge(s_g[t], 16 * TOPK)
                link(v.scalar_tensor_tensor(out=gg[t][:, 0, :], in0=gg[t][:, 0, :], scalar=wk[:, t, 0:1],
                                            in1=x2[:, t, :], op0=ALU.mult, op1=ALU.add))
                v.scalar_tensor_tensor(out=gg[t][:, 1, :], in0=gg[t][:, 1, :], scalar=wk[:, t, 1:2],
                                       in1=gg[t][:, 0, :], op0=ALU.mult, op1=ALU.add).then_inc(s_fin, 1)


_INS = ['x', 'src', 'dst', 'L0_gnn_W_ah', 'L0_gnn_b_ah', 'L0_gnn_W0', 'L0_gnn_a_src0', 'L0_gnn_a_dst0', 'L0_gnn_b0',
        'L0_gnn_W1', 'L0_gnn_a_src1', 'L0_gnn_a_dst1', 'L0_gnn_b1', 'L0_gnn_W2', 'L0_gnn_a_src2', 'L0_gnn_a_dst2',
        'L0_gnn_b2', 'L0_gnn_W_out', 'L0_gnn_b_out', 'L0_ffn_Wg', 'L0_ffn_W1', 'L0_ffn_W2']


def kernel(**inputs):
    import numpy as _np
    import concourse.bacc as _bacc
    from concourse import mybir as _mybir
    from concourse.bass_utils import run_bass_kernel_spmd as _run

    nc = _bacc.Bacc("TRN2", target_bir_lowering=False, num_devices=1)
    arrays, aps = {}, {}
    for name in _INS:
        a = _np.ascontiguousarray(inputs[name])
        arrays[f"in_{name}_dram"] = a
        aps[name.replace("L0_gnn_", "").replace("L0_", "")] = nc.dram_tensor(
            f"in_{name}_dram", a.shape, _mybir.dt.from_np(a.dtype), kind="ExternalInput").ap()
    out = nc.dram_tensor("out_0_dram", (N, D), F32, kind="ExternalOutput").ap()
    gnn_moe(nc, aps["x"], aps["src"], aps["dst"], aps["W_ah"], aps["b_ah"],
            [aps[f"W{l}"] for l in range(LAYERS)], [aps[f"a_src{l}"] for l in range(LAYERS)],
            [aps[f"a_dst{l}"] for l in range(LAYERS)], [aps[f"b{l}"] for l in range(LAYERS)],
            aps["W_out"], aps["b_out"], aps["ffn_Wg"], aps["ffn_W1"], aps["ffn_W2"], out)
    r = _run(nc, [arrays], core_ids=[0])
    return r.results[0]["out_0_dram"]
```
